# Optimizing a Trainium2 kernel written in Bass

```python
import numpy as np
import jax
import jax.numpy as jnp

def _softmax(x, axis=-1):
    return jax.nn.softmax(x, axis=axis)

def _gelu(x):
    return jax.nn.gelu(x, approximate=True)

def _silu(x):
    return jax.nn.silu(x)

def _sigmoid(x):
    return jax.nn.sigmoid(x)

def _layernorm(x, axis=-1, eps=1e-05):
    m = jnp.mean(x, axis=axis, keepdims=True)
    v = jnp.var(x, axis=axis, keepdims=True)
    return (x - m) / jnp.sqrt(v + eps)

def _scatter_add(tgt, idx, src, axis=0):
    return tgt.at[idx].add(src)

def _segment_sum(src, seg, n):
    return jax.ops.segment_sum(src, seg, n)
kernel_name = 'mk_flamingo_gated_d1_seqx_r4_82731d'

def setup_inputs(seed: int=0):
    np.random.seed(seed)
    _w = jnp.asarray

    def _rec_inputs():
        import jax
        import jax.numpy as jnp
        _rk = jax.random.key(seed)
        x = 7.22e-05 + 1 * jax.random.normal(jax.random.fold_in(_rk, 1), (8, 512, 256), jnp.float32)
        _lenS = 512 - jax.random.randint(jax.random.fold_in(_rk, 7), (8,), 0, max(1, 512 // 4) + 1, jnp.int32)
        _lenS2 = 512 - jax.random.randint(jax.random.fold_in(_rk, 8), (8,), 0, max(1, 512 // 4) + 1, jnp.int32)
        _ctx_1024P = jax.random.normal(jax.random.fold_in(_rk, 11), (8, 16, 256), jnp.float32)
        _ctx_1024c = jax.random.dirichlet(jax.random.fold_in(_rk, 511), 0.3 * jnp.ones((16,), jnp.float32), (8, 512))
        _ctx_1024t = jnp.einsum('bsk,bkd->bsd', _ctx_1024c, _ctx_1024P)
        _ctx_1024t = _ctx_1024t * jax.lax.rsqrt(jnp.mean(jnp.square(_ctx_1024t)) + 1e-12) * 0.953939
        ctx_1024 = 4.13588e-05 + 0.999923 * (_ctx_1024t + 0.3 * jax.random.normal(jax.random.fold_in(_rk, 611), (8, 512, 256), jnp.float32))
        _validS = jnp.arange(512)[None, :] < _lenS[:, None]
        _validS2 = jnp.arange(512)[None, :] < _lenS2[:, None]
        _causal = jnp.tril(jnp.ones((512, 512), dtype=bool))
        mask_1x1xSxS2_ik0 = jnp.where(jnp.broadcast_to(_validS2[0:1, None, None, :], (1, 1, 512, 512)), 0, 1).astype(jnp.int32)
        _g = jax.random.normal(jax.random.fold_in(_rk, 9001), (2, 1), jnp.float32)
        _g = jnp.sign(_g) * jnp.maximum(jnp.abs(_g), 1.0) + (_g == 0) * 1.0
        g_xattn = _g[0]
        g_ffn = _g[1]
        return (x, ctx_1024, mask_1x1xSxS2_ik0, g_xattn, g_ffn)
    x, ctx_1024, mask_1x1xSxS2_ik0, g_xattn, g_ffn = _rec_inputs()

    def _L0_xattn_setup():
        import jax, jax.numpy as jnp
        import numpy as np
        import math
        D_MODEL = 256
        N_HEADS = 16
        D_HEAD = D_MODEL // N_HEADS
        B, S = (4, 512)
        key = jax.random.key(seed)
        ks = jax.random.split(key, 11)
        sc = 1.0 / math.sqrt(D_MODEL)
        inp = {'query': jax.random.normal(ks[0], (B, S, D_MODEL), jnp.float32), 'key': jax.random.normal(ks[1], (B, S, D_MODEL), jnp.float32), 'value': jax.random.normal(ks[2], (B, S, D_MODEL), jnp.float32), 'mask': jnp.tril(jnp.ones((S, S), jnp.int32))[None, None, :, :], 'wq': jax.random.normal(ks[3], (D_MODEL, D_MODEL), jnp.float32) * sc, 'bq': jax.random.normal(ks[4], (D_MODEL,), jnp.float32) * sc, 'wk': jax.random.normal(ks[5], (D_MODEL, D_MODEL), jnp.float32) * sc, 'bk': jax.random.normal(ks[6], (D_MODEL,), jnp.float32) * sc, 'wv': jax.random.normal(ks[7], (D_MODEL, D_MODEL), jnp.float32) * sc, 'bv': jax.random.normal(ks[8], (D_MODEL,), jnp.float32) * sc, 'wo': jax.random.normal(ks[9], (D_MODEL, D_MODEL), jnp.float32) * sc, 'bo': jax.random.normal(ks[10], (D_MODEL,), jnp.float32) * sc}
        return inp
    _L0_xattn_all = _L0_xattn_setup()
    _L0_xattn_in = {k: v for k, v in _L0_xattn_all.items() if k in ('wq', 'bq', 'wk', 'bk', 'wv', 'bv', 'wo', 'bo')}
    del _L0_xattn_all

    def _L0_ffn_setup():
        import jax, jax.numpy as jnp
        import numpy as np
        D_MODEL = 256
        N_EXPERTS = 8
        TOP_K = 2
        key = jax.random.key(seed)
        k1, k2, k3, k4 = jax.random.split(key, 4)
        B, S, D, E = (4, 512, D_MODEL, N_EXPERTS)
        dff = 4 * D
        lim = float(np.sqrt(6.0 / (D + dff)))
        return {'x': jax.random.normal(k1, (B, S, D), dtype=jnp.float32), 'router_w': jax.random.normal(k2, (D, E), dtype=jnp.float32) * (1.0 / np.sqrt(D)), 'router_b': jnp.zeros((E,), dtype=jnp.float32), 'expert_up': jax.random.uniform(k3, (E, dff, D), dtype=jnp.float32, minval=-lim, maxval=lim), 'expert_down': jax.random.uniform(k4, (E, D, dff), dtype=jnp.float32, minval=-lim, maxval=lim)}
    _L0_ffn_all = _L0_ffn_setup()
    _L0_ffn_in = {k: v for k, v in _L0_ffn_all.items() if k in ('router_w', 'router_b', 'expert_up', 'expert_down')}
    del _L0_ffn_all
    return {'x': x, 'ctx_1024': ctx_1024, 'mask_1x1xSxS2_ik0': mask_1x1xSxS2_ik0, 'g_xattn': g_xattn, 'g_ffn': g_ffn, 'L0_xattn_wq': _L0_xattn_in['wq'], 'L0_xattn_bq': _L0_xattn_in['bq'], 'L0_xattn_wk': _L0_xattn_in['wk'], 'L0_xattn_bk': _L0_xattn_in['bk'], 'L0_xattn_wv': _L0_xattn_in['wv'], 'L0_xattn_bv': _L0_xattn_in['bv'], 'L0_xattn_wo': _L0_xattn_in['wo'], 'L0_xattn_bo': _L0_xattn_in['bo'], 'L0_ffn_router_w': _L0_ffn_in['router_w'], 'L0_ffn_router_b': _L0_ffn_in['router_b'], 'L0_ffn_expert_up': _L0_ffn_in['expert_up'], 'L0_ffn_expert_down': _L0_ffn_in['expert_down']}

def reference(x, ctx_1024, mask_1x1xSxS2_ik0, g_xattn, g_ffn, L0_xattn_wq, L0_xattn_bq, L0_xattn_wk, L0_xattn_bk, L0_xattn_wv, L0_xattn_bv, L0_xattn_wo, L0_xattn_bo, L0_ffn_router_w, L0_ffn_router_b, L0_ffn_expert_up, L0_ffn_expert_down):
    import jax
    import jax.numpy as jnp

    def _L0_xattn_ref(query, key, value, mask, wq, bq, wk, bk, wv, bv, wo, bo):
        import jax, jax.numpy as jnp
        import numpy as np
        import math
        D_MODEL = 256
        N_HEADS = 16
        D_HEAD = D_MODEL // N_HEADS
        B, S = (4, 512)
        b, s, _ = query.shape
        q = query @ wq.T + bq
        k = key @ wk.T + bk
        v = value @ wv.T + bv
        q = q.reshape(b, s, N_HEADS, D_HEAD).transpose(0, 2, 1, 3)
        k = k.reshape(b, s, N_HEADS, D_HEAD).transpose(0, 2, 1, 3)
        v = v.reshape(b, s, N_HEADS, D_HEAD).transpose(0, 2, 1, 3)
        scores = jnp.einsum('bhqd,bhkd->bhqk', q, k) / math.sqrt(D_HEAD)
        scores = jnp.where(mask == 0, jnp.float32(-1000000000.0), scores)
        attn = jax.nn.softmax(scores, axis=-1)
        out = jnp.einsum('bhqk,bhkd->bhqd', attn, v)
        out = out.transpose(0, 2, 1, 3).reshape(b, s, D_MODEL)
        return out @ wo.T + bo

    def _L0_ffn_ref(x, router_w, router_b, expert_up, expert_down):
        import jax, jax.numpy as jnp
        import numpy as np
        D_MODEL = 256
        N_EXPERTS = 8
        TOP_K = 2
        B, S, D = x.shape
        E = expert_up.shape[0]
        x_flat = x.reshape(-1, D)
        logits = x_flat @ router_w + router_b
        probs = jax.nn.softmax(logits, axis=-1)
        top_w, top_idx = jax.lax.top_k(probs, TOP_K)
        comb = jnp.sum(top_w[..., None] * jax.nn.one_hot(top_idx, E, dtype=x.dtype), axis=1)
        output = jnp.zeros_like(x_flat)
        for e in range(E):
            h = jax.nn.gelu(x_flat @ expert_up[e].T, approximate=False)
            out_e = h @ expert_down[e].T
            output = output + comb[:, e:e + 1] * out_e
        return output.reshape(B, S, D)
    x = x + jnp.tanh(g_xattn[0]) * _L0_xattn_ref(_layernorm(x, axis=-1), ctx_1024, ctx_1024, mask_1x1xSxS2_ik0, L0_xattn_wq, L0_xattn_bq, L0_xattn_wk, L0_xattn_bk, L0_xattn_wv, L0_xattn_bv, L0_xattn_wo, L0_xattn_bo)
    x = x + jnp.tanh(g_ffn[0]) * _L0_ffn_ref(_layernorm(x, axis=-1), L0_ffn_router_w, L0_ffn_router_b, L0_ffn_expert_up, L0_ffn_expert_down)
    return x

_drawn_inputs = setup_inputs


def setup_inputs(seed=0):
    import zlib

    import numpy as np

    out = dict(_drawn_inputs(seed))
    spreads = {'L0_ffn_router_b': (0.0, 0.277)}
    factors = {'L0_xattn_bq': 3.746, 'L0_xattn_bk': 8.0}
    for name, (base, spread) in spreads.items():
        noise = np.random.default_rng([zlib.crc32(name.encode()), seed]).standard_normal(out[name].shape)
        drawn = base * np.exp(spread * noise) if base else spread * noise
        out[name] = jnp.asarray(drawn.astype(out[name].dtype))
    for name, factor in factors.items():
        out[name] = (out[name] * factor).astype(out[name].dtype)
    return out
```

```python
from contextlib import ExitStack

import concourse.bass as bass
import numpy as np
from concourse import mybir

F32 = mybir.dt.float32
F32R = mybir.dt.float32r
BF16 = mybir.dt.bfloat16
I32 = mybir.dt.int32
ACT = mybir.ActivationFunctionType
ALU = mybir.AluOpType
AX = mybir.AxisListType

P = 128
B, S, D = 8, 512, 256
H, DH = 16, 16
HG = 4
E, FF = 8, 1024
QT = S // P
KD = D // P
TOK = B * S
CAP = TOK + 2 * P
TILE = 2 * P
ROW = D + 1 + E
MASKED = -(2.0 ** 100)
SCALE = DH ** -0.5
EPS = 1e-5


def work_items(nt, last):
    items = [("score", 0, i) for i in range(4 if nt == 1 else 16)]
    items += [("v", i) for i in range(1 if nt == 1 else 2)]
    if not last:
        items += base_items(nt)
    for g in range(HG):
        if g + 1 < HG:
            items += [("score", g + 1, i) for i in range(4 if nt == 1 else 16)]
        items += [("shift", g)]
        if not last:
            items += stack_items(nt, g)
    items += [("proj", 0), ("proj", 1), ("x2t", 0), ("x2t", 1), ("logits",), ("rank",)]
    return items


def base_items(nt):
    n = 1 if nt == 1 else 2
    return ([("xt", k) for k in range(2)] + [("ct", k) for k in range(n)]
            + [("q", m) for m in range(2)] + [("k", m) for m in range(n)])


def stack_items(nt, g):
    keys = [("ks", g, 0)] if nt == 1 else [("ks", g, 0), ("ks", g, 1)]
    return [("qs", g, 0), ("qs", g, 1)] + keys


class Work:

    def __init__(self, items, base):
        self.at, used = {}, [0, 0, 0]
        for n, item in enumerate(items):
            self.at[item] = (n % 3, used[n % 3])
            used[n % 3] += 1
        self.used, self.base = used, base

    def bank(self, item):
        return self.at[item][0]

    def before(self, item):
        bank, n = self.at[item]
        return self.base[bank] + n


def xattn_moe(nc, t):
    out = t["out"]
    routed = nc.dram_tensor("routed", (E * CAP, ROW), F32).ap()

    with ExitStack() as ctx:
        def sb(name, shape, dt=F32):
            return ctx.enter_context(nc.sbuf_tensor(name, shape, dt))

        def sem(name):
            return ctx.enter_context(nc.semaphore(name))

        ident = sb("ident", [P, P])
        identb = sb("identb", [P, P], BF16)
        trib = sb("trib", [P, P], BF16)
        onesb = sb("onesb", [P, P], BF16)
        key_ones = sb("key_ones", [P, 2])
        region = sb("region", [P, E])
        padrow0 = sb("padrow0", [P, 2, E])
        lane = sb("lane", [P, E])
        gate_x = sb("gate_x", [P, 1])
        gate_f = sb("gate_f", [P, 1])
        one_pt5 = sb("one_pt5", [P, 1])
        rw = sb("rw", [P, KD, E])
        rb = sb("rb", [P, E])
        counts = sb("counts", [P, E])
        tiles_i = sb("tiles_i", [1, 2 * E], I32)
        flag_i = sb("flag_i", [1, 2], I32)

        sbA = ExitStack()
        sb_outer = sb

        def sba(name, shape, dt=F32):
            return sbA.enter_context(nc.sbuf_tensor(name, shape, dt))

        raw = sba("raw", [P, 2048])
        xin = sba("xin", [P, QT, D])
        cin = sba("cin", [P, QT, D])
        xt = sba("xt_r", [P, 2, KD, S], F32R)
        ct = sba("ct_r", [P, 2, KD, S], F32R)
        qb = sba("qb_r", [P, 2, KD, S], F32R)
        kb = sba("kb_r", [P, 2, KD, S], F32R)
        Wr = {n: sba(f"{n}_r", [P, 2, KD, D], F32R) for n in ("wq", "wk", "wv", "wo")}
        selq = sba("selq_r", [P, 4, 2, P], F32R)
        selk = sba("selk_r", [P, 4, 2, P], F32R)
        bq = sba("bq_c", [P, 2])
        bk = sba("bk_c", [P, 2])
        bv = sba("bv_b", [P, D])
        gbo = sba("gbo_b", [P, D])
        mask_s = sba("mask_s", [P, QT, S], BF16)
        mask_t = sba("mask_t", [P, QT, S], BF16)
        mask_s1 = sba("mask_s1", [P, QT, P], BF16)
        mask_t1 = sba("mask_t1", [P, S], BF16)
        any_q = sba("any_q", [P, QT, QT])
        any_b = sba("any_b", [P, QT, QT], BF16)
        small = sba("small", [P, 32])
        xn = sba("xn", [P, QT, D])
        xres = sba("xres", [P, QT, D])
        QS = sba("QS_r", [P, 8, S], F32R)
        KS = sba("KS_r", [P, 8, S], F32R)
        V = sba("V", [P, QT, H, 32])
        prob = sba("prob", [P, 2, 4, S])
        mx = sba("mx", [P, 16])
        MT = sba("MT", [P, QT, P])
        T1 = sba("T1", [P, S // 32, 32])
        T2 = sba("T2", [P, S // 32, 32])
        T3 = sba("T3", [P, S])
        den = sba("den", [P, S // 32])
        OT = sba("OT_r", [P, 2, 2, S], F32R)
        x2t = sba("x2t", [P, KD, S])
        st = sba("st", [P, 2, QT, 6])
        mv = sba("mv", [P, 2, QT, 2])
        nw = sba("nw", [P, 2, 4, QT])
        lg = sba("lg", [P, 8, QT, E])
        l1 = sba("l1", [P, 8, QT])
        Cb = sba("Cb", [P, QT, E], BF16)
        Rb = sba("Rb", [P, QT + 1, E], BF16)
        slot_i = sba("slot_i", [P, 2, QT], I32)
        tokf = sba("tokf", [P, QT])
        x1 = sba("x1", [P, QT, D])
        pay = sba("pay", [P, QT, ROW])

        sbA.close()
        sbE = ExitStack()

        def sbe(name, shape, dt=F32):
            return sbE.enter_context(nc.sbuf_tensor(name, shape, dt))

        up_raw = sbe("up_raw", [P, KD, FF])
        dn_raw = sbe("dn_raw", [P, FF // P, D])
        up_r, dn_r = [], []
        for i in range(2):
            up_r.append(sbe(f"up_r{i}", [P, 2, KD, FF], F32R))
            dn_r.append(sbe(f"dn_r{i}", [P, 2, FF // P, D], F32R))
        xe = sbe("xe", [P, 2, ROW])
        meta = sbe("meta", [P, 2, 1 + E])
        xet = sbe("xet_r", [P, 2, KD, TILE], F32R)
        hf = sbe("hf", [P, 4, 2 * TILE])
        hr = sbe("hr_r", [P, 2, 4, 2 * TILE], F32R)
        ye = sbe("ye", [P, 2, D])
        pads = sbe("pads", [P, 2, ROW])
        pad_i = sbe("pad_i", [P, 2, E], I32)
        tf = sbe("tf", [1, 4 * E])
        ti = sbe("ti", [1, 2 * E], I32)
        sbE.close()

        ps = ctx.enter_context(nc.psum_tensor("ps", [P, 8, S], F32))
        psb = ps
        UPB = [0, 1, 2, 6]
        WORK, SC, AV = 0, 3, 7

        names = """const_dma raw_free const_done flag_dma flag_act flag_pe flag_done mask_ready gates
            x_in ctx_in xres_in stats1 xn_done xres_done hi_done lo_done qs_ready ks_ready v_ready
            neg_done aug_done st_full exp_done av_done av_free ot_ready x1_done x1_stored xn2_done
            x2t_done exp_log comb_done slots_done scattered chain_v chain_a chain_p zero_out
            counted tiles_done pads_set pads_in w_dma w_hi w_lo pads0_in w_pool x_dma meta_dma
            x_used xt_hi xt_lo up_full act_f act_r h_lo down_done y_full y_done added xt_full pre passed""".split()
        s = {n: sem(n) for n in names}
        full = [sem(f"work_full{i}") for i in range(3)]
        free = [sem(f"work_free{i}") for i in range(3)]

        block = ctx.enter_context(nc.Block())

        class Chain:

            def __init__(self, eng, sem_, base=0):
                self.eng, self.sem, self.n, self.base = eng, sem_, 0, base

            def __call__(self, ins):
                self.n += 1
                ins.then_inc(self.sem, 1)
                return ins

            def wait(self):
                self.eng.wait_ge(self.sem, self.base + self.n)

        def wait_reg(eng, sem_, value):
            eng.wait_ge(sem_, value)
            eng.sem_inc(s["passed"], 1)

        def both(eng, run, extra=None):
            eng.wait_ge(s["flag_done"], 1)
            fast = eng.value_load(flag_i[0:1, 0:1], min_val=0, max_val=1)
            with eng.If(fast == 1):
                run(1)
            with eng.Else():
                run(QT)
            eng.end_ifs()

        def batches(eng, nt, prologue, body):
            first = Work([i for i in base_items(nt)] + [i for g in range(HG) for i in stack_items(nt, g)], [0, 0, 0])
            if prologue:
                prologue(nt, first)
            steady = Work(work_items(nt, False), first.used)
            with eng.Fori(0, B - 1) as b:
                body(nt, b, Work(work_items(nt, False), [first.used[i] + b * steady.used[i] for i in range(3)]), False)
            body(nt, B - 1, Work(work_items(nt, True), [first.used[i] + (B - 1) * steady.used[i] for i in range(3)]), True)

        def n_split(nt):
            return 2 + 2 + 2 * (1 if nt == 1 else 2)

        def split_no(nt, item):
            return base_items(nt).index(item)

        def w_raw(j):
            return up_raw[:, j, :] if j < 2 else dn_raw[:, 4 * j - 8:4 * j - 4, :].rearrange("p c d -> p (c d)")

        def w_part(par, low, j):
            return up_r[par][:, low, j, :] if j < 2 else dn_r[par][:, low, 4 * j - 8:4 * j - 4, :].rearrange("p c d -> p (c d)")

        CONST = ["ident", "trimat", "selq", "selk"]

        @block.sync
        def _(sp):
            sp.dma_start(key_ones[:, :], t["key_ones"]).then_inc(s["const_dma"], 16)
            sp.dma_start(region[:, :], t["region"]).then_inc(s["const_dma"], 16)
            sp.dma_start(padrow0[:, :, :], t["padrow0"]).then_inc(s["const_dma"], 16)
            sp.dma_start(lane[:, :], t["lane"]).then_inc(s["const_dma"], 16)
            sp.dma_start(ident[:, :], t["ident"]).then_inc(s["const_dma"], 16)
            sp.dma_start(rw[:, :, :], t["router_w"].rearrange("(k p) e -> p k e", p=P)).then_inc(s["const_dma"], 16)
            sp.dma_start(rb[:, :], t["router_b"].unsqueeze(0).to_broadcast([P, E])).then_inc(s["const_dma"], 16)
            sp.dma_start(gate_x[:, :], t["g_xattn"].unsqueeze(0).to_broadcast([P, 1])).then_inc(s["const_dma"], 16)
            sp.dma_start(gate_f[:, :], t["g_ffn"].unsqueeze(0).to_broadcast([P, 1])).then_inc(s["const_dma"], 16)
            sp.dma_start(bq[:, :], t["bq"]).then_inc(s["const_dma"], 16)
            sp.dma_start(bk[:, :], t["bk"]).then_inc(s["const_dma"], 16)
            sp.dma_start(bv[:, :], t["bv"].unsqueeze(0).to_broadcast([P, D])).then_inc(s["const_dma"], 16)
            sp.dma_start(gbo[:, :], t["bo"].unsqueeze(0).to_broadcast([P, D])).then_inc(s["const_dma"], 16)
            sp.dma_start(tokf[:, :], t["tokens"]).then_inc(s["const_dma"], 16)
            stage = [(raw[:, 0:2048].bitcast(I32).rearrange("p (t k) -> p t k", t=QT), t["mask"].rearrange("(t p) k -> p t k", p=P)),
                     (raw[:, 0:2048].bitcast(I32).rearrange("p (t k) -> p t k", t=QT), t["mask_t"].rearrange("(t p) k -> p t k", p=P)),
                     (raw[:, 0:P], t["trimat"]),
                     (raw[:, 0:1024], t["selq"]),
                     (raw[:, 0:1024], t["selk"])]
            stage += [(raw[:, 0:512].rearrange("p (k n) -> p k n", k=KD), t[n].rearrange("(k p) n -> p k n", p=P))
                      for n in ("wq", "wk", "wv", "wo")]
            for n, (dst, src) in enumerate(stage):
                if n:
                    sp.wait_ge(s["raw_free"], n)
                sp.dma_start(dst, src).then_inc(s["flag_dma"], 16)

            def prologue(nt, w):
                sp.dma_start(xin[:, :, :], t["x"][0].rearrange("(q p) d -> p q d", p=P)).then_inc(s["x_in"], 16)
                load_ctx(nt, 0)

            def load_ctx(nt, b):
                if nt == 1:
                    src = t["ctx"][bass.ds(b, 1), bass.ds(tile_reg * P, P), :].rearrange("a p d -> p (a d)")
                    sp.dma_start(cin[:, 0, :], src).then_inc(s["ctx_in"], 16)
                else:
                    sp.dma_start(cin[:, :, :], t["ctx"][bass.ds(b, 1)].rearrange("a (q p) d -> p (a q) d", p=P)).then_inc(s["ctx_in"], 16)

            def body(nt, b, w, last):
                if last:
                    sp.wait_ge(s["xn_done"], B)
                    sp.wait_ge(s["lo_done"], n_split(nt) * B)
                    load_w(0)
                sp.wait_ge(s["x1_done"], 2 * b + 2)
                sp.dma_start(xres[:, :, :], t["x"][bass.ds(b, 1)].rearrange("a (q p) d -> p (a q) d", p=P)).then_inc(s["xres_in"], 16)
                if not last:
                    sp.wait_ge(s["xn_done"], b + 1)
                    sp.dma_start(xin[:, :, :], t["x"][bass.ds(b + 1, 1)].rearrange("a (q p) d -> p (a q) d", p=P)).then_inc(s["x_in"], 16)
                    sp.wait_ge(s["lo_done"], n_split(nt) * b + split_no(nt, ("ct", (1 if nt == 1 else 2) - 1)) + 1)
                    load_ctx(nt, b + 1)
                sp.wait_ge(s["x1_done"], 2 * b + 4)
                sp.dma_start(out[bass.ds(b * S, S), :].rearrange("(q p) d -> p q d", p=P), x1[:, :, :]).then_inc(s["x1_stored"], 16)

            def load_w(e):
                sp.dma_start(up_raw[:, :, :], t["up"][bass.ds(e, 1)].rearrange("a (k p) f -> p (a k) f", p=P)).then_inc(s["w_dma"], 16)
                sp.dma_start(dn_raw[:, :, :], t["down"][bass.ds(e, 1)].rearrange("a (c p) d -> p (a c) d", p=P)).then_inc(s["w_dma"], 16)

            sp.wait_ge(s["flag_done"], 1)
            tile_reg = sp.value_load(flag_i[0:1, 1:2], min_val=0, max_val=QT - 1)
            both(sp, lambda nt: batches(sp, nt, prologue, body))

            sp.wait_ge(s["tiles_done"], 1)
            sp.wait_ge(s["scattered"], 16 * 2 * TOK // P + 16)
            sp.wait_ge(s["pads0_in"], 16 * 2)
            sp.dma_start(xe[:, :, :], routed[0:TILE, :].rearrange("(h p) r -> p h r", p=P)).then_inc(s["x_dma"], 16)

            def expert(e, nxt):
                n = sp.value_load(tiles_i[0:1, bass.ds(e, 1)], min_val=1, max_val=TOK // TILE)
                base = sp.value_load(tiles_i[0:1, bass.ds(e + E, 1)], min_val=0, max_val=2 * TOK // TILE + E)
                if nxt:
                    sp.wait_ge(s["w_lo"], 4 * e + 4)
                    load_w(e + 1)
                sp.wait_ge(s["pads_in"], 16 * 2 * (E - 1))
                with sp.Fori(0, n) as i:
                    sp.wait_ge(s["xt_full"], base + i + 1)
                    sp.dma_start(xe[:, :, :], routed[bass.ds(next_row(e, i, n), TILE), :].rearrange("(h p) r -> p h r", p=P)).then_inc(s["x_dma"], 16)
                    sp.wait_ge(s["added"], 32 * (base + i) + 16)
                    sp.dma_start(meta[:, :, :], routed[bass.ds(within(e * CAP + i * TILE), TILE), D:ROW].rearrange("(h p) r -> p h r", p=P)).then_inc(s["meta_dma"], 16)

            def within(row):
                return nc.s_assert_within(row, 0, E * CAP - TILE, skip_runtime_bounds_check_because="an expert has at most TOK rows and the padding")

            def next_row(e, i, n):
                more = sp.snap((i + 1) < n)
                return within(more * (e * CAP + (i + 1) * TILE) + (1 - more) * nxt_row(e))

            def nxt_row(e):
                return ((e + 1) % E) * CAP

            with sp.Fori(0, E // 2 - 1) as k:
                expert(2 * k, True)
                expert(2 * k + 1, True)
            expert(E - 2, True)
            expert(E - 1, False)

        @block.scalar
        def _(act):
            ch = Chain(act, s["chain_a"])
            act.wait_ge(s["const_dma"], 16 * 14)
            nc.scalar.activation(gate_x[:, :], gate_x[:, :], ACT.Tanh).then_inc(s["gates"], 1)
            nc.scalar.activation(gate_f[:, :], gate_f[:, :], ACT.Tanh).then_inc(s["gates"], 1)

            def hi(nt, b, w, item, dst, src, bias=None):
                act.wait_ge(full[w.bank(item)], w.before(item) + 1)
                if bias is None:
                    ins = nc.scalar.activation(dst, src, ACT.Copy)
                else:
                    ins = nc.scalar.activation(dst, src, ACT.Identity, bias=bias)
                return ins

            def base(nt, b, w, bnext):
                for item in base_items(nt):
                    kind, m = item
                    bank = ps[:, WORK + w.bank(item), :]
                    if kind == "xt":
                        hi(nt, b, w, item, xt[:, 0, m, :], bank).then_inc(s["hi_done"], 1)
                    elif kind == "ct" and nt == 1:
                        hi(nt, b, w, item, ct[:, 0, :, 0:P], bank[:, 0:2 * P].rearrange("p (k n) -> p k n", k=2)).then_inc(s["hi_done"], 1)
                    elif kind == "ct":
                        hi(nt, b, w, item, ct[:, 0, m, :], bank).then_inc(s["hi_done"], 1)
                    elif kind == "q":
                        hi(nt, b, w, item, qb[:, 0, m, :], bank, bq[:, m:m + 1]).then_inc(s["hi_done"], 1)
                    elif nt == 1:
                        hi(nt, b, w, item, kb[:, 0, 0, 0:P], bank[:, 0:P], bk[:, 0:1])
                        nc.scalar.activation(kb[:, 0, 1, 0:P], bank[:, P:2 * P], ACT.Identity, bias=bk[:, 1:2]).then_inc(s["hi_done"], 1)
                    else:
                        hi(nt, b, w, item, kb[:, 0, m, :], bank, bk[:, m:m + 1]).then_inc(s["hi_done"], 1)

            def stacks(nt, b, w, g):
                for item in stack_items(nt, g):
                    kind, _, j = item
                    act.wait_ge(full[w.bank(item)], w.before(item) + 1)
                    bank = ps[:, WORK + w.bank(item), :]
                    if kind == "qs":
                        nc.scalar.activation(QS[:, 2 * g + j, :], bank, ACT.Copy).then_inc(s["qs_ready"], 1)
                        free_it = s["qs_ready"]
                    elif nt == 1:
                        nc.scalar.activation(KS[:, 2 * g, 0:P], bank[:, 0:P], ACT.Identity, bias=key_ones[:, 0:1])
                        nc.scalar.activation(KS[:, 2 * g + 1, 0:P], bank[:, P:2 * P], ACT.Identity, bias=key_ones[:, 1:2]).then_inc(s["ks_ready"], 1)
                    else:
                        nc.scalar.activation(KS[:, 2 * g + j, :], bank, ACT.Identity, bias=key_ones[:, j:j + 1]).then_inc(s["ks_ready"], 1)

            def prologue(nt, w):
                base(nt, 0, w, 0)
                for g in range(HG):
                    stacks(nt, 0, w, g)

            def body(nt, b, w, last):
                if not last:
                    act.wait_ge(s["v_ready"], b + 1)
                    base(nt, b, w, b + 1)
                for g in range(HG):
                    for kt in range(nt):
                        u = (b * HG + g) * nt + kt
                        slot = (g * nt + kt) % 2
                        for j in range(2):
                            act.wait_ge(s["st_full"], 2 * u + j + 1)
                            if j == 0:
                                act.wait_ge(s["av_done"], u + 1)
                            nc.scalar.activation(prob[:, slot, 2 * j:2 * j + 2, :], ps[:, SC + 2 * j:SC + 2 * j + 2, :],
                                                 ACT.Exp, scale=SCALE).then_inc(s["exp_done"], 1)
                    if not last:
                        stacks(nt, b, w, g)
                for k in range(2):
                    item = ("x2t", k)
                    act.wait_ge(full[w.bank(item)], w.before(item) + 1)
                    nc.scalar.activation(x2t[:, k, :], ps[:, WORK + w.bank(item), :], ACT.Copy).then_inc(s["x2t_done"], 1)
                act.wait_ge(s["exp_log"], 2 * b + 1)
                nc.scalar.activation(lg[:, 1, :, :], lg[:, 0, :, :], ACT.Exp).then_inc(s["exp_log"], 1)

            both(act, lambda nt: batches(act, nt, prologue, body))

            act.wait_ge(s["tiles_done"], 1)

            def high_x(n):
                act.wait_ge(s["xt_full"], n + 1)
                nc.scalar.activation(xet[:, 0, :, :], ps[:, 5, :].rearrange("p (k n) -> p k n", k=2), ACT.Copy).then_inc(s["xt_hi"], 1)

            high_x(0)

            def expert(e, par, nxt):
                n = act.value_load(tiles_i[0:1, bass.ds(e, 1)], min_val=1, max_val=TOK // TILE)
                base_ = act.value_load(tiles_i[0:1, bass.ds(e + E, 1)], min_val=0, max_val=2 * TOK // TILE + E)

                def tile(T, split):
                    for p in range(4):
                        act.wait_ge(s["up_full"], 4 * T + p + 1)
                        act.wait_ge(s["down_done"], 4 * T + p + 1)
                        bank = ps[:, UPB[p], :]
                        nc.scalar.activation(hr[:, 0, p, :], bank, ACT.Gelu).then_inc(s["act_r"], 1)
                        nc.scalar.activation(hf[:, p, :], bank, ACT.Gelu).then_inc(s["act_f"], 1)
                        if split:
                            if p == 0:
                                act.wait_ge(s["w_dma"], 32 * e + 64)
                                act.wait_ge(s["down_done"], 4 * T + 4)
                            nc.scalar.activation(w_part(1 - par, 0, p), w_raw(p), ACT.Copy).then_inc(s["w_hi"], 1)
                    high_x(T + 1)

                tile(base_, nxt)
                with act.If(n > 1):
                    with act.Fori(1, n) as i:
                        tile(act.snap(base_ + i), False)
                act.end_ifs()

            with act.Fori(0, E // 2 - 1) as k:
                expert(2 * k, 0, True)
                expert(2 * k + 1, 1, True)
            expert(E - 2, 0, True)
            expert(E - 1, 1, False)

        @block.tensor
        def _(pe):
            def mm(o, a, b_, start, stop):
                return pe.matmul(o, a, b_, start=start, stop=stop, skip_group_check=True)

            def three(o, a_h, a_l, b_h, b_l, parts):
                n = 0
                for k in parts:
                    for x_, y_ in ((a_h, b_h), (a_l, b_h), (a_h, b_l)):
                        ins = mm(o, x_(k), y_(k), n == 0, n == 3 * len(parts) - 1)
                        n += 1
                return ins

            pe.wait_ge(s["flag_pe"], 1)
            for qt in range(QT):
                ins = mm(ps[:, 0, 0:QT], onesb[:, :], any_b[:, qt, :], qt == 0, qt == QT - 1)
            ins.then_inc(s["flag_act"], 1)
            pe.wait_ge(s["const_done"], 1)

            def take(w, item):
                n = w.before(item)
                if not (isinstance(n, int) and n <= 0):
                    pe.wait_ge(free[w.bank(item)], n)
                return ps[:, WORK + w.bank(item), :]

            def give(w, item, ins):
                ins.then_inc(full[w.bank(item)], 1)

            def base(nt, w, b):
                ns = n_split(nt)
                for item in base_items(nt):
                    kind, m = item
                    if kind == "xt":
                        pe.wait_ge(s["xn_done"], b + 1)
                        o = take(w, item)
                        for q in range(QT):
                            ins = pe.transpose(o[:, q * P:(q + 1) * P], xn[:, q, m * P:(m + 1) * P], ident[:, :])
                    elif kind == "ct":
                        pe.wait_ge(s["ctx_in"], 16 * b + 16)
                        o = take(w, item)
                        for j in range(2 if nt == 1 else QT):
                            src = cin[:, 0, j * P:(j + 1) * P] if nt == 1 else cin[:, j, m * P:(m + 1) * P]
                            ins = pe.transpose(o[:, j * P:(j + 1) * P], src, ident[:, :])
                    elif kind == "q":
                        pe.wait_ge(s["lo_done"], ns * b + 2)
                        o = take(w, item)
                        ins = three(o, lambda k: Wr["wq"][:, 0, k, m * P:(m + 1) * P], lambda k: Wr["wq"][:, 1, k, m * P:(m + 1) * P],
                                    lambda k: xt[:, 0, k, :], lambda k: xt[:, 1, k, :], range(KD))
                    else:
                        pe.wait_ge(s["lo_done"], ns * b + split_no(nt, ("q", 0)))
                        o = take(w, item)
                        ms = range(2) if nt == 1 else [m]
                        for mm_ in ms:
                            dst = o[:, mm_ * P:(mm_ + 1) * P] if nt == 1 else o
                            ins = three(dst, lambda k: Wr["wk"][:, 0, k, mm_ * P:(mm_ + 1) * P], lambda k: Wr["wk"][:, 1, k, mm_ * P:(mm_ + 1) * P],
                                        lambda k: ct[:, 0, k, 0:nt * P], lambda k: ct[:, 1, k, 0:nt * P], range(KD))
                    give(w, item, ins)

            def stacks(nt, w, b, g):
                ns = n_split(nt)
                for item in stack_items(nt, g):
                    kind, _, j = item
                    if kind == "qs":
                        pe.wait_ge(s["lo_done"], ns * b + split_no(nt, ("q", (2 * g + j) // 4)) + 1)
                        o = take(w, item)
                        pair = 2 * g + j
                        mm(o, selq[:, pair % 4, 0, :], qb[:, 0, pair // 4, :], True, False)
                        ins = mm(o, selq[:, pair % 4, 1, :], qb[:, 1, pair // 4, :], False, True)
                    else:
                        pe.wait_ge(s["lo_done"], ns * b + ns)
                        o = take(w, item)
                        for jj in (range(2) if nt == 1 else [j]):
                            pair = 2 * g + jj
                            dst = o[:, jj * P:(jj + 1) * P] if nt == 1 else o
                            mm(dst, selk[:, pair % 4, 0, :], kb[:, 0, pair // 4, 0:nt * P], True, False)
                            ins = mm(dst, selk[:, pair % 4, 1, :], kb[:, 1, pair // 4, 0:nt * P], False, True)
                    give(w, item, ins)

            def scores(nt, w, b, g):
                pe.wait_ge(s["qs_ready"], 8 * b + 2 * g + 2)
                pe.wait_ge(s["ks_ready"], (4 * b + g + 1) if nt == 1 else (8 * b + 2 * g + 2))
                for i in range(4 if nt == 1 else 16):
                    item = ("score", g, i)
                    o = take(w, item)
                    if nt == 1:
                        x_, q0 = i % 2, 2 * (i // 2)
                        mm(o.rearrange("p (q j n) -> p q j n", q=2, j=2), identb[:, :],
                           mask_s1[:, q0:q0 + 2, :].unsqueeze(2).to_broadcast([P, 2, 2, P]), True, False)
                        for n in range(4):
                            q, pair, r = q0 + n // 2, 2 * g + n % 2, 64 * x_
                            ins = mm(o[:, n * P:(n + 1) * P], QS[r:r + 64, pair, q * P:(q + 1) * P], KS[r:r + 64, pair, 0:P], False, n == 3)
                    else:
                        q, h = i // 4, i % 4
                        pair, r = 2 * g + h // 2, 64 * (h % 2)
                        mm(o, identb[:, :], mask_s[:, q, :], True, False)
                        ins = mm(o, QS[r:r + 64, pair, q * P:(q + 1) * P], KS[r:r + 64, pair, :], False, True)
                    give(w, item, ins)

            def av(nt, b, g, kt):
                u = (b * HG + g) * nt + kt
                pe.wait_ge(s["exp_done"], 2 * u + 2 + 2)
                if g == 0 and kt == 0:
                    pe.wait_ge(s["v_ready"], b + 1)
                if kt == 0:
                    pe.wait_ge(s["av_free"], b * HG + g + 1)
                slot = (g * nt + kt) % 2
                for h in range(4):
                    ins = mm(ps[32 * h:32 * h + 32, AV, :], V[:, kt, 4 * g + h, :], prob[:, slot, h, :], kt == 0, kt == nt - 1)
                ins.then_inc(s["av_done"], 1)

            def prologue(nt, w):
                pe.wait_ge(s["mask_ready"], 2)
                base(nt, w, 0)
                for g in range(HG):
                    stacks(nt, w, 0, g)

            def body(nt, b, w, last):
                scores(nt, w, b, 0)
                for i in range(1 if nt == 1 else 2):
                    item = ("v", i)
                    o = take(w, item)
                    for j in range(1 if nt == 1 else 2):
                        kt = 2 * i + j
                        ins = three(o[:, j * D:(j + 1) * D], lambda k: ct[:, 0, k, kt * P:(kt + 1) * P], lambda k: ct[:, 1, k, kt * P:(kt + 1) * P],
                                    lambda k: Wr["wv"][:, 0, k, :], lambda k: Wr["wv"][:, 1, k, :], range(KD))
                    give(w, item, ins)
                if not last:
                    base(nt, w, b + 1)
                for g in range(HG):
                    if g + 1 < HG:
                        scores(nt, w, b, g + 1)
                    pe.wait_ge(s["neg_done"], b * HG + g + 1)
                    item = ("shift", g)
                    o = take(w, item)
                    for q in range(QT):
                        ins = pe.transpose(o[:, q * P:(q + 1) * P], MT[:, q, :], ident[:, :])
                    give(w, item, ins)
                    pe.wait_ge(s["aug_done"], b * HG + g + 1)
                    for kt in range(nt):
                        u = (b * HG + g) * nt + kt
                        for j in range(2):
                            pe.wait_ge(s["exp_done"], 2 * u + j + 1)
                            for x_ in range(2):
                                pair, r = 2 * g + j, 64 * x_
                                o = ps[:, SC + 2 * j + x_, :]
                                mm(o, identb[:, :], mask_t1[:, :] if nt == 1 else mask_t[:, kt, :], True, False)
                                ins = mm(o, KS[r:r + 64, pair, kt * P:(kt + 1) * P], QS[r:r + 64, pair, :], False, True)
                            ins.then_inc(s["st_full"], 1)
                        if kt:
                            av(nt, b, g, kt - 1)
                    if not last:
                        stacks(nt, w, b + 1, g)
                    av(nt, b, g, nt - 1)
                pe.wait_ge(s["ot_ready"], 2 * b + 2)
                for i in range(2):
                    item = ("proj", i)
                    o = take(w, item)
                    for j in range(2):
                        q = 2 * i + j
                        ins = three(o[:, j * D:(j + 1) * D], lambda k: OT[:, 0, k, q * P:(q + 1) * P], lambda k: OT[:, 1, k, q * P:(q + 1) * P],
                                    lambda k: Wr["wo"][:, 0, k, :], lambda k: Wr["wo"][:, 1, k, :], range(KD))
                    give(w, item, ins)
                pe.wait_ge(s["xn2_done"], b + 1)
                for k in range(2):
                    item = ("x2t", k)
                    o = take(w, item)
                    for q in range(QT):
                        ins = pe.transpose(o[:, q * P:(q + 1) * P], pay[:, q, k * P:(k + 1) * P], ident[:, :])
                    give(w, item, ins)
                pe.wait_ge(s["x2t_done"], 2 * b + 2)
                item = ("logits",)
                o = take(w, item)
                for q in range(QT):
                    for k in range(KD):
                        ins = mm(o[:, q * E:(q + 1) * E], x2t[:, k, q * P:(q + 1) * P], rw[:, k, :], k == 0, k == KD - 1)
                give(w, item, ins)
                pe.wait_ge(s["comb_done"], b + 1)
                item = ("rank",)
                o = take(w, item)
                mm(o[:, 0:QT * E], trib[:, :], Cb[:, :, :].rearrange("p t e -> p (t e)"), True, False)
                ins = mm(o[:, 0:QT * E], onesb[:, :], Rb[:, 0:QT, :].rearrange("p t e -> p (t e)"), False, True)
                give(w, item, ins)

            both(pe, lambda nt: batches(pe, nt, prologue, body))

            pe.wait_ge(s["slots_done"], B)
            mm(ps[:, 6, 0:E], onesb[:, :], Rb[:, 0, :], True, True).then_inc(s["counted"], 1)

            def transpose_x(n):
                pe.wait_ge(s["x_dma"], 16 * n + 16)
                pe.wait_ge(s["xt_lo"], n + 1)
                for k in range(KD):
                    for h in range(2):
                        ins = pe.transpose(ps[:, 5, k * TILE + h * P:k * TILE + (h + 1) * P], xe[:, h, k * P:(k + 1) * P], ident[:, :])
                ins.then_inc(s["xt_full"], 1)

            pe.wait_ge(s["tiles_done"], 1)
            transpose_x(0)

            def expert(e, par):
                n = pe.value_load(tiles_i[0:1, bass.ds(e, 1)], min_val=1, max_val=TOK // TILE)
                base_ = pe.value_load(tiles_i[0:1, bass.ds(e + E, 1)], min_val=0, max_val=2 * TOK // TILE + E)
                wait_reg(pe, s["w_lo"], 4 * e + 4)
                with pe.Fori(0, n) as i:
                    T = pe.snap(base_ + i)

                    def up(p):
                        pe.wait_ge(s["act_f"], 4 * T + p + 1)
                        for c in range(2 * p, 2 * p + 2):
                            ins = three(ps[:, UPB[p], (c % 2) * TILE:(c % 2 + 1) * TILE],
                                        lambda k: up_r[par][:, 0, k, c * P:(c + 1) * P], lambda k: up_r[par][:, 1, k, c * P:(c + 1) * P],
                                        lambda k: xet[:, 0, k, :], lambda k: xet[:, 1, k, :], range(KD))
                        ins.then_inc(s["up_full"], 1)

                    def down(p):
                        pe.wait_ge(s["h_lo"], 4 * T + p + 1)
                        if p == 0:
                            pe.wait_ge(s["y_done"], T + 1)
                        for half in range(2):
                            n_ = 0
                            for c in range(2):
                                hs = slice(c * TILE + half * P, c * TILE + (half + 1) * P)
                                for a, b_ in ((0, 0), (1, 0), (0, 1)):
                                    ins = mm(ps[:, 3 + half, 0:D], hr[:, a, p, hs], dn_r[par][:, b_, 2 * p + c, :],
                                             p == 0 and n_ == 0, p == 3 and n_ == 5)
                                    n_ += 1
                        ins.then_inc(s["down_done"], 1)

                    pe.wait_ge(s["xt_lo"], T + 2)
                    up(0)
                    up(1)
                    up(2)
                    down(0)
                    up(3)
                    down(1)
                    pe.wait_ge(s["x_dma"], 16 * T + 32)
                    for k in range(KD):
                        for h in range(2):
                            ins = pe.transpose(ps[:, 5, k * TILE + h * P:k * TILE + (h + 1) * P], xe[:, h, k * P:(k + 1) * P], ident[:, :])
                    ins.then_inc(s["xt_full"], 1)
                    down(2)
                    down(3)

            with pe.Fori(0, E // 2) as k:
                expert(2 * k, 0)
                expert(2 * k + 1, 1)

        @block.vector
        def _(dve):
            v = nc.vector
            ch = Chain(dve, s["chain_v"])

            ch(v.memset(onesb[:, :], 1.0))
            ch(v.memset(MT[:, :, :], 0.0))
            ch(v.memset(V[:, :, :, :], 1.0))
            ch(v.memset(Rb[:, :, :], 0.0))
            ch(v.memset(one_pt5[:, :], 1.5))
            dve.sem_inc(s["x1_done"], 2)
            dve.sem_inc(s["av_free"], 1)
            dve.sem_inc(s["exp_done"], 2)
            dve.sem_inc(s["av_done"], 2)
            dve.sem_inc(s["act_f"], 4)
            dve.sem_inc(s["down_done"], 4)
            dve.sem_inc(s["xt_lo"], 1)
            dve.sem_inc(s["y_done"], 1)

            rawi = raw[:, 0:2048].bitcast(I32).rearrange("p (t k) -> p t k", t=QT)
            dve.wait_ge(s["flag_dma"], 16)
            ch(v.tensor_scalar(mask_s[:, :, :], rawi, 0.0, MASKED, ALU.is_equal, ALU.mult))
            ch.wait()
            dve.sem_inc(s["raw_free"], 1)
            for q in range(QT):
                ch(v.tensor_reduce(any_q[:, q, :], mask_s[:, q, :].rearrange("p (a n) -> p a n", a=QT), AX.X, ALU.max))
            ch.wait()
            ch(v.tensor_scalar(any_b[:, :, :], any_q[:, :, :], 0.0, None, ALU.is_equal))
            ch.wait()
            dve.sem_inc(s["flag_pe"], 1)
            dve.wait_ge(s["flag_act"], 1)
            ch(v.tensor_scalar(small[:, 10:14], ps[:, 0, 0:QT], float(S), None, ALU.is_equal))
            ch(v.tensor_reduce(small[:, 14:15], ps[:, 0, 0:QT], AX.X, ALU.add))
            ch.wait()
            dve.wait_ge(s["const_dma"], 16 * 14)
            ch(v.tensor_tensor(small[:, 16:20], small[:, 10:14], lane[:, 0:QT], ALU.mult))
            ch(v.tensor_reduce(small[:, 15:16], small[:, 10:14], AX.X, ALU.max))
            ch(v.tensor_scalar(small[:, 20:21], small[:, 14:15], float(S), None, ALU.is_equal))
            ch.wait()
            ch(v.tensor_reduce(small[:, 22:23], small[:, 16:20], AX.X, ALU.max))
            ch(v.tensor_tensor(small[:, 21:22], small[:, 20:21], small[:, 15:16], ALU.mult))
            ch.wait()
            ch(v.tensor_copy(flag_i[0:1, :], small[0:1, 21:23]))
            ch.wait()
            dve.wait_ge(s["flag_dma"], 32)
            ch(v.tensor_scalar(mask_t[:, :, :], rawi, 0.0, MASKED, ALU.is_equal, ALU.mult))
            ch.wait()
            dve.sem_inc(s["raw_free"], 1)
            dve.sem_inc(s["flag_done"], 1)
            dve.wait_ge(s["flag_dma"], 48)
            ch(v.tensor_copy(trib[:, :], raw[:, 0:P]))
            ch(v.tensor_copy(identb[:, :], ident[:, :]))
            ch.wait()
            dve.sem_inc(s["raw_free"], 1)
            for n, tile in enumerate((selq, selk)):
                dve.wait_ge(s["flag_dma"], 64 + 16 * n)
                ch(v.tensor_copy(tile[:, :, :, :], raw[:, 0:1024].rearrange("p (a b c) -> p a b c", a=4, b=2)))
                ch.wait()
                dve.sem_inc(s["raw_free"], 1)
            dve.wait_ge(s["gates"], 2)
            for n, name in enumerate(("wq", "wk", "wv", "wo")):
                dve.wait_ge(s["flag_dma"], 96 + 16 * n)
                src = raw[:, 0:512].rearrange("p (k n) -> p k n", k=KD)
                if name == "wo":
                    ch(v.tensor_scalar(raw[:, 0:512], raw[:, 0:512], gate_x[:, 0:1], None, ALU.mult))
                    ch(v.tensor_scalar(gbo[:, :], gbo[:, :], gate_x[:, 0:1], None, ALU.mult))
                    ch.wait()
                ch(v.tensor_copy(Wr[name][:, 0, :, :], src))
                ch.wait()
                ch(v.tensor_tensor(Wr[name][:, 1, :, :], src, Wr[name][:, 0, :, :].bitcast(F32), ALU.subtract))
                ch.wait()
                dve.sem_inc(s["raw_free"], 1)
            dve.sem_inc(s["const_done"], 1)

            def free_work(w, item, ins):
                ins.then_inc(free[w.bank(item)], 1)

            def rstd(c, which):
                var = mv[:, which, :, 1]
                a, y, u, z = (nw[:, which, i, :] for i in range(4))
                c(v.tensor_scalar(a, var, EPS, None, ALU.add))
                c.wait()
                c(v.tensor_scalar(u.bitcast(I32), a.bitcast(I32), 1, None, ALU.logical_shift_right))
                c.wait()
                c(v.tensor_scalar(y.bitcast(I32), u.bitcast(I32), -1.0, float(0x5F3759DF), ALU.mult, ALU.add))
                for _ in range(3):
                    c.wait()
                    c(v.scalar_tensor_tensor(out=u, in0=y, scalar=-0.5, in1=a, op0=ALU.mult, op1=ALU.mult))
                    c.wait()
                    c(v.tensor_tensor(z, u, y, ALU.mult))
                    c.wait()
                    c(v.scalar_tensor_tensor(out=y, in0=z, scalar=1.5, in1=y, op0=ALU.add, op1=ALU.mult))

            def stats(c, which, src):
                for q in range(QT):
                    c(v.bn_stats(st[:, which, q, :], src[:, q, :]))
                wait_reg(dve, c.sem, c.base + c.n)
                for q in range(QT):
                    c(v.bn_aggr(mv[:, which, q, :], st[:, which, q, :]))
                c.wait()
                rstd(c, which)

            def ln1(c, b):
                dve.wait_ge(s["x_in"], 16 * b + 16)
                stats(c, 0, xin)
                c.wait()
                dve.sem_inc(s["stats1"], 1)

            def base(nt, c, b, w):
                for n, item in enumerate(base_items(nt)):
                    kind, m = item
                    dve.wait_ge(s["hi_done"], n_split(nt) * b + n + 1)
                    bank = ps[:, WORK + w.bank(item), :]
                    if kind == "xt":
                        ins = v.tensor_tensor(xt[:, 1, m, :], bank, xt[:, 0, m, :].bitcast(F32), ALU.subtract)
                    elif kind == "ct" and nt == 1:
                        ins = v.tensor_tensor(ct[:, 1, :, 0:P], bank[:, 0:2 * P].rearrange("p (k n) -> p k n", k=2), ct[:, 0, :, 0:P].bitcast(F32), ALU.subtract)
                    elif kind == "ct":
                        ins = v.tensor_tensor(ct[:, 1, m, :], bank, ct[:, 0, m, :].bitcast(F32), ALU.subtract)
                    elif kind == "q":
                        ins = v.scalar_tensor_tensor(out=qb[:, 1, m, :], in0=bank, scalar=bq[:, m:m + 1], in1=qb[:, 0, m, :].bitcast(F32),
                                                     op0=ALU.add, op1=ALU.subtract)
                    elif nt == 1:
                        v.scalar_tensor_tensor(out=kb[:, 1, 0, 0:P], in0=bank[:, 0:P], scalar=bk[:, 0:1], in1=kb[:, 0, 0, 0:P].bitcast(F32),
                                               op0=ALU.add, op1=ALU.subtract)
                        ins = v.scalar_tensor_tensor(out=kb[:, 1, 1, 0:P], in0=bank[:, P:2 * P], scalar=bk[:, 1:2], in1=kb[:, 0, 1, 0:P].bitcast(F32),
                                                     op0=ALU.add, op1=ALU.subtract)
                    else:
                        ins = v.scalar_tensor_tensor(out=kb[:, 1, m, :], in0=bank, scalar=bk[:, m:m + 1], in1=kb[:, 0, m, :].bitcast(F32),
                                                     op0=ALU.add, op1=ALU.subtract)
                    ins.then_inc(s["lo_done"], 1)
                    dve.wait_ge(s["lo_done"], n_split(nt) * b + n + 1)
                    dve.sem_inc(free[w.bank(item)], 1)

            def release_stacks(nt, w, b, g):
                for item in stack_items(nt, g):
                    kind, _, j = item
                    if kind == "qs":
                        dve.wait_ge(s["qs_ready"], 8 * b + 2 * g + j + 1)
                    else:
                        dve.wait_ge(s["ks_ready"], (4 * b + g + 1) if nt == 1 else (8 * b + 2 * g + j + 1))
                    dve.sem_inc(free[w.bank(item)], 1)

            def maxima(nt, w, g):
                for i in range(4 if nt == 1 else 16):
                    item = ("score", g, i)
                    dve.wait_ge(full[w.bank(item)], w.before(item) + 1)
                    bank = ps[:, WORK + w.bank(item), :]
                    if nt == 1:
                        q0 = 2 * (i // 2)
                        dst = mx[:, :].rearrange("p (q j x) -> p q j x", q=QT, j=2)[:, q0:q0 + 2, :, i % 2]
                        ins = v.tensor_reduce(dst, bank.rearrange("p (q j n) -> p q j n", q=2, j=2), AX.X, ALU.max)
                    else:
                        ins = v.tensor_reduce(mx[:, i:i + 1], bank, AX.X, ALU.max)
                    free_work(w, item, ins)

            def negate(nt, w, g, b):
                for i in range(3):
                    item = ("score", g, (4 if nt == 1 else 16) - 1 - i)
                    dve.wait_ge(free[w.bank(item)], w.before(item) + 1)
                dst = MT[:, :, 48:50].rearrange("p q j -> p q j")
                src = mx[:, :].rearrange("p (q j x) -> p q j x", q=QT, j=2)
                for x_ in range(2):
                    ins = v.tensor_scalar(MT[:, :, 48 + 64 * x_:50 + 64 * x_], src[:, :, :, x_], -1.0, None, ALU.mult)
                ins.then_inc(s["neg_done"], 1)

            def prologue(nt, w):
                if nt == 1:
                    v.tensor_copy(mask_s1[:, :, :], mask_s[:, :, bass.ds(tile_reg * P, P)]).then_inc(s["mask_ready"], 1)
                    v.tensor_copy(mask_t1[:, :], mask_t[:, bass.ds(tile_reg, 1), :].rearrange("p a q -> p (a q)")).then_inc(s["mask_ready"], 1)
                else:
                    dve.sem_inc(s["mask_ready"], 2)
                c = Chain(dve, s["chain_v"], ch.n)
                ln1(c, 0)
                prologue.n = c.n
                base(nt, c, 0, w)
                for g in range(HG):
                    release_stacks(nt, w, 0, g)

            def body(nt, b, w, last):
                c = Chain(dve, s["chain_v"], ch.n + prologue.n + b * body.per)
                maxima(nt, w, 0)
                negate(nt, w, 0, b)
                for i in range(1 if nt == 1 else 2):
                    item = ("v", i)
                    dve.wait_ge(full[w.bank(item)], w.before(item) + 1)
                    for j in range(1 if nt == 1 else 2):
                        kt = 2 * i + j
                        ins = v.tensor_tensor(V[:, kt, :, 0:DH], ps[:, WORK + w.bank(item), j * D:(j + 1) * D].rearrange("p (h d) -> p h d", h=H),
                                              bv[:, :].rearrange("p (h d) -> p h d", h=H), ALU.add)
                    free_work(w, item, ins)
                    dve.wait_ge(free[w.bank(item)], w.before(item) + 1)
                dve.sem_inc(s["v_ready"], 1)
                if not last:
                    ln1(c, b + 1)
                    base(nt, c, b + 1, w)
                for g in range(HG):
                    if g + 1 < HG:
                        maxima(nt, w, g + 1)
                    item = ("shift", g)
                    dve.wait_ge(full[w.bank(item)], w.before(item) + 1)
                    for j in range(2):
                        ins = v.tensor_tensor(QS[:, 2 * g + j, :], ps[:, WORK + w.bank(item), :], QS[:, 2 * g + j, :].bitcast(F32), ALU.add)
                        if j == 0:
                            c(ins)
                    ins.then_inc(s["aug_done"], 1)
                    c.wait()
                    dve.wait_ge(s["aug_done"], b * HG + g + 1)
                    dve.sem_inc(free[w.bank(item)], 1)
                    if g + 1 < HG:
                        negate(nt, w, g + 1, b)
                    if not last:
                        release_stacks(nt, w, b + 1, g)
                    dve.wait_ge(s["av_done"], (b * HG + g + 1) * nt + 2)
                    c(v.transpose(T1[:, :, :].rearrange("p a n -> p (a n)"), ps[:, AV, :]))
                    c.wait()
                    dve.sem_inc(s["av_free"], 1)
                    c(v.reciprocal(den[:, :], T1[:, :, DH]))
                    c.wait()
                    ab = g % 2
                    c(v.tensor_tensor(T2[:, :, ab * DH:(ab + 1) * DH], T1[:, :, 0:DH], den[:, :].unsqueeze(2).to_broadcast([P, S // 32, DH]), ALU.mult))
                    c.wait()
                    if ab:
                        c(v.transpose(T3[:, :], T2[:, :, :].rearrange("p a n -> p (a n)")))
                        c.wait()
                        c(v.tensor_copy(OT[:, 0, g // 2, :], T3[:, :]))
                        c.wait()
                        v.tensor_tensor(OT[:, 1, g // 2, :], T3[:, :], OT[:, 0, g // 2, :].bitcast(F32), ALU.subtract).then_inc(s["ot_ready"], 1)
                        dve.wait_ge(s["ot_ready"], 2 * b + g // 2 + 1)
                dve.wait_ge(s["xres_done"], b + 1)
                if isinstance(b, int) and b > 0 or not isinstance(b, int):
                    pass
                dve.wait_ge(s["x1_stored"], 16 * b + 16)
                for i in range(2):
                    item = ("proj", i)
                    dve.wait_ge(full[w.bank(item)], w.before(item) + 1)
                    v.tensor_tensor(x1[:, 2 * i:2 * i + 2, :], ps[:, WORK + w.bank(item), :].rearrange("p (q d) -> p q d", q=2),
                                    xres[:, 2 * i:2 * i + 2, :], ALU.add).then_inc(s["x1_done"], 1)
                    dve.wait_ge(s["x1_done"], 2 * b + i + 3)
                    dve.sem_inc(free[w.bank(item)], 1)
                stats(c, 1, x1)
                c.wait()
                dve.sem_inc(s["stats1"], 1)
                for k in range(2):
                    item = ("x2t", k)
                    dve.wait_ge(s["x2t_done"], 2 * b + k + 1)
                    dve.sem_inc(free[w.bank(item)], 1)
                item = ("logits",)
                L, X, Pr, EQ, PEN, O1, O2, TM = (lg[:, i, :, :] for i in range(8))
                m1, r1, i1, m2, i2, sl1, sl2, _ = (l1[:, i, :] for i in range(8))

                def bc(a):
                    return a.unsqueeze(2).to_broadcast([P, QT, E])

                def bce(a):
                    return a.unsqueeze(1).to_broadcast([P, QT, E])

                dve.wait_ge(full[w.bank(item)], w.before(item) + 1)
                c(v.tensor_tensor(TM, ps[:, WORK + w.bank(item), 0:QT * E].rearrange("p (q e) -> p q e", q=QT), bce(rb[:, :]), ALU.add))
                c.wait()
                dve.sem_inc(free[w.bank(item)], 1)
                c(v.tensor_reduce(m1, TM, AX.X, ALU.max))
                c.wait()
                v.tensor_tensor(L, TM, bc(m1), ALU.subtract).then_inc(s["exp_log"], 1)
                dve.wait_ge(s["exp_log"], 2 * b + 2)
                c(v.tensor_reduce(r1, X, AX.X, ALU.add))
                c.wait()
                c(v.reciprocal(i1, r1))
                c.wait()
                c(v.tensor_tensor(Pr, X, bc(i1), ALU.mult))
                c.wait()

                def pick(src, m, idx, o):
                    c(v.tensor_reduce(m, src, AX.X, ALU.max))
                    c.wait()
                    c(v.tensor_tensor(EQ, src, bc(m), ALU.is_equal))
                    c.wait()
                    c(v.scalar_tensor_tensor(out=PEN, in0=EQ, scalar=-100.0, in1=bce(lane[:, :]), op0=ALU.mult, op1=ALU.add))
                    c.wait()
                    c(v.tensor_reduce(idx, PEN, AX.X, ALU.min))
                    c.wait()
                    c(v.tensor_tensor(o, PEN, bc(idx), ALU.is_equal))
                    c.wait()

                pick(Pr, m1, i1, O1)
                c(v.scalar_tensor_tensor(out=TM, in0=O1, scalar=-2.0, in1=Pr, op0=ALU.mult, op1=ALU.add))
                c.wait()
                pick(TM, m2, i2, O2)
                c(v.tensor_tensor(Cb[:, :, :], O1, O2, ALU.add))
                c.wait()
                for q in range(QT):
                    c(v.tensor_tensor(Rb[:, q + 1, :], Rb[:, q, :], Cb[:, q, :], ALU.add))
                    c.wait()
                dve.sem_inc(s["comb_done"], 1)
                c(v.tensor_tensor(L, O1, bc(m1), ALU.mult))
                c(v.tensor_tensor(X, O2, bc(m2), ALU.mult))
                c.wait()
                c(v.tensor_tensor(TM, L, X, ALU.add))
                c.wait()
                dve.wait_ge(s["xn2_done"], b + 1)
                c(v.tensor_scalar(pay[:, :, D + 1:ROW], TM, gate_f[:, 0:1], None, ALU.mult))
                c(v.tensor_copy(pay[:, :, D].bitcast(I32), tokf[:, :]))
                c.wait()
                c(v.tensor_scalar(tokf[:, :], tokf[:, :], float(S), None, ALU.add))
                item = ("rank",)
                dve.wait_ge(full[w.bank(item)], w.before(item) + 1)
                c(v.tensor_tensor(PEN, ps[:, WORK + w.bank(item), 0:QT * E].rearrange("p (q e) -> p q e", q=QT), bce(region[:, :]), ALU.add))
                c.wait()
                dve.sem_inc(free[w.bank(item)], 1)
                c(v.tensor_tensor(L, O1, PEN, ALU.mult))
                c(v.tensor_tensor(X, O2, PEN, ALU.mult))
                c.wait()
                c(v.tensor_reduce(sl1, L, AX.X, ALU.add))
                c(v.tensor_reduce(sl2, X, AX.X, ALU.add))
                c.wait()
                c(v.tensor_copy(slot_i[:, 0, :], sl1))
                c(v.tensor_copy(slot_i[:, 1, :], sl2))
                c(v.tensor_copy(Rb[:, 0, :], Rb[:, QT, :]))
                c.wait()
                dve.sem_inc(s["slots_done"], 1)
                if not last:
                    body.count = c.n
                else:
                    body.count_last = c.n

            LN = 4 + 4 + 3 + 9
            body.per = 2 * LN + 5 + 12 + 4 + 3 + 12 + 1 + 4 + 2 + 1 + 2 + 1 + 1 + 2 + 2 + 3
            prologue.n = LN
            dve.wait_ge(s["pre"], 1)
            tile_reg = dve.value_load(flag_i[0:1, 1:2], min_val=0, max_val=QT - 1)
            both(dve, lambda nt: batches(dve, nt, prologue, body))
            assert body.count == body.per, (body.count, body.per)

            c = Chain(dve, s["chain_v"], ch.n + LN + 7 * body.per + body.count_last)
            dve.wait_ge(s["counted"], 1)
            c(v.tensor_copy(counts[:, :], ps[:, 6, 0:E]))
            c(v.memset(pads[:, :, :], 0.0))
            c.wait()
            for h in range(2):
                c(v.tensor_tensor(pad_i[:, h, :], counts[:, :], padrow0[:, h, :], ALU.add))
                c(v.tensor_scalar(pads[:, h, D:D + 1].bitcast(I32), padrow0[:, h, 0:1], float(TOK), None, ALU.add))
            c.wait()
            dve.sem_inc(s["pads_set"], 1)
            c(v.tensor_scalar(ti[:, 0:E], counts[0:1, :], float(TILE - 1), None, ALU.add))
            c.wait()
            c(v.tensor_scalar(ti[:, E:2 * E], ti[:, 0:E], TILE.bit_length() - 1, None, ALU.logical_shift_right))
            c.wait()
            c(v.tensor_scalar(tf[:, 0:E], ti[:, E:2 * E], 1.0, None, ALU.max))
            c(v.memset(tf[:, E:2 * E], 0.0))
            c.wait()
            for e in range(1, E):
                c(v.tensor_tensor(tf[:, E + e:E + e + 1], tf[:, E + e - 1:E + e], tf[:, e - 1:e], ALU.add))
                c.wait()
            c(v.tensor_copy(tiles_i[:, :], tf[:, 0:2 * E]))
            c.wait()
            dve.sem_inc(s["tiles_done"], 1)

            def low_x(n):
                dve.wait_ge(s["xt_hi"], n + 1)
                v.tensor_tensor(xet[:, 1, :, :], ps[:, 5, :].rearrange("p (k n) -> p k n", k=2), xet[:, 0, :, :].bitcast(F32),
                                ALU.subtract).then_inc(s["xt_lo"], 1)

            low_x(0)

            def expert(e, par, nxt):
                n = dve.value_load(tiles_i[0:1, bass.ds(e, 1)], min_val=1, max_val=TOK // TILE)
                base_ = dve.value_load(tiles_i[0:1, bass.ds(e + E, 1)], min_val=0, max_val=2 * TOK // TILE + E)

                def tile(T, split):
                    for p in range(4):
                        dve.wait_ge(s["act_f"], 4 * T + p + 5)
                        v.tensor_tensor(hr[:, 1, p, :], hf[:, p, :], hr[:, 0, p, :].bitcast(F32), ALU.subtract).then_inc(s["h_lo"], 1)
                        if split:
                            dve.wait_ge(s["w_hi"], 4 * e + p + 1)
                            v.tensor_tensor(w_part(1 - par, 1, p), w_raw(p), w_part(1 - par, 0, p).bitcast(F32), ALU.subtract).then_inc(s["w_lo"], 1)
                    low_x(T + 1)
                    dve.wait_ge(s["down_done"], 4 * T + 8)
                    dve.wait_ge(s["meta_dma"], 16 * T + 16)
                    dve.wait_ge(s["added"], 32 * T + 16)
                    for half in range(2):
                        ins = v.tensor_scalar(ye[:, half, :], ps[:, 3 + half, 0:D], meta[:, half, bass.ds(e + 1, 1)], None, ALU.mult)
                    ins.then_inc(s["y_done"], 1)

                tile(base_, nxt)
                with dve.If(n > 1):
                    with dve.Fori(1, n) as i:
                        tile(dve.snap(base_ + i), False)
                dve.end_ifs()

            with dve.Fori(0, E // 2 - 1) as k:
                expert(2 * k, 0, True)
                expert(2 * k + 1, 1, True)
            expert(E - 2, 0, True)
            expert(E - 1, 1, False)

        @block.gpsimd
        def _(pool):
            g_ = nc.gpsimd
            ch = Chain(pool, s["chain_p"])
            ch(g_.memset(x1[:, 0:2, :], 0.0))
            ch.wait()
            for h, name in enumerate(("scattered", "added")):
                pool.dma_start(out[TOK + h * P:TOK + (h + 1) * P, :], x1[:, h, :]).then_inc(s[name], 16)
                pool.wait_ge(s[name], 16)
            pool.sem_inc(s["x1_stored"], 16)
            pool.sem_inc(s["pre"], 1)

            def normalise(b, x_, mean, r, dst, done, chain_sem, need):
                for q in range(QT):
                    ins = g_.tensor_scalar(dst[:, q, 0:D], x_[:, q, :], mean[:, q:q + 1], r[:, q:q + 1], ALU.subtract, ALU.mult)
                ins.then_inc(s[done], 1)

            def ln1(b):
                wait_reg(pool, s["stats1"], 2 * b + 1 if not isinstance(b, int) or b else 1)
                normalise(b, xin, mv[:, 0, :, 0], nw[:, 0, 1, :], xn, "xn_done", None, None)

            def prologue(nt, w):
                ln1(0)

            def split_first(nt):
                wait_reg(pool, s["w_dma"], 32)
                wait_reg(pool, s["v_ready"], B)
                wait_reg(pool, s["qs_ready"], 8 * B)
                wait_reg(pool, s["ks_ready"], 4 * B if nt == 1 else 8 * B)
                g_.tensor_copy(up_r[0][:, 0, :, :], up_raw[:, :, :]).then_inc(s["w_pool"], 1)
                g_.tensor_copy(dn_r[0][:, 0, :, :], dn_raw[:, :, :]).then_inc(s["w_pool"], 1)
                wait_reg(pool, s["w_pool"], 2)
                g_.tensor_tensor(up_r[0][:, 1, :, :], up_raw[:, :, :], up_r[0][:, 0, :, :].bitcast(F32), ALU.subtract).then_inc(s["w_lo"], 2)
                g_.tensor_tensor(dn_r[0][:, 1, :, :], dn_raw[:, :, :], dn_r[0][:, 0, :, :].bitcast(F32), ALU.subtract).then_inc(s["w_lo"], 2)

            def body(nt, b, w, last):
                wait_reg(pool, s["xres_in"], 16 * b + 16)
                ins = g_.tensor_tensor(xres[:, :, :], xres[:, :, :], gbo[:, :].unsqueeze(1).to_broadcast([P, QT, D]), ALU.add)
                ins.then_inc(s["xres_done"], 1)
                if last:
                    split_first(nt)
                if not last:
                    wait_reg(pool, s["stats1"], 2 * b + 2)
                    normalise(b, xin, mv[:, 0, :, 0], nw[:, 0, 1, :], xn, "xn_done", None, None)
                    wait_reg(pool, s["stats1"], 2 * b + 3)
                else:
                    wait_reg(pool, s["stats1"], 2 * b + 2)
                wait_reg(pool, s["scattered"], 16 * 8 * b + 16)
                normalise(b, x1, mv[:, 1, :, 0], nw[:, 1, 1, :], pay, "xn2_done", None, None)
                wait_reg(pool, s["slots_done"], b + 1)
                for q in range(QT):
                    for j in range(2):
                        pool.indirect_dma_start(routed, bass.IndirectOffsetOnAxis(ap=slot_i[:, j, q:q + 1], axis=0),
                                                pay[:, q, :], None).then_inc(s["scattered"], 16)

            both(pool, lambda nt: batches(pool, nt, prologue, body))

            pool.wait_ge(s["pads_set"], 1)
            for e in range(E):
                for h in range(2):
                    pool.indirect_dma_start(routed, bass.IndirectOffsetOnAxis(ap=pad_i[:, h, e:e + 1], axis=0),
                                            pads[:, h, :], None).then_inc(s["pads_in" if e else "pads0_in"], 16)
            pool.wait_ge(s["tiles_done"], 1)

            def expert(e):
                n = pool.value_load(tiles_i[0:1, bass.ds(e, 1)], min_val=1, max_val=TOK // TILE)
                base_ = pool.value_load(tiles_i[0:1, bass.ds(e + E, 1)], min_val=0, max_val=2 * TOK // TILE + E)
                with pool.Fori(0, n) as i:
                    T = pool.snap(base_ + i)
                    pool.wait_ge(s["meta_dma"], 16 * T + 16)
                    wait_reg(pool, s["y_done"], T + 2)
                    for half in range(2):
                        pool.indirect_dma_start(out, bass.IndirectOffsetOnAxis(ap=meta[:, half, 0:1].bitcast(I32), axis=0),
                                                ye[:, half, :], None, compute_op=ALU.add).then_inc(s["added"], 16)

            pool.wait_ge(s["x1_stored"], 16 * B + 16)
            with pool.Fori(0, E) as e:
                expert(e)
            total = pool.value_load(tiles_i[0:1, E - 1:E], min_val=1, max_val=TOK // TILE)
            base_ = pool.value_load(tiles_i[0:1, 2 * E - 1:2 * E], min_val=0, max_val=2 * TOK // TILE + E)
            wait_reg(pool, s["added"], 32 * (total + base_) + 16)


_INPUTS = ["x", "ctx", "mask", "mask_t", "g_xattn", "g_ffn", "wq", "bq", "wk", "bk", "wv", "bv", "wo", "bo",
           "router_w", "router_b", "up", "down", "ident", "trimat", "selq", "selk", "key_ones", "region",
           "padrow0", "lane", "tokens"]


def shape_constants():
    rows = np.arange(P)
    c = {"ident": np.eye(P, dtype=np.float32), "trimat": np.triu(np.ones((P, P), np.float32), 1)}
    selq = np.zeros((P, 4, 2, P), np.float32)
    selk = np.zeros((P, 4, 2, P), np.float32)
    for pair in range(4):
        for x in range(2):
            for d in range(DH):
                r = 32 * pair + DH * x + d
                for term, (pq, pk) in enumerate(((0, 0), (1, 0), (0, 1))):
                    selq[r, pair, pq, 64 * x + DH * term + d] = 1
                    selk[r, pair, pk, 64 * x + DH * term + d] = 1
    c["selq"], c["selk"] = selq.reshape(P, -1), selk.reshape(P, -1)
    ones = np.zeros((P, 2), np.float32)
    for j in range(2):
        ones[[48 + j, 112 + j], j] = 1
    c["key_ones"] = ones
    c["region"] = np.tile((np.arange(E) * CAP).astype(np.float32), (P, 1))
    c["padrow0"] = (np.arange(E)[None, None] * CAP + np.arange(2)[None, :, None] * P + rows[:, None, None]).astype(np.float32)
    c["lane"] = np.tile(np.arange(E, dtype=np.float32), (P, 1))
    c["tokens"] = (np.arange(QT)[None] * P + rows[:, None]).astype(np.float32)
    return c


def kernel(x, ctx_1024, mask_1x1xSxS2_ik0, g_xattn, g_ffn, L0_xattn_wq, L0_xattn_bq, L0_xattn_wk, L0_xattn_bk,
           L0_xattn_wv, L0_xattn_bv, L0_xattn_wo, L0_xattn_bo, L0_ffn_router_w, L0_ffn_router_b,
           L0_ffn_expert_up, L0_ffn_expert_down):
    import concourse.bacc as bacc
    from concourse.bass_utils import run_bass_kernel_spmd

    mask = np.asarray(mask_1x1xSxS2_ik0)[0, 0]
    wo = np.asarray(L0_xattn_wo).T.reshape(2, 2, 4, DH, D).transpose(0, 2, 1, 3, 4).reshape(D, D)
    arrays = {
        "x": x, "ctx": ctx_1024, "mask": mask, "mask_t": mask.T, "g_xattn": g_xattn, "g_ffn": g_ffn,
        "wq": np.asarray(L0_xattn_wq).T, "bq": np.asarray(L0_xattn_bq).reshape(KD, P).T, "wk": np.asarray(L0_xattn_wk).T, "bk": np.asarray(L0_xattn_bk).reshape(KD, P).T,
        "wv": np.asarray(L0_xattn_wv).T, "bv": L0_xattn_bv, "wo": wo, "bo": L0_xattn_bo,
        "router_w": L0_ffn_router_w, "router_b": L0_ffn_router_b,
        "up": np.asarray(L0_ffn_expert_up).transpose(0, 2, 1), "down": np.asarray(L0_ffn_expert_down).transpose(0, 2, 1),
        **shape_constants(),
    }
    nc = bacc.Bacc("TRN2", target_bir_lowering=False, num_devices=1)
    t, feeds = {}, {}
    for name in _INPUTS:
        a = np.ascontiguousarray(arrays[name])
        feeds[f"in_{name}"] = a
        t[name] = nc.dram_tensor(f"in_{name}", a.shape, mybir.dt.from_np(a.dtype), kind="ExternalInput").ap()
    t["out"] = nc.dram_tensor("out_rows", (TOK + TILE, D), F32, kind="ExternalOutput").ap()
    xattn_moe(nc, t)
    r = run_bass_kernel_spmd(nc, [feeds], core_ids=[0])
    return r.results[0]["out_rows"][:TOK].reshape(B, S, D)
```

```python
from contextlib import ExitStack

import concourse.bass as bass
import numpy as np
from concourse import mybir

F32 = mybir.dt.float32
F32R = mybir.dt.float32r
BF16 = mybir.dt.bfloat16
I32 = mybir.dt.int32
ACT = mybir.ActivationFunctionType
ALU = mybir.AluOpType
AX = mybir.AxisListType

P = 128
B, S, D = 8, 512, 256
H, DH = 16, 16
HG = 4
E, FF = 8, 1024
QT = S // P
KD = D // P
TOK = B * S
CAP = TOK + 2 * P
TILE = 2 * P
ROW = D + 1 + E
MASKED = -(2.0 ** 100)
SCALE = DH ** -0.5
EPS = 1e-5


def score_items(nt, ahead, g):
    return [("score", ahead, g, i) for i in range(4 if nt == 1 else 16)]


def stack_items(nt, g):
    return [("qs", g, 0), ("qs", g, 1)] + [("ks", g, j) for j in range(1 if nt == 1 else 2)]


def input_items(nt):
    return [("xt", k) for k in range(2)] + [("ct", k) for k in range(1 if nt == 1 else 2)]


def project_items(nt):
    return [("q", m) for m in range(2)] + [("k", m) for m in range(1 if nt == 1 else 2)]


def v_items(nt):
    return [("v", i) for i in range(1 if nt == 1 else 2)]


def prologue_items(nt):
    return (input_items(nt) + project_items(nt) + stack_items(nt, 0) + score_items(nt, 1, 0) + stack_items(nt, 1)
            + [("shift", 1, 0)] + stack_items(nt, 2) + score_items(nt, 1, 1) + stack_items(nt, 3) + v_items(nt))


def body_items(nt):
    return ([("shift", 0, 1), ("proj", 0), ("proj", 1)] + score_items(nt, 0, 2)
            + [("shift", 0, 2)] + input_items(nt) + score_items(nt, 0, 3) + [("x2t", 0), ("x2t", 1)]
            + [("shift", 0, 3)] + project_items(nt) + [("logits",)] + stack_items(nt, 0)
            + stack_items(nt, 1) + [("rank",)] + score_items(nt, 1, 0) + stack_items(nt, 2) + [("shift", 1, 0)]
            + stack_items(nt, 3) + score_items(nt, 1, 1) + v_items(nt))


TAIL_ITEMS = [("proj", 0), ("proj", 1), ("x2t", 0), ("x2t", 1), ("logits",), ("rank",)]


class Work:

    def __init__(self, items, base, prev=None):
        self.at, used = {}, [0, 0, 0]
        for n, item in enumerate(items):
            self.at[item] = (n % 3, used[n % 3])
            used[n % 3] += 1
        self.used, self.base, self.prev = used, base, prev

    def bank(self, item):
        return self.at[item][0]

    def before(self, item):
        bank, n = self.at[item]
        return self.base[bank] + n


def xattn_moe(nc, t):
    out = t["out"]
    routed = nc.dram_tensor("routed", (E * CAP, ROW), F32).ap()

    with ExitStack() as ctx:
        def sb(name, shape, dt=F32):
            return ctx.enter_context(nc.sbuf_tensor(name, shape, dt))

        def sem(name):
            return ctx.enter_context(nc.semaphore(name))

        ident = sb("ident", [P, P])
        identb = sb("identb", [P, P], BF16)
        trib = sb("trib", [P, P], BF16)
        onesb = sb("onesb", [P, P], BF16)
        key_ones = sb("key_ones", [P, 2])
        region = sb("region", [P, E])
        padrow0 = sb("padrow0", [P, 2, E])
        lane = sb("lane", [P, E])
        gate_x = sb("gate_x", [P, 1])
        gate_f = sb("gate_f", [P, 1])
        consts = sb("consts", [P, 4])
        rw = sb("rw", [P, KD, E])
        rb = sb("rb", [P, E])
        counts = sb("counts", [P, E])
        tiles_i = sb("tiles_i", [1, 2 * E], I32)
        flag_i = sb("flag_i", [1, 2], I32)

        sbA = ExitStack()
        sb_outer = sb

        def sba(name, shape, dt=F32):
            return sbA.enter_context(nc.sbuf_tensor(name, shape, dt))

        raw = sba("raw", [P, 2048])
        xin = sba("xin", [P, QT, D])
        cin = sba("cin", [P, QT, D])
        xt = sba("xt_r", [P, 2, KD, S], F32R)
        ct = sba("ct_r", [P, 2, KD, S], F32R)
        qb = sba("qb_r", [P, 2, KD, S], F32R)
        kb = sba("kb_r", [P, 2, KD, S], F32R)
        Wr = {n: sba(f"{n}_r", [P, 2, KD, D], F32R) for n in ("wq", "wk", "wv", "wo")}
        selq = sba("selq_r", [P, 4, 2, P], F32R)
        selk = sba("selk_r", [P, 4, 2, P], F32R)
        bq = sba("bq_c", [P, 2])
        bk = sba("bk_c", [P, 2])
        bv = sba("bv_b", [P, D])
        gbo = sba("gbo_b", [P, D])
        mask_s = sba("mask_s", [P, QT, S], BF16)
        mask_t = sba("mask_t", [P, QT, S], BF16)
        mask_s1 = sba("mask_s1", [P, QT, P], BF16)
        mask_t1 = sba("mask_t1", [P, S], BF16)
        any_q = sba("any_q", [P, QT, QT])
        any_b = sba("any_b", [P, QT, QT], BF16)
        small = sba("small", [P, 32])
        xn = sba("xn", [P, QT, D])
        xres = sba("xres", [P, QT, D])
        QS = sba("QS_r", [P, 8, S], F32R)
        KS = sba("KS_r", [P, 8, S], F32R)
        V = sba("V", [P, QT, H, 32])
        prob = sba("prob", [P, 2, 4, S])
        mx = sba("mx", [P, 16])
        MT = sba("MT", [P, QT, P])
        T1 = sba("T1", [P, S // 32, 32])
        T2 = sba("T2", [P, S // 32, 32])
        T3 = sba("T3", [P, S])
        den = sba("den", [P, S // 32])
        OT = sba("OT_r", [P, 2, 2, S], F32R)
        x2t = sba("x2t", [P, KD, S])
        st = sba("st", [P, 2, QT, 6])
        mv = sba("mv", [P, 2, QT, 2])
        nw = sba("nw", [P, 2, 5, QT])
        lg = sba("lg", [P, 8, QT, E])
        l1 = sba("l1", [P, 8, QT])
        Cb = sba("Cb", [P, QT, E], BF16)
        Rb = sba("Rb", [P, QT + 1, E], BF16)
        slot_i = sba("slot_i", [P, 2, QT], I32)
        tokf = sba("tokf", [P, QT])
        x1 = sba("x1", [P, QT, D])
        pay = sba("pay", [P, QT, ROW])

        sbA.close()
        sbE = ExitStack()

        def sbe(name, shape, dt=F32):
            return sbE.enter_context(nc.sbuf_tensor(name, shape, dt))

        up_raw = sbe("up_raw", [P, KD, FF])
        dn_raw = sbe("dn_raw", [P, FF // P, D])
        up_r, dn_r = [], []
        for i in range(2):
            up_r.append(sbe(f"up_r{i}", [P, 2, KD, FF], F32R))
            dn_r.append(sbe(f"dn_r{i}", [P, 2, FF // P, D], F32R))
        xe = sbe("xe", [P, 2, ROW])
        meta = sbe("meta", [P, 2, 1 + E])
        xet = sbe("xet_r", [P, 2, KD, TILE], F32R)
        hf = sbe("hf", [P, 4, 2 * TILE])
        hr = sbe("hr_r", [P, 2, 4, 2 * TILE], F32R)
        ye = sbe("ye", [P, 2, D])
        pads = sbe("pads", [P, 2, ROW])
        pad_i = sbe("pad_i", [P, 2, E], I32)
        tf = sbe("tf", [1, 4 * E])
        ti = sbe("ti", [1, 2 * E], I32)
        sbE.close()

        ps = ctx.enter_context(nc.psum_tensor("ps", [P, 8, S], F32))
        psb = ps
        UPB = [0, 1, 2, 6]
        WORK, SC, AV = 0, 3, 7

        names = """const_dma raw_free const_done flag_dma flag_act flag_pe flag_done mask_ready gates
            x_in ctx_in xres_in guess1 guess2 step1 step2 scale1 scale2 xn_done xres_done hi_done 
            neg_done aug_done st_full exp_done av_done av_free ot_ready x1_done x1_stored xn2_done
            log_in log_exp comb_done slots_done scattered chain_v chain_a chain_p zero_out
            counted tiles_done pads_set pads_in w_dma w_hi w_lo pads0_in w_pool x_dma meta_dma
            x_used xt_hi xt_lo up_full act_f act_r h_lo down_done y_full y_done added xt_full pre passed""".split()
        s = {n: sem(n) for n in names}
        full = [sem(f"work_full{i}") for i in range(3)]
        free = [sem(f"work_free{i}") for i in range(3)]

        block = ctx.enter_context(nc.Block())

        class Chain:

            def __init__(self, eng, sem_, base=0):
                self.eng, self.sem, self.n, self.base = eng, sem_, 0, base

            def __call__(self, ins):
                self.n += 1
                ins.then_inc(self.sem, 1)
                return ins

            def wait(self):
                self.eng.wait_ge(self.sem, self.base + self.n)

        def wait_reg(eng, sem_, value):
            eng.wait_ge(sem_, value)
            eng.sem_inc(s["passed"], 1)

        def both(eng, run, extra=None):
            eng.wait_ge(s["flag_done"], 1)
            fast = eng.value_load(flag_i[0:1, 0:1], min_val=0, max_val=1)
            with eng.If(fast == 1):
                run(1)
            with eng.Else():
                run(QT)
            eng.end_ifs()

        def batches(eng, nt, prologue, body, tail=None):
            items = body_items(nt)
            start = Work(prologue_items(nt), [0, 0, 0])
            used = Work(items, None).used

            def work(b):
                base = [start.used[i] + b * used[i] for i in range(3)]
                back = [start.used[i] + (b - 1) * used[i] for i in range(3)]
                return Work(items, base, start if isinstance(b, int) and b == 0 else Work(items, back))

            prologue(nt, start)
            body(nt, 0, work(0), False, True)
            with eng.Fori(1, B - 1) as b:
                body(nt, b, work(b), True, True)
            body(nt, B - 1, work(B - 1), True, False)
            if tail:
                tail(nt, Work(TAIL_ITEMS, [start.used[i] + B * used[i] for i in range(3)]))

        def n_split(nt):
            return 4 + 2 * (1 if nt == 1 else 2)

        def split_no(nt, item):
            return (input_items(nt) + project_items(nt)).index(item)

        def w_raw(j):
            return up_raw[:, j, :] if j < 2 else dn_raw[:, 4 * j - 8:4 * j - 4, :].rearrange("p c d -> p (c d)")

        def w_part(par, low, j):
            return up_r[par][:, low, j, :] if j < 2 else dn_r[par][:, low, 4 * j - 8:4 * j - 4, :].rearrange("p c d -> p (c d)")

        CONST = ["ident", "trimat", "selq", "selk"]

        @block.sync
        def _(sp):
            sp.dma_start(key_ones[:, :], t["key_ones"]).then_inc(s["const_dma"], 16)
            sp.dma_start(region[:, :], t["region"]).then_inc(s["const_dma"], 16)
            sp.dma_start(padrow0[:, :, :], t["padrow0"]).then_inc(s["const_dma"], 16)
            sp.dma_start(lane[:, :], t["lane"]).then_inc(s["const_dma"], 16)
            sp.dma_start(ident[:, :], t["ident"]).then_inc(s["const_dma"], 16)
            sp.dma_start(rw[:, :, :], t["router_w"].rearrange("(k p) e -> p k e", p=P)).then_inc(s["const_dma"], 16)
            sp.dma_start(rb[:, :], t["router_b"].unsqueeze(0).to_broadcast([P, E])).then_inc(s["const_dma"], 16)
            sp.dma_start(gate_x[:, :], t["g_xattn"].unsqueeze(0).to_broadcast([P, 1])).then_inc(s["const_dma"], 16)
            sp.dma_start(gate_f[:, :], t["g_ffn"].unsqueeze(0).to_broadcast([P, 1])).then_inc(s["const_dma"], 16)
            sp.dma_start(bq[:, :], t["bq"]).then_inc(s["const_dma"], 16)
            sp.dma_start(bk[:, :], t["bk"]).then_inc(s["const_dma"], 16)
            sp.dma_start(bv[:, :], t["bv"].unsqueeze(0).to_broadcast([P, D])).then_inc(s["const_dma"], 16)
            sp.dma_start(gbo[:, :], t["bo"].unsqueeze(0).to_broadcast([P, D])).then_inc(s["const_dma"], 16)
            sp.dma_start(tokf[:, :], t["tokens"]).then_inc(s["const_dma"], 16)
            stage = [(raw[:, 0:2048].bitcast(I32).rearrange("p (t k) -> p t k", t=QT), t["mask"].rearrange("(t p) k -> p t k", p=P)),
                     (raw[:, 0:2048].bitcast(I32).rearrange("p (t k) -> p t k", t=QT), t["mask_t"].rearrange("(t p) k -> p t k", p=P)),
                     (raw[:, 0:P], t["trimat"]),
                     (raw[:, 0:1024], t["selq"]),
                     (raw[:, 0:1024], t["selk"])]
            stage += [(raw[:, 0:512].rearrange("p (k n) -> p k n", k=KD), t[n].rearrange("(k p) n -> p k n", p=P))
                      for n in ("wq", "wk", "wv", "wo")]
            for n, (dst, src) in enumerate(stage):
                if n:
                    sp.wait_ge(s["raw_free"], n)
                sp.dma_start(dst, src).then_inc(s["flag_dma"], 16)

            def load_x(n, row):
                sp.wait_ge(s["xn_done"], n) if not (isinstance(n, int) and n == 0) else None
                sp.dma_start(xin[:, :, :], t["x"][bass.ds(row, 1)].rearrange("a (q p) d -> p (a q) d", p=P)).then_inc(s["x_in"], 16)

            def load_ctx(nt, b):
                if nt == 1:
                    src = t["ctx"][bass.ds(b, 1), bass.ds(tile_reg * P, P), :].rearrange("a p d -> p (a d)")
                    sp.dma_start(cin[:, 0, :], src).then_inc(s["ctx_in"], 16)
                else:
                    sp.dma_start(cin[:, :, :], t["ctx"][bass.ds(b, 1)].rearrange("a (q p) d -> p (a q) d", p=P)).then_inc(s["ctx_in"], 16)

            def load_xres(b):
                sp.dma_start(xres[:, :, :], t["x"][bass.ds(b, 1)].rearrange("a (q p) d -> p (a q) d", p=P)).then_inc(s["xres_in"], 16)

            def store_x1(b):
                sp.dma_start(out[bass.ds(b * S, S), :].rearrange("(q p) d -> p q d", p=P), x1[:, :, :]).then_inc(s["x1_stored"], 16)

            def prologue(nt, w):
                load_x(0, 0)
                load_ctx(nt, 0)
                load_xres(0)
                load_x(1, 1)

            def body(nt, b, w, has_before, has_next):
                if has_next:
                    sp.wait_ge(s["hi_done"], n_split(nt) * b + len(input_items(nt)))
                    load_ctx(nt, b + 1)
                    load_x(b + 2, b + 2 if isinstance(b, int) else
                           nc.s_assert_within(sp.snap(((b + 2) < B) * (b + 2)), 0, B - 1, skip_runtime_bounds_check_because="it is 0 past the last batch"))
                else:
                    sp.wait_ge(s["xn_done"], B + 1)
                    sp.wait_ge(s["hi_done"], n_split(nt) * B)
                    load_w(0)
                if has_before:
                    sp.wait_ge(s["x1_done"], 2 * b)
                    load_xres(b)
                    store_x1(b - 1)

            def tail(nt, w):
                sp.wait_ge(s["x1_done"], 2 * B)
                store_x1(B - 1)

            def load_w(e):
                sp.dma_start(up_raw[:, :, :], t["up"][bass.ds(e, 1)].rearrange("a (k p) f -> p (a k) f", p=P)).then_inc(s["w_dma"], 16)
                sp.dma_start(dn_raw[:, :, :], t["down"][bass.ds(e, 1)].rearrange("a (c p) d -> p (a c) d", p=P)).then_inc(s["w_dma"], 16)

            sp.wait_ge(s["flag_done"], 1)
            tile_reg = sp.value_load(flag_i[0:1, 1:2], min_val=0, max_val=QT - 1)
            both(sp, lambda nt: batches(sp, nt, prologue, body, tail))

            sp.wait_ge(s["tiles_done"], 1)
            sp.wait_ge(s["scattered"], 16 * 2 * TOK // P + 16)
            sp.wait_ge(s["pads0_in"], 16 * 2)
            sp.dma_start(xe[:, :, :], routed[0:TILE, :].rearrange("(h p) r -> p h r", p=P)).then_inc(s["x_dma"], 16)

            def expert(e, nxt):
                n = sp.value_load(tiles_i[0:1, bass.ds(e, 1)], min_val=1, max_val=TOK // TILE)
                base = sp.value_load(tiles_i[0:1, bass.ds(e + E, 1)], min_val=0, max_val=2 * TOK // TILE + E)
                if nxt:
                    sp.wait_ge(s["w_lo"], 4 * e + 4)
                    load_w(e + 1)
                sp.wait_ge(s["pads_in"], 16 * 2 * (E - 1))
                with sp.Fori(0, n) as i:
                    sp.wait_ge(s["xt_full"], base + i + 1)
                    sp.dma_start(xe[:, :, :], routed[bass.ds(next_row(e, i, n), TILE), :].rearrange("(h p) r -> p h r", p=P)).then_inc(s["x_dma"], 16)
                    sp.wait_ge(s["added"], 32 * (base + i) + 16)
                    sp.dma_start(meta[:, :, :], routed[bass.ds(within(e * CAP + i * TILE), TILE), D:ROW].rearrange("(h p) r -> p h r", p=P)).then_inc(s["meta_dma"], 16)

            def within(row):
                return nc.s_assert_within(row, 0, E * CAP - TILE, skip_runtime_bounds_check_because="an expert has at most TOK rows and the padding")

            def next_row(e, i, n):
                more = sp.snap((i + 1) < n)
                return within(more * (e * CAP + (i + 1) * TILE) + (1 - more) * nxt_row(e))

            def nxt_row(e):
                return ((e + 1) % E) * CAP

            with sp.Fori(0, E // 2 - 1) as k:
                expert(2 * k, True)
                expert(2 * k + 1, True)
            expert(E - 2, True)
            expert(E - 1, False)

        @block.scalar
        def _(act):
            ch = Chain(act, s["chain_a"])
            act.wait_ge(s["const_dma"], 16 * 14)
            nc.scalar.activation(gate_x[:, :], gate_x[:, :], ACT.Tanh).then_inc(s["gates"], 1)
            nc.scalar.activation(gate_f[:, :], gate_f[:, :], ACT.Tanh).then_inc(s["gates"], 1)

            def hi(w, item, dst, src, bias=None):
                act.wait_ge(full[w.bank(item)], w.before(item) + 1)
                if bias is None:
                    ins = nc.scalar.activation(dst, src, ACT.Copy)
                else:
                    ins = nc.scalar.activation(dst, src, ACT.Identity, bias=bias)
                return ins

            def split(nt, w, items):
                for item in items:
                    kind, m = item
                    bank = ps[:, WORK + w.bank(item), :]
                    if kind == "xt":
                        ins = hi(w, item, xt[:, 0, m, :], bank)
                    elif kind == "ct" and nt == 1:
                        ins = hi(w, item, ct[:, 0, :, 0:P], bank[:, 0:2 * P].rearrange("p (k n) -> p k n", k=2))
                    elif kind == "ct":
                        ins = hi(w, item, ct[:, 0, m, :], bank)
                    elif kind == "q":
                        ins = hi(w, item, qb[:, 0, m, :], bank, bq[:, m:m + 1])
                    elif nt == 1:
                        hi(w, item, kb[:, 0, 0, 0:P], bank[:, 0:P], bk[:, 0:1])
                        ins = nc.scalar.activation(kb[:, 0, 1, 0:P], bank[:, P:2 * P], ACT.Identity, bias=bk[:, 1:2])
                    else:
                        ins = hi(w, item, kb[:, 0, m, :], bank, bk[:, m:m + 1])
                    ins.then_inc(s["hi_done"], 1)

            def stacks(nt, w, g):
                for item in stack_items(nt, g):
                    kind, _, j = item
                    act.wait_ge(full[w.bank(item)], w.before(item) + 1)
                    bank = ps[:, WORK + w.bank(item), :]
                    if kind == "qs":
                        ins = nc.scalar.activation(QS[:, 2 * g + j, :], bank, ACT.Copy)
                    elif nt == 1:
                        for jj in range(2):
                            for x_ in range(2):
                                r = slice(64 * x_, 64 * x_ + 64)
                                ins = nc.scalar.activation(KS[r, 2 * g + jj, x_ * P:(x_ + 1) * P], bank[r, jj * P:(jj + 1) * P],
                                                           ACT.Identity, bias=key_ones[r, jj:jj + 1])
                    else:
                        ins = nc.scalar.activation(KS[:, 2 * g + j, :], bank, ACT.Identity, bias=key_ones[:, j:j + 1])
                    ins.then_inc(free[w.bank(item)], 1)

            def exps(nt, b, g):
                for kt in range(nt):
                    u = (b * HG + g) * nt + kt
                    slot = (g * nt + kt) % 2
                    for j in range(2):
                        act.wait_ge(s["st_full"], 2 * u + j + 1)
                        if j == 0:
                            act.wait_ge(s["av_done"], u + 1)
                        nc.scalar.activation(prob[:, slot, 2 * j:2 * j + 2, :], ps[:, SC + 2 * j:SC + 2 * j + 2, :],
                                             ACT.Exp, scale=SCALE).then_inc(s["exp_done"], 1)

            def copy_x2t(w):
                for k in range(2):
                    item = ("x2t", k)
                    act.wait_ge(full[w.bank(item)], w.before(item) + 1)
                    nc.scalar.activation(x2t[:, k, :], ps[:, WORK + w.bank(item), :], ACT.Copy).then_inc(free[w.bank(item)], 1)

            def exp_logits(n):
                act.wait_ge(s["log_in"], n + 1)
                nc.scalar.activation(lg[:, 1, :, :], lg[:, 0, :, :], ACT.Exp).then_inc(s["log_exp"], 1)

            def normalise(k, x_, dst):
                for q in range(QT):
                    ins = nc.scalar.activation(dst[:, q, 0:D], x_[:, q, :], ACT.Identity, scale=nw[:, k, 1, q:q + 1], bias=nw[:, k, 4, q:q + 1])
                return ins

            def normalise1(n):
                act.wait_ge(s["scale1"], n + 1)
                normalise(0, xin, xn).then_inc(s["xn_done"], 1)

            def normalise2(n):
                act.wait_ge(s["scattered"], 16 * 8 * n + 16)
                act.wait_ge(s["scale2"], n + 1)
                normalise(1, x1, pay).then_inc(s["xn2_done"], 1)

            def prologue(nt, w):
                normalise1(0)
                split(nt, w, input_items(nt) + project_items(nt))
                for g in range(HG):
                    stacks(nt, w, g)
                normalise1(1)

            def body(nt, b, w, has_before, has_next):
                exps(nt, b, 0)
                exps(nt, b, 1)
                if has_next:
                    split(nt, w, input_items(nt))
                if has_before:
                    normalise2(b - 1)
                    copy_x2t(w)
                exps(nt, b, 2)
                if has_next:
                    split(nt, w, project_items(nt))
                if has_before:
                    exp_logits(b - 1)
                if has_next:
                    stacks(nt, w, 0)
                exps(nt, b, 3)
                if has_next:
                    for g in range(1, HG):
                        stacks(nt, w, g)
                    normalise1(b + 2)

            def tail(nt, w):
                normalise2(B - 1)
                copy_x2t(w)
                exp_logits(B - 1)

            both(act, lambda nt: batches(act, nt, prologue, body, tail))

            act.wait_ge(s["tiles_done"], 1)

            def high_x(n):
                act.wait_ge(s["xt_full"], n + 1)
                nc.scalar.activation(xet[:, 0, :, :], ps[:, 5, :].rearrange("p (k n) -> p k n", k=2), ACT.Copy).then_inc(s["xt_hi"], 1)

            high_x(0)

            def expert(e, par, nxt):
                n = act.value_load(tiles_i[0:1, bass.ds(e, 1)], min_val=1, max_val=TOK // TILE)
                base_ = act.value_load(tiles_i[0:1, bass.ds(e + E, 1)], min_val=0, max_val=2 * TOK // TILE + E)

                def tile(T, split):
                    for p in range(4):
                        act.wait_ge(s["up_full"], 4 * T + p + 1)
                        act.wait_ge(s["down_done"], 4 * T + p + 1)
                        bank = ps[:, UPB[p], :]
                        nc.scalar.activation(hr[:, 0, p, :], bank, ACT.Gelu).then_inc(s["act_r"], 1)
                        nc.scalar.activation(hf[:, p, :], bank, ACT.Gelu).then_inc(s["act_f"], 1)
                        if split:
                            if p == 0:
                                act.wait_ge(s["w_dma"], 32 * e + 64)
                                act.wait_ge(s["down_done"], 4 * T + 4)
                            nc.scalar.activation(w_part(1 - par, 0, p), w_raw(p), ACT.Copy).then_inc(s["w_hi"], 1)
                    high_x(T + 1)

                tile(base_, nxt)
                with act.If(n > 1):
                    with act.Fori(1, n) as i:
                        tile(act.snap(base_ + i), False)
                act.end_ifs()

            with act.Fori(0, E // 2 - 1) as k:
                expert(2 * k, 0, True)
                expert(2 * k + 1, 1, True)
            expert(E - 2, 0, True)
            expert(E - 1, 1, False)

        @block.tensor
        def _(pe):
            def mm(o, a, b_, start, stop):
                return pe.matmul(o, a, b_, start=start, stop=stop, skip_group_check=True)

            def three(o, a_h, a_l, b_h, b_l, parts):
                n = 0
                for k in parts:
                    for x_, y_ in ((a_h, b_h), (a_l, b_h), (a_h, b_l)):
                        ins = mm(o, x_(k), y_(k), n == 0, n == 3 * len(parts) - 1)
                        n += 1
                return ins

            pe.wait_ge(s["flag_pe"], 1)
            for qt in range(QT):
                ins = mm(ps[:, 0, 0:QT], onesb[:, :], any_b[:, qt, :], qt == 0, qt == QT - 1)
            ins.then_inc(s["flag_act"], 1)
            pe.wait_ge(s["const_done"], 1)

            def take(w, item, made=(), made_by=None):
                latest = {}
                for other in made:
                    latest[(made_by or w).bank(other)] = other
                for bank, other in latest.items():
                    if bank != w.bank(item):
                        pe.wait_ge(free[bank], (made_by or w).before(other) + 1)
                n = w.before(item)
                if not (isinstance(n, int) and n <= 0):
                    pe.wait_ge(free[w.bank(item)], n)
                return ps[:, WORK + w.bank(item), :]

            def give(w, item, ins):
                ins.then_inc(full[w.bank(item)], 1)

            def skip(w, items):
                for item in items:
                    take(w, item)
                    pe.sem_inc(full[w.bank(item)], 1)
                    pe.sem_inc(free[w.bank(item)], 1)

            def is_read(w, item):
                pe.wait_ge(free[w.bank(item)], w.before(item) + 1)

            def inputs(nt, w, n):
                for item in input_items(nt):
                    kind, m = item
                    if kind == "xt":
                        pe.wait_ge(s["xn_done"], n + 1)
                        o = take(w, item)
                        for q in range(QT):
                            ins = pe.transpose(o[:, q * P:(q + 1) * P], xn[:, q, m * P:(m + 1) * P], ident[:, :])
                    else:
                        pe.wait_ge(s["ctx_in"], 16 * n + 16)
                        o = take(w, item)
                        for j in range(2 if nt == 1 else QT):
                            src = cin[:, 0, j * P:(j + 1) * P] if nt == 1 else cin[:, j, m * P:(m + 1) * P]
                            ins = pe.transpose(o[:, j * P:(j + 1) * P], src, ident[:, :])
                    give(w, item, ins)

            def project(nt, w):
                for item in project_items(nt):
                    kind, m = item
                    if kind == "q":
                        o = take(w, item, [("xt", 0), ("xt", 1)])
                        ins = three(o, lambda k: Wr["wq"][:, 0, k, m * P:(m + 1) * P], lambda k: Wr["wq"][:, 1, k, m * P:(m + 1) * P],
                                    lambda k: xt[:, 0, k, :], lambda k: xt[:, 1, k, :], range(KD))
                    else:
                        o = take(w, item, input_items(nt)[2:])
                        for mk in (range(2) if nt == 1 else [m]):
                            dst = o[:, mk * P:(mk + 1) * P] if nt == 1 else o
                            ins = three(dst, lambda k: Wr["wk"][:, 0, k, mk * P:(mk + 1) * P], lambda k: Wr["wk"][:, 1, k, mk * P:(mk + 1) * P],
                                        lambda k: ct[:, 0, k, 0:nt * P], lambda k: ct[:, 1, k, 0:nt * P], range(KD))
                    give(w, item, ins)

            def values(nt, w):
                for item in v_items(nt):
                    o = take(w, item)
                    for j in range(1 if nt == 1 else 2):
                        kt = 2 * item[1] + j
                        ins = three(o[:, j * D:(j + 1) * D], lambda k: ct[:, 0, k, kt * P:(kt + 1) * P], lambda k: ct[:, 1, k, kt * P:(kt + 1) * P],
                                    lambda k: Wr["wv"][:, 0, k, :], lambda k: Wr["wv"][:, 1, k, :], range(KD))
                    give(w, item, ins)

            def stacks(nt, w, g):
                for item in stack_items(nt, g):
                    kind, _, j = item
                    if kind == "qs":
                        o = take(w, item, [("q", (2 * g + j) // 4)])
                        pair = 2 * g + j
                        mm(o, selq[:, pair % 4, 0, :], qb[:, 0, pair // 4, :], True, False)
                        ins = mm(o, selq[:, pair % 4, 1, :], qb[:, 1, pair // 4, :], False, True)
                    else:
                        o = take(w, item, [project_items(nt)[2 if nt == 1 else 2 + (2 * g + j) // 4]])
                        for jj in (range(2) if nt == 1 else [j]):
                            pair = 2 * g + jj
                            dst = o[:, jj * P:(jj + 1) * P] if nt == 1 else o
                            mm(dst, selk[:, pair % 4, 0, :], kb[:, 0, pair // 4, 0:nt * P], True, False)
                            ins = mm(dst, selk[:, pair % 4, 1, :], kb[:, 1, pair // 4, 0:nt * P], False, True)
                    give(w, item, ins)

            def scores(nt, w, ahead, g):
                made_by = w if ahead else w.prev
                for item in score_items(nt, ahead, g):
                    i = item[3]
                    o = take(w, item, stack_items(nt, g) if i == 0 else (), made_by)
                    if nt == 1:
                        mm(o.rearrange("p (h n) -> p h n", h=4), identb[:, :], mask_s1[:, i, :].unsqueeze(1).to_broadcast([P, 4, P]), True, False)
                        for j in range(2):
                            ins = mm(o[:, j * 2 * P:(j + 1) * 2 * P], QS[:, 2 * g + j, i * P:(i + 1) * P], KS[:, 2 * g + j, 0:2 * P], False, j == 1)
                    else:
                        q, h = i // 4, i % 4
                        pair, r = 2 * g + h // 2, 64 * (h % 2)
                        mm(o, identb[:, :], mask_s[:, q, :], True, False)
                        ins = mm(o, QS[r:r + 64, pair, q * P:(q + 1) * P], KS[r:r + 64, pair, :], False, True)
                    give(w, item, ins)

            def shift(w, b, ahead, g):
                pe.wait_ge(s["neg_done"], b * HG + g + 1)
                item = ("shift", ahead, g)
                o = take(w, item)
                for q in range(QT):
                    ins = pe.transpose(o[:, q * P:(q + 1) * P], MT[:, q, :], ident[:, :])
                give(w, item, ins)

            def av(nt, w, b, g, kt):
                u = (b * HG + g) * nt + kt
                pe.wait_ge(s["exp_done"], 2 * u + 2 + 2)
                if g == 0 and kt == 0:
                    for item in v_items(nt):
                        is_read(w.prev, item)
                if kt == 0:
                    pe.wait_ge(s["av_free"], b * HG + g + 1)
                slot = (g * nt + kt) % 2
                for h in range(4):
                    ins = mm(ps[32 * h:32 * h + 32, AV, :], V[:, kt, 4 * g + h, :], prob[:, slot, h, :], kt == 0, kt == nt - 1)
                ins.then_inc(s["av_done"], 1)

            def shifted(nt, w, b, g):
                pe.wait_ge(s["aug_done"], b * HG + g + 1)
                for kt in range(nt):
                    u = (b * HG + g) * nt + kt
                    for j in range(2):
                        pe.wait_ge(s["exp_done"], 2 * u + j + 1)
                        for x_ in range(2):
                            pair, r = 2 * g + j, 64 * x_
                            o = ps[:, SC + 2 * j + x_, :]
                            mm(o, identb[:, :], mask_t1[:, :] if nt == 1 else mask_t[:, kt, :], True, False)
                            keys = x_ if nt == 1 else kt
                            ins = mm(o, KS[r:r + 64, pair, keys * P:(keys + 1) * P], QS[r:r + 64, pair, :], False, True)
                        ins.then_inc(s["st_full"], 1)
                    if kt:
                        av(nt, w, b, g, kt - 1)

            def proj(w, n):
                pe.wait_ge(s["ot_ready"], 2 * n + 2)
                for i in range(2):
                    item = ("proj", i)
                    o = take(w, item)
                    for j in range(2):
                        q = 2 * i + j
                        ins = three(o[:, j * D:(j + 1) * D], lambda k: OT[:, 0, k, q * P:(q + 1) * P], lambda k: OT[:, 1, k, q * P:(q + 1) * P],
                                    lambda k: Wr["wo"][:, 0, k, :], lambda k: Wr["wo"][:, 1, k, :], range(KD))
                    give(w, item, ins)

            def turn_x2(w, n):
                pe.wait_ge(s["xn2_done"], n + 1)
                for k in range(2):
                    item = ("x2t", k)
                    o = take(w, item)
                    for q in range(QT):
                        ins = pe.transpose(o[:, q * P:(q + 1) * P], pay[:, q, k * P:(k + 1) * P], ident[:, :])
                    give(w, item, ins)

            def logits(w):
                item = ("logits",)
                o = take(w, item, [("x2t", 0), ("x2t", 1)])
                for q in range(QT):
                    for k in range(KD):
                        ins = mm(o[:, q * E:(q + 1) * E], x2t[:, k, q * P:(q + 1) * P], rw[:, k, :], k == 0, k == KD - 1)
                give(w, item, ins)

            def rank(w, n):
                pe.wait_ge(s["comb_done"], n + 1)
                item = ("rank",)
                o = take(w, item)
                mm(o[:, 0:QT * E], trib[:, :], Cb[:, :, :].rearrange("p t e -> p (t e)"), True, False)
                ins = mm(o[:, 0:QT * E], onesb[:, :], Rb[:, 0:QT, :].rearrange("p t e -> p (t e)"), False, True)
                give(w, item, ins)

            def prologue(nt, w):
                pe.wait_ge(s["mask_ready"], 3)
                inputs(nt, w, 0)
                project(nt, w)
                stacks(nt, w, 0)
                scores(nt, w, 1, 0)
                stacks(nt, w, 1)
                shift(w, 0, 1, 0)
                stacks(nt, w, 2)
                scores(nt, w, 1, 1)
                stacks(nt, w, 3)
                values(nt, w)

            def body(nt, b, w, has_before, has_next):
                def before(run, items, *args):
                    run(w, *args) if has_before else skip(w, items)

                def ahead(run, items, *args):
                    run(*args) if has_next else skip(w, items)

                shifted(nt, w, b, 0)
                shift(w, b, 0, 1)
                before(proj, [("proj", 0), ("proj", 1)], b - 1)
                scores(nt, w, 0, 2)
                av(nt, w, b, 0, nt - 1)
                shifted(nt, w, b, 1)
                shift(w, b, 0, 2)
                ahead(inputs, input_items(nt), nt, w, b + 1)
                scores(nt, w, 0, 3)
                before(turn_x2, [("x2t", 0), ("x2t", 1)], b - 1)
                av(nt, w, b, 1, nt - 1)
                shifted(nt, w, b, 2)
                shift(w, b, 0, 3)
                ahead(project, project_items(nt), nt, w)
                before(logits, [("logits",)])
                av(nt, w, b, 2, nt - 1)
                ahead(stacks, stack_items(nt, 0), nt, w, 0)
                shifted(nt, w, b, 3)
                ahead(stacks, stack_items(nt, 1), nt, w, 1)
                before(rank, [("rank",)], b - 1)
                ahead(scores, score_items(nt, 1, 0), nt, w, 1, 0)
                ahead(stacks, stack_items(nt, 2), nt, w, 2)
                ahead(shift, [("shift", 1, 0)], w, b + 1, 1, 0)
                av(nt, w, b, 3, nt - 1)
                ahead(stacks, stack_items(nt, 3), nt, w, 3)
                ahead(scores, score_items(nt, 1, 1), nt, w, 1, 1)
                ahead(values, v_items(nt), nt, w)

            def tail(nt, w):
                proj(w, B - 1)
                turn_x2(w, B - 1)
                logits(w)
                rank(w, B - 1)

            both(pe, lambda nt: batches(pe, nt, prologue, body, tail))

            pe.wait_ge(s["slots_done"], B)
            mm(ps[:, 6, 0:E], onesb[:, :], Rb[:, 0, :], True, True).then_inc(s["counted"], 1)

            def transpose_x(n):
                pe.wait_ge(s["x_dma"], 16 * n + 16)
                pe.wait_ge(s["xt_lo"], n + 1)
                for k in range(KD):
                    for h in range(2):
                        ins = pe.transpose(ps[:, 5, k * TILE + h * P:k * TILE + (h + 1) * P], xe[:, h, k * P:(k + 1) * P], ident[:, :])
                ins.then_inc(s["xt_full"], 1)

            pe.wait_ge(s["tiles_done"], 1)
            transpose_x(0)

            def expert(e, par):
                n = pe.value_load(tiles_i[0:1, bass.ds(e, 1)], min_val=1, max_val=TOK // TILE)
                base_ = pe.value_load(tiles_i[0:1, bass.ds(e + E, 1)], min_val=0, max_val=2 * TOK // TILE + E)
                wait_reg(pe, s["w_lo"], 4 * e + 4)
                with pe.Fori(0, n) as i:
                    T = pe.snap(base_ + i)

                    def up(p):
                        pe.wait_ge(s["act_f"], 4 * T + p + 1)
                        for c in range(2 * p, 2 * p + 2):
                            ins = three(ps[:, UPB[p], (c % 2) * TILE:(c % 2 + 1) * TILE],
                                        lambda k: up_r[par][:, 0, k, c * P:(c + 1) * P], lambda k: up_r[par][:, 1, k, c * P:(c + 1) * P],
                                        lambda k: xet[:, 0, k, :], lambda k: xet[:, 1, k, :], range(KD))
                        ins.then_inc(s["up_full"], 1)

                    def down(p):
                        pe.wait_ge(s["h_lo"], 4 * T + p + 1)
                        if p == 0:
                            pe.wait_ge(s["y_done"], T + 1)
                        for half in range(2):
                            n_ = 0
                            for c in range(2):
                                hs = slice(c * TILE + half * P, c * TILE + (half + 1) * P)
                                for a, b_ in ((0, 0), (1, 0), (0, 1)):
                                    ins = mm(ps[:, 3 + half, 0:D], hr[:, a, p, hs], dn_r[par][:, b_, 2 * p + c, :],
                                             p == 0 and n_ == 0, p == 3 and n_ == 5)
                                    n_ += 1
                        ins.then_inc(s["down_done"], 1)

                    pe.wait_ge(s["xt_lo"], T + 2)
                    up(0)
                    up(1)
                    up(2)
                    down(0)
                    up(3)
                    down(1)
                    pe.wait_ge(s["x_dma"], 16 * T + 32)
                    for k in range(KD):
                        for h in range(2):
                            ins = pe.transpose(ps[:, 5, k * TILE + h * P:k * TILE + (h + 1) * P], xe[:, h, k * P:(k + 1) * P], ident[:, :])
                    ins.then_inc(s["xt_full"], 1)
                    down(2)
                    down(3)

            with pe.Fori(0, E // 2) as k:
                expert(2 * k, 0)
                expert(2 * k + 1, 1)

        @block.vector
        def _(dve):
            v = nc.vector
            ch = Chain(dve, s["chain_v"])

            ch(v.memset(onesb[:, :], 1.0))
            ch(v.memset(MT[:, :, :], 0.0))
            ch(v.memset(V[:, :, :, :], 1.0))
            ch(v.memset(Rb[:, :, :], 0.0))
            for n, value in enumerate((-0.5, 1.5, -1.0, 0.0)):
                ch(v.memset(consts[:, n:n + 1], value))
            dve.sem_inc(s["av_free"], 1)
            dve.sem_inc(s["exp_done"], 2)
            dve.sem_inc(s["av_done"], 2)
            dve.sem_inc(s["act_f"], 4)
            dve.sem_inc(s["down_done"], 4)
            dve.sem_inc(s["xt_lo"], 1)
            dve.sem_inc(s["y_done"], 1)

            rawi = raw[:, 0:2048].bitcast(I32).rearrange("p (t k) -> p t k", t=QT)
            dve.wait_ge(s["flag_dma"], 16)
            ch(v.tensor_scalar(mask_s[:, :, :], rawi, 0.0, MASKED, ALU.is_equal, ALU.mult))
            ch.wait()
            dve.sem_inc(s["raw_free"], 1)
            for q in range(QT):
                ch(v.tensor_reduce(any_q[:, q, :], mask_s[:, q, :].rearrange("p (a n) -> p a n", a=QT), AX.X, ALU.max))
            ch.wait()
            ch(v.tensor_scalar(any_b[:, :, :], any_q[:, :, :], 0.0, None, ALU.is_equal))
            ch.wait()
            dve.sem_inc(s["flag_pe"], 1)
            dve.wait_ge(s["flag_act"], 1)
            ch(v.tensor_scalar(small[:, 10:14], ps[:, 0, 0:QT], float(S), None, ALU.is_equal))
            ch(v.tensor_reduce(small[:, 14:15], ps[:, 0, 0:QT], AX.X, ALU.add))
            ch.wait()
            dve.wait_ge(s["const_dma"], 16 * 14)
            ch(v.tensor_tensor(small[:, 16:20], small[:, 10:14], lane[:, 0:QT], ALU.mult))
            ch(v.tensor_reduce(small[:, 15:16], small[:, 10:14], AX.X, ALU.max))
            ch(v.tensor_scalar(small[:, 20:21], small[:, 14:15], float(S), None, ALU.is_equal))
            ch.wait()
            ch(v.tensor_reduce(small[:, 22:23], small[:, 16:20], AX.X, ALU.max))
            ch(v.tensor_tensor(small[:, 21:22], small[:, 20:21], small[:, 15:16], ALU.mult))
            ch.wait()
            ch(v.tensor_copy(flag_i[0:1, :], small[0:1, 21:23]))
            ch.wait()
            dve.wait_ge(s["flag_dma"], 32)
            ch(v.tensor_scalar(mask_t[:, :, :], rawi, 0.0, MASKED, ALU.is_equal, ALU.mult))
            ch.wait()
            dve.sem_inc(s["raw_free"], 1)
            dve.sem_inc(s["flag_done"], 1)
            dve.wait_ge(s["flag_dma"], 48)
            ch(v.tensor_copy(trib[:, :], raw[:, 0:P]))
            ch(v.tensor_copy(identb[:, :], ident[:, :]))
            ch.wait()
            dve.sem_inc(s["raw_free"], 1)
            for n, tile in enumerate((selq, selk)):
                dve.wait_ge(s["flag_dma"], 64 + 16 * n)
                ch(v.tensor_copy(tile[:, :, :, :], raw[:, 0:1024].rearrange("p (a b c) -> p a b c", a=4, b=2)))
                ch.wait()
                dve.sem_inc(s["raw_free"], 1)
            dve.wait_ge(s["gates"], 2)
            for n, name in enumerate(("wq", "wk", "wv", "wo")):
                dve.wait_ge(s["flag_dma"], 96 + 16 * n)
                src = raw[:, 0:512].rearrange("p (k n) -> p k n", k=KD)
                if name == "wo":
                    ch(v.tensor_scalar(raw[:, 0:512], raw[:, 0:512], gate_x[:, 0:1], None, ALU.mult))
                    ch(v.tensor_scalar(gbo[:, :], gbo[:, :], gate_x[:, 0:1], None, ALU.mult))
                    ch.wait()
                ch(v.tensor_copy(Wr[name][:, 0, :, :], src))
                ch.wait()
                ch(v.tensor_tensor(Wr[name][:, 1, :, :], src, Wr[name][:, 0, :, :].bitcast(F32), ALU.subtract))
                ch.wait()
                dve.sem_inc(s["raw_free"], 1)
            dve.sem_inc(s["const_done"], 1)

            def wait_full(w, item):
                dve.wait_ge(full[w.bank(item)], w.before(item) + 1)
                return ps[:, WORK + w.bank(item), :]

            def norm(c, k, x_no=None):
                if k == 0:
                    dve.wait_ge(s["x_in"], 16 * x_no + 16)
                for q in range(QT):
                    c(v.bn_stats(st[:, k, q, :], (xin, x1)[k][:, q, :]))
                wait_reg(dve, c.sem, c.base + c.n)
                for q in range(QT):
                    c(v.bn_aggr(mv[:, k, q, :], st[:, k, q, :]))
                c.wait()
                a, y, u = (nw[:, k, i, :] for i in range(3))
                c(v.tensor_scalar(a, mv[:, k, :, 1], EPS, None, ALU.add))
                c.wait()
                c(v.tensor_scalar(u.bitcast(I32), a.bitcast(I32), 1, None, ALU.logical_shift_right))
                c.wait()
                v.tensor_scalar(y.bitcast(I32), u.bitcast(I32), -1.0, float(0x5F3759DF), ALU.mult, ALU.add).then_inc(s[("guess1", "guess2")[k]], 1)

            def split(nt, w, b, items):
                for item in items:
                    kind, m = item
                    dve.wait_ge(s["hi_done"], n_split(nt) * b + split_no(nt, item) + 1)
                    bank = ps[:, WORK + w.bank(item), :]
                    if kind == "xt":
                        ins = v.tensor_tensor(xt[:, 1, m, :], bank, xt[:, 0, m, :].bitcast(F32), ALU.subtract)
                    elif kind == "ct" and nt == 1:
                        ins = v.tensor_tensor(ct[:, 1, :, 0:P], bank[:, 0:2 * P].rearrange("p (k n) -> p k n", k=2), ct[:, 0, :, 0:P].bitcast(F32), ALU.subtract)
                    elif kind == "ct":
                        ins = v.tensor_tensor(ct[:, 1, m, :], bank, ct[:, 0, m, :].bitcast(F32), ALU.subtract)
                    elif kind == "q":
                        ins = v.scalar_tensor_tensor(out=qb[:, 1, m, :], in0=bank, scalar=bq[:, m:m + 1], in1=qb[:, 0, m, :].bitcast(F32),
                                                     op0=ALU.add, op1=ALU.subtract)
                    elif nt == 1:
                        v.scalar_tensor_tensor(out=kb[:, 1, 0, 0:P], in0=bank[:, 0:P], scalar=bk[:, 0:1], in1=kb[:, 0, 0, 0:P].bitcast(F32),
                                               op0=ALU.add, op1=ALU.subtract)
                        ins = v.scalar_tensor_tensor(out=kb[:, 1, 1, 0:P], in0=bank[:, P:2 * P], scalar=bk[:, 1:2], in1=kb[:, 0, 1, 0:P].bitcast(F32),
                                                     op0=ALU.add, op1=ALU.subtract)
                    else:
                        ins = v.scalar_tensor_tensor(out=kb[:, 1, m, :], in0=bank, scalar=bk[:, m:m + 1], in1=kb[:, 0, m, :].bitcast(F32),
                                                     op0=ALU.add, op1=ALU.subtract)
                    ins.then_inc(free[w.bank(item)], 1)

            def maxima(nt, w, ahead, g):
                items = score_items(nt, ahead, g)
                for i, item in enumerate(items):
                    bank = wait_full(w, item)
                    if nt == 1:
                        ins = v.tensor_reduce(mx[:, 4 * i:4 * i + 4], bank.rearrange("p (h n) -> p h n", h=4), AX.X, ALU.max)
                    else:
                        ins = v.tensor_reduce(mx[:, i:i + 1], bank, AX.X, ALU.max)
                    ins.then_inc(free[w.bank(item)], 1)
                for item in items[-3:]:
                    dve.wait_ge(free[w.bank(item)], w.before(item) + 1)
                src = mx[:, :].rearrange("p (q j x) -> p q j x", q=QT, j=2)
                for x_ in range(2):
                    ins = v.tensor_scalar(MT[:, :, 48 + 64 * x_:50 + 64 * x_], src[:, :, :, x_], -1.0, None, ALU.mult)
                ins.then_inc(s["neg_done"], 1)

            def augment(w, b, ahead, g):
                item = ("shift", ahead, g)
                bank = wait_full(w, item)
                for j in range(2):
                    ins = v.tensor_tensor(QS[:, 2 * g + j, :], bank, QS[:, 2 * g + j, :].bitcast(F32), ALU.add)
                ins.then_inc(s["aug_done"], 1)
                dve.wait_ge(s["aug_done"], b * HG + g + 1)
                dve.sem_inc(free[w.bank(item)], 1)

            def values(nt, w):
                for item in v_items(nt):
                    bank = wait_full(w, item)
                    for j in range(1 if nt == 1 else 2):
                        kt = 2 * item[1] + j
                        ins = v.tensor_tensor(V[:, kt, :, 0:DH], bank[:, j * D:(j + 1) * D].rearrange("p (h d) -> p h d", h=H),
                                              bv[:, :].rearrange("p (h d) -> p h d", h=H), ALU.add)
                    ins.then_inc(free[w.bank(item)], 1)

            def heads_out(nt, c, b, g):
                dve.wait_ge(s["av_done"], (b * HG + g + 1) * nt + 2)
                c(v.transpose(T1[:, :, :].rearrange("p a n -> p (a n)"), ps[:, AV, :]))
                c.wait()
                dve.sem_inc(s["av_free"], 1)
                c(v.reciprocal(den[:, :], T1[:, :, DH]))
                c.wait()
                half = g % 2
                c(v.tensor_tensor(T2[:, :, half * DH:(half + 1) * DH], T1[:, :, 0:DH], den[:, :].unsqueeze(2).to_broadcast([P, S // 32, DH]), ALU.mult))
                c.wait()
                if half:
                    c(v.transpose(T3[:, :], T2[:, :, :].rearrange("p a n -> p (a n)")))
                    c.wait()
                    c(v.tensor_copy(OT[:, 0, g // 2, :], T3[:, :]))
                    c.wait()
                    v.tensor_tensor(OT[:, 1, g // 2, :], T3[:, :], OT[:, 0, g // 2, :].bitcast(F32), ALU.subtract).then_inc(s["ot_ready"], 1)

            def residual(c, w, n):
                dve.wait_ge(s["xres_done"], n + 1)
                dve.wait_ge(s["x1_stored"], 16 * n + 16)
                for i in range(2):
                    item = ("proj", i)
                    bank = wait_full(w, item)
                    v.tensor_tensor(x1[:, 2 * i:2 * i + 2, :], bank.rearrange("p (q d) -> p q d", q=2),
                                    xres[:, 2 * i:2 * i + 2, :], ALU.add).then_inc(s["x1_done"], 1)
                    dve.wait_ge(s["x1_done"], 2 * n + i + 1)
                    dve.sem_inc(free[w.bank(item)], 1)

            L, X, Pr, EQ, PEN, O1, O2, TM = (lg[:, i, :, :] for i in range(8))
            m1, r1, i1, m2, i2, sl1, sl2, _ = (l1[:, i, :] for i in range(8))

            def bc(a):
                return a.unsqueeze(2).to_broadcast([P, QT, E])

            def bce(a):
                return a.unsqueeze(1).to_broadcast([P, QT, E])

            def choose(c, w, n):
                item = ("logits",)
                bank = wait_full(w, item)
                c(v.tensor_tensor(TM, bank[:, 0:QT * E].rearrange("p (q e) -> p q e", q=QT), bce(rb[:, :]), ALU.add))
                c.wait()
                dve.sem_inc(free[w.bank(item)], 1)
                c(v.tensor_reduce(m1, TM, AX.X, ALU.max))
                c.wait()
                v.tensor_tensor(L, TM, bc(m1), ALU.subtract).then_inc(s["log_in"], 1)
                dve.wait_ge(s["log_exp"], n + 1)
                c(v.tensor_reduce(r1, X, AX.X, ALU.add))
                c.wait()
                c(v.reciprocal(i1, r1))
                c.wait()
                c(v.tensor_tensor(Pr, X, bc(i1), ALU.mult))
                c.wait()

                def pick(src, m, idx, o):
                    c(v.tensor_reduce(m, src, AX.X, ALU.max))
                    c.wait()
                    c(v.tensor_tensor(EQ, src, bc(m), ALU.is_equal))
                    c.wait()
                    c(v.scalar_tensor_tensor(out=PEN, in0=EQ, scalar=-100.0, in1=bce(lane[:, :]), op0=ALU.mult, op1=ALU.add))
                    c.wait()
                    c(v.tensor_reduce(idx, PEN, AX.X, ALU.min))
                    c.wait()
                    c(v.tensor_tensor(o, PEN, bc(idx), ALU.is_equal))
                    c.wait()

                pick(Pr, m1, i1, O1)
                c(v.scalar_tensor_tensor(out=TM, in0=O1, scalar=-2.0, in1=Pr, op0=ALU.mult, op1=ALU.add))
                c.wait()
                pick(TM, m2, i2, O2)
                c(v.tensor_tensor(Cb[:, :, :], O1, O2, ALU.add))
                c.wait()
                for q in range(QT):
                    c(v.tensor_tensor(Rb[:, q + 1, :], Rb[:, q, :], Cb[:, q, :], ALU.add))
                    c.wait()
                dve.sem_inc(s["comb_done"], 1)
                c(v.tensor_tensor(L, O1, bc(m1), ALU.mult))
                c(v.tensor_tensor(X, O2, bc(m2), ALU.mult))
                c.wait()
                c(v.tensor_tensor(TM, L, X, ALU.add))
                c.wait()
                c(v.tensor_scalar(pay[:, :, D + 1:ROW], TM, gate_f[:, 0:1], None, ALU.mult))
                c(v.tensor_copy(pay[:, :, D].bitcast(I32), tokf[:, :]))
                c.wait()
                c(v.tensor_scalar(tokf[:, :], tokf[:, :], float(S), None, ALU.add))

            def place(c, w):
                item = ("rank",)
                bank = wait_full(w, item)
                c(v.tensor_tensor(PEN, bank[:, 0:QT * E].rearrange("p (q e) -> p q e", q=QT), bce(region[:, :]), ALU.add))
                c.wait()
                dve.sem_inc(free[w.bank(item)], 1)
                c(v.tensor_tensor(L, O1, PEN, ALU.mult))
                c(v.tensor_tensor(X, O2, PEN, ALU.mult))
                c.wait()
                c(v.tensor_reduce(sl1, L, AX.X, ALU.add))
                c(v.tensor_reduce(sl2, X, AX.X, ALU.add))
                c.wait()
                c(v.tensor_copy(slot_i[:, 0, :], sl1))
                c(v.tensor_copy(slot_i[:, 1, :], sl2))
                c(v.tensor_copy(Rb[:, 0, :], Rb[:, QT, :]))
                c.wait()
                dve.sem_inc(s["slots_done"], 1)

            NORM = 4 + 4 + 2
            HEADS = 2 * 3 + 2 * 5
            ROUTE = 27 + 8
            chained = {"start": 2 * NORM, (False, True): NORM + HEADS, (True, True): 2 * NORM + HEADS + ROUTE,
                       (True, False): NORM + HEADS + ROUTE, "tail": NORM + ROUTE}

            def prologue(nt, w):
                if nt == 1:
                    zeros = MT[:, 0:2, :].rearrange("p a n -> p (a n)").unsqueeze(1).to_broadcast([P, 8, 2 * P])
                    v.tensor_copy(KS[:, :, 0:2 * P], zeros).then_inc(s["mask_ready"], 1)
                    v.tensor_copy(mask_s1[:, :, :], mask_s[:, :, bass.ds(tile_reg * P, P)]).then_inc(s["mask_ready"], 1)
                    v.tensor_copy(mask_t1[:, :], mask_t[:, bass.ds(tile_reg, 1), :].rearrange("p a q -> p (a q)")).then_inc(s["mask_ready"], 1)
                else:
                    dve.sem_inc(s["mask_ready"], 3)
                c = Chain(dve, s["chain_v"], ch.n)
                norm(c, 0, 0)
                split(nt, w, 0, input_items(nt))
                split(nt, w, 0, project_items(nt))
                maxima(nt, w, 1, 0)
                augment(w, 0, 1, 0)
                norm(c, 0, 1)
                maxima(nt, w, 1, 1)
                values(nt, w)
                assert c.n == chained["start"], c.n

            def body(nt, b, w, has_before, has_next):
                base = ch.n + chained["start"]
                if has_before:
                    base = base + chained[False, True] + (b - 1) * chained[True, True]
                c = Chain(dve, s["chain_v"], base)
                augment(w, b, 0, 1)
                if has_before:
                    residual(c, w, b - 1)
                maxima(nt, w, 0, 2)
                if has_before:
                    norm(c, 1)
                heads_out(nt, c, b, 0)
                augment(w, b, 0, 2)
                if has_next:
                    split(nt, w, b + 1, input_items(nt))
                maxima(nt, w, 0, 3)
                heads_out(nt, c, b, 1)
                augment(w, b, 0, 3)
                if has_next:
                    split(nt, w, b + 1, project_items(nt))
                if has_before:
                    choose(c, w, b - 1)
                heads_out(nt, c, b, 2)
                if has_before:
                    place(c, w)
                if has_next:
                    maxima(nt, w, 1, 0)
                    norm(c, 0, b + 2)
                    augment(w, b + 1, 1, 0)
                    maxima(nt, w, 1, 1)
                    values(nt, w)
                heads_out(nt, c, b, 3)
                assert c.n == chained[has_before, has_next], (c.n, has_before, has_next, chained)

            before_tail = ch.n + chained["start"] + chained[False, True] + (B - 2) * chained[True, True] + chained[True, False]

            def tail(nt, w):
                c = Chain(dve, s["chain_v"], before_tail)
                dve.wait_ge(s["ot_ready"], 2 * B)
                residual(c, w, B - 1)
                norm(c, 1)
                choose(c, w, B - 1)
                place(c, w)
                assert c.n == chained["tail"], c.n

            dve.wait_ge(s["pre"], 1)
            tile_reg = dve.value_load(flag_i[0:1, 1:2], min_val=0, max_val=QT - 1)
            both(dve, lambda nt: batches(dve, nt, prologue, body, tail))

            c = Chain(dve, s["chain_v"], before_tail + chained["tail"])
            dve.wait_ge(s["counted"], 1)
            c(v.tensor_copy(counts[:, :], ps[:, 6, 0:E]))
            c(v.memset(pads[:, :, :], 0.0))
            c.wait()
            for h in range(2):
                c(v.tensor_tensor(pad_i[:, h, :], counts[:, :], padrow0[:, h, :], ALU.add))
                c(v.tensor_scalar(pads[:, h, D:D + 1].bitcast(I32), padrow0[:, h, 0:1], float(TOK), None, ALU.add))
            c.wait()
            dve.sem_inc(s["pads_set"], 1)
            c(v.tensor_scalar(ti[:, 0:E], counts[0:1, :], float(TILE - 1), None, ALU.add))
            c.wait()
            c(v.tensor_scalar(ti[:, E:2 * E], ti[:, 0:E], TILE.bit_length() - 1, None, ALU.logical_shift_right))
            c.wait()
            c(v.tensor_scalar(tf[:, 0:E], ti[:, E:2 * E], 1.0, None, ALU.max))
            c(v.memset(tf[:, E:2 * E], 0.0))
            c.wait()
            for e in range(1, E):
                c(v.tensor_tensor(tf[:, E + e:E + e + 1], tf[:, E + e - 1:E + e], tf[:, e - 1:e], ALU.add))
                c.wait()
            c(v.tensor_copy(tiles_i[:, :], tf[:, 0:2 * E]))
            c.wait()
            dve.sem_inc(s["tiles_done"], 1)

            def low_x(n):
                dve.wait_ge(s["xt_hi"], n + 1)
                v.tensor_tensor(xet[:, 1, :, :], ps[:, 5, :].rearrange("p (k n) -> p k n", k=2), xet[:, 0, :, :].bitcast(F32),
                                ALU.subtract).then_inc(s["xt_lo"], 1)

            low_x(0)

            def expert(e, par, nxt):
                n = dve.value_load(tiles_i[0:1, bass.ds(e, 1)], min_val=1, max_val=TOK // TILE)
                base_ = dve.value_load(tiles_i[0:1, bass.ds(e + E, 1)], min_val=0, max_val=2 * TOK // TILE + E)

                def tile(T, split):
                    for p in range(4):
                        dve.wait_ge(s["act_f"], 4 * T + p + 5)
                        v.tensor_tensor(hr[:, 1, p, :], hf[:, p, :], hr[:, 0, p, :].bitcast(F32), ALU.subtract).then_inc(s["h_lo"], 1)
                        if split:
                            dve.wait_ge(s["w_hi"], 4 * e + p + 1)
                            v.tensor_tensor(w_part(1 - par, 1, p), w_raw(p), w_part(1 - par, 0, p).bitcast(F32), ALU.subtract).then_inc(s["w_lo"], 1)
                    low_x(T + 1)
                    dve.wait_ge(s["down_done"], 4 * T + 8)
                    dve.wait_ge(s["meta_dma"], 16 * T + 16)
                    dve.wait_ge(s["added"], 32 * T + 16)
                    for half in range(2):
                        ins = v.tensor_scalar(ye[:, half, :], ps[:, 3 + half, 0:D], meta[:, half, bass.ds(e + 1, 1)], None, ALU.mult)
                    ins.then_inc(s["y_done"], 1)

                tile(base_, nxt)
                with dve.If(n > 1):
                    with dve.Fori(1, n) as i:
                        tile(dve.snap(base_ + i), False)
                dve.end_ifs()

            with dve.Fori(0, E // 2 - 1) as k:
                expert(2 * k, 0, True)
                expert(2 * k + 1, 1, True)
            expert(E - 2, 0, True)
            expert(E - 1, 1, False)

        @block.gpsimd
        def _(pool):
            g_ = nc.gpsimd
            ch = Chain(pool, s["chain_p"])
            ch(g_.memset(x1[:, 0:2, :], 0.0))
            ch.wait()
            for h, name in enumerate(("scattered", "added")):
                pool.dma_start(out[TOK + h * P:TOK + (h + 1) * P, :], x1[:, h, :]).then_inc(s[name], 16)
                pool.wait_ge(s[name], 16)
            pool.sem_inc(s["x1_stored"], 16)
            pool.sem_inc(s["pre"], 1)

            def newton(k, n):
                wait_reg(pool, s[("guess1", "guess2")[k]], n + 1)
                a, y, u, z, shift = (nw[:, k, i, :] for i in range(5))
                done = s[("step1", "step2")[k]]
                base = n * 13
                for i in range(3):
                    g_.tensor_tensor(u, y, y, ALU.mult).then_inc(done, 1)
                    wait_reg(pool, done, base + 4 * i + 1)
                    g_.tensor_tensor(z, u, a, ALU.mult).then_inc(done, 1)
                    wait_reg(pool, done, base + 4 * i + 2)
                    g_.tensor_scalar(u, z, consts[:, 0:1], consts[:, 1:2], ALU.mult, ALU.add).then_inc(done, 1)
                    wait_reg(pool, done, base + 4 * i + 3)
                    g_.tensor_tensor(y, y, u, ALU.mult).then_inc(done, 1)
                    wait_reg(pool, done, base + 4 * i + 4)
                g_.tensor_tensor(z, mv[:, k, :, 0], y, ALU.mult).then_inc(done, 1)
                wait_reg(pool, done, base + 13)
                g_.tensor_scalar(shift, z, consts[:, 2:3], consts[:, 3:4], ALU.mult, ALU.add).then_inc(s[("scale1", "scale2")[k]], 1)

            def add_bias(b):
                wait_reg(pool, s["xres_in"], 16 * b + 16)
                ins = g_.tensor_tensor(xres[:, :, :], xres[:, :, :], gbo[:, :].unsqueeze(1).to_broadcast([P, QT, D]), ALU.add)
                ins.then_inc(s["xres_done"], 1)

            def scatter(n):
                wait_reg(pool, s["slots_done"], n + 1)
                for q in range(QT):
                    for j in range(2):
                        pool.indirect_dma_start(routed, bass.IndirectOffsetOnAxis(ap=slot_i[:, j, q:q + 1], axis=0),
                                                pay[:, q, :], None).then_inc(s["scattered"], 16)

            def prologue(nt, w):
                newton(0, 0)
                add_bias(0)
                newton(0, 1)

            def split_first(w):
                wait_reg(pool, s["w_dma"], 32)
                for i in range(3):
                    wait_reg(pool, free[i], w.base[i])
                g_.tensor_copy(up_r[0][:, 0, :, :], up_raw[:, :, :]).then_inc(s["w_pool"], 1)
                g_.tensor_copy(dn_r[0][:, 0, :, :], dn_raw[:, :, :]).then_inc(s["w_pool"], 1)
                wait_reg(pool, s["w_pool"], 2)
                g_.tensor_tensor(up_r[0][:, 1, :, :], up_raw[:, :, :], up_r[0][:, 0, :, :].bitcast(F32), ALU.subtract).then_inc(s["w_lo"], 2)
                g_.tensor_tensor(dn_r[0][:, 1, :, :], dn_raw[:, :, :], dn_r[0][:, 0, :, :].bitcast(F32), ALU.subtract).then_inc(s["w_lo"], 2)

            def body(nt, b, w, has_before, has_next):
                if has_before:
                    newton(1, b - 1)
                    add_bias(b)
                if not has_next:
                    split_first(w)
                if has_before:
                    scatter(b - 1)
                if has_next:
                    newton(0, b + 2)

            def tail(nt, w):
                newton(1, B - 1)
                scatter(B - 1)

            both(pool, lambda nt: batches(pool, nt, prologue, body, tail))

            pool.wait_ge(s["pads_set"], 1)
            for e in range(E):
                for h in range(2):
                    pool.indirect_dma_start(routed, bass.IndirectOffsetOnAxis(ap=pad_i[:, h, e:e + 1], axis=0),
                                            pads[:, h, :], None).then_inc(s["pads_in" if e else "pads0_in"], 16)
            pool.wait_ge(s["tiles_done"], 1)

            def expert(e):
                n = pool.value_load(tiles_i[0:1, bass.ds(e, 1)], min_val=1, max_val=TOK // TILE)
                base_ = pool.value_load(tiles_i[0:1, bass.ds(e + E, 1)], min_val=0, max_val=2 * TOK // TILE + E)
                with pool.Fori(0, n) as i:
                    T = pool.snap(base_ + i)
                    pool.wait_ge(s["meta_dma"], 16 * T + 16)
                    wait_reg(pool, s["y_done"], T + 2)
                    for half in range(2):
                        pool.indirect_dma_start(out, bass.IndirectOffsetOnAxis(ap=meta[:, half, 0:1].bitcast(I32), axis=0),
                                                ye[:, half, :], None, compute_op=ALU.add).then_inc(s["added"], 16)

            pool.wait_ge(s["x1_stored"], 16 * B + 16)
            with pool.Fori(0, E) as e:
                expert(e)
            total = pool.value_load(tiles_i[0:1, E - 1:E], min_val=1, max_val=TOK // TILE)
            base_ = pool.value_load(tiles_i[0:1, 2 * E - 1:2 * E], min_val=0, max_val=2 * TOK // TILE + E)
            wait_reg(pool, s["added"], 32 * (total + base_) + 16)


_INPUTS = ["x", "ctx", "mask", "mask_t", "g_xattn", "g_ffn", "wq", "bq", "wk", "bk", "wv", "bv", "wo", "bo",
           "router_w", "router_b", "up", "down", "ident", "trimat", "selq", "selk", "key_ones", "region",
           "padrow0", "lane", "tokens"]


def shape_constants():
    rows = np.arange(P)
    c = {"ident": np.eye(P, dtype=np.float32), "trimat": np.triu(np.ones((P, P), np.float32), 1)}
    selq = np.zeros((P, 4, 2, P), np.float32)
    selk = np.zeros((P, 4, 2, P), np.float32)
    for pair in range(4):
        for x in range(2):
            for d in range(DH):
                r = 32 * pair + DH * x + d
                for term, (pq, pk) in enumerate(((0, 0), (1, 0), (0, 1))):
                    selq[r, pair, pq, 64 * x + DH * term + d] = 1
                    selk[r, pair, pk, 64 * x + DH * term + d] = 1
    c["selq"], c["selk"] = selq.reshape(P, -1), selk.reshape(P, -1)
    ones = np.zeros((P, 2), np.float32)
    for j in range(2):
        ones[[48 + j, 112 + j], j] = 1
    c["key_ones"] = ones
    c["region"] = np.tile((np.arange(E) * CAP).astype(np.float32), (P, 1))
    c["padrow0"] = (np.arange(E)[None, None] * CAP + np.arange(2)[None, :, None] * P + rows[:, None, None]).astype(np.float32)
    c["lane"] = np.tile(np.arange(E, dtype=np.float32), (P, 1))
    c["tokens"] = (np.arange(QT)[None] * P + rows[:, None]).astype(np.float32)
    return c


def kernel(x, ctx_1024, mask_1x1xSxS2_ik0, g_xattn, g_ffn, L0_xattn_wq, L0_xattn_bq, L0_xattn_wk, L0_xattn_bk,
           L0_xattn_wv, L0_xattn_bv, L0_xattn_wo, L0_xattn_bo, L0_ffn_router_w, L0_ffn_router_b,
           L0_ffn_expert_up, L0_ffn_expert_down):
    import concourse.bacc as bacc
    from concourse.bass_utils import run_bass_kernel_spmd

    mask = np.asarray(mask_1x1xSxS2_ik0)[0, 0]
    wo = np.asarray(L0_xattn_wo).T.reshape(2, 2, 4, DH, D).transpose(0, 2, 1, 3, 4).reshape(D, D)
    arrays = {
        "x": x, "ctx": ctx_1024, "mask": mask, "mask_t": mask.T, "g_xattn": g_xattn, "g_ffn": g_ffn,
        "wq": np.asarray(L0_xattn_wq).T, "bq": np.asarray(L0_xattn_bq).reshape(KD, P).T, "wk": np.asarray(L0_xattn_wk).T, "bk": np.asarray(L0_xattn_bk).reshape(KD, P).T,
        "wv": np.asarray(L0_xattn_wv).T, "bv": L0_xattn_bv, "wo": wo, "bo": L0_xattn_bo,
        "router_w": L0_ffn_router_w, "router_b": L0_ffn_router_b,
        "up": np.asarray(L0_ffn_expert_up).transpose(0, 2, 1), "down": np.asarray(L0_ffn_expert_down).transpose(0, 2, 1),
        **shape_constants(),
    }
    nc = bacc.Bacc("TRN2", target_bir_lowering=False, num_devices=1)
    t, feeds = {}, {}
    for name in _INPUTS:
        a = np.ascontiguousarray(arrays[name])
        feeds[f"in_{name}"] = a
        t[name] = nc.dram_tensor(f"in_{name}", a.shape, mybir.dt.from_np(a.dtype), kind="ExternalInput").ap()
    t["out"] = nc.dram_tensor("out_rows", (TOK + TILE, D), F32, kind="ExternalOutput").ap()
    xattn_moe(nc, t)
    r = run_bass_kernel_spmd(nc, [feeds], core_ids=[0])
    return r.results[0]["out_rows"][:TOK].reshape(B, S, D)
```

```python
from contextlib import ExitStack

import concourse.bass as bass
import numpy as np
from concourse import mybir

F32 = mybir.dt.float32
F32R = mybir.dt.float32r
BF16 = mybir.dt.bfloat16
I32 = mybir.dt.int32
ACT = mybir.ActivationFunctionType
ALU = mybir.AluOpType
AX = mybir.AxisListType

P = 128
B, S, D = 8, 512, 256
H, DH = 16, 16
HG = 4
E, FF = 8, 1024
QT = S // P
KD = D // P
TOK = B * S
CAP = TOK + 2 * P
TILE = 2 * P
ROW = D + 1 + E
MASKED = -(2.0 ** 100)
SCALE = DH ** -0.5
EPS = 1e-5


def score_items(nt, ahead, g):
    return [("score", ahead, g, i) for i in range(4 if nt == 1 else 16)]


def stack_items(nt, g):
    return [("qs", g, 0), ("qs", g, 1)] + [("ks", g, j) for j in range(1 if nt == 1 else 2)]


def input_items(nt):
    return [("xt", k) for k in range(2)] + [("ct", k) for k in range(1 if nt == 1 else 2)]


def project_items(nt):
    return [("q", m) for m in range(2)] + [("k", m) for m in range(1 if nt == 1 else 2)]


def v_items(nt):
    return [("v", i) for i in range(1 if nt == 1 else 2)]


def prologue_items(nt):
    return (input_items(nt) + project_items(nt) + stack_items(nt, 0) + score_items(nt, 1, 0) + stack_items(nt, 1)
            + [("shift", 1, 0)] + stack_items(nt, 2) + score_items(nt, 1, 1) + stack_items(nt, 3) + v_items(nt))


def body_items(nt):
    return ([("shift", 0, 1)] + score_items(nt, 0, 2) + [("proj", 0), ("proj", 1)]
            + [("shift", 0, 2)] + input_items(nt) + score_items(nt, 0, 3)
            + [("shift", 0, 3), ("x2t", 0), ("x2t", 1)] + project_items(nt) + [("logits",)] + stack_items(nt, 0)
            + stack_items(nt, 1) + score_items(nt, 1, 0) + [("rank",)] + stack_items(nt, 2) + [("shift", 1, 0)]
            + stack_items(nt, 3) + score_items(nt, 1, 1) + v_items(nt))


TAIL_ITEMS = [("proj", 0), ("proj", 1), ("x2t", 0), ("x2t", 1), ("logits",), ("rank",)]


FIXED = {"ident": P, "trimat": P,
         "max_rows": 2,
         "region": E,
         "padrow0": 2 * E,
         "lane": E,
         "tokens": QT}


class Work:

    def __init__(self, items, base, prev=None):
        self.at, used = {}, [0, 0, 0]
        for n, item in enumerate(items):
            self.at[item] = (n % 3, used[n % 3])
            used[n % 3] += 1
        self.used, self.base, self.prev = used, base, prev

    def bank(self, item):
        return self.at[item][0]

    def before(self, item):
        bank, n = self.at[item]
        return self.base[bank] + n


def xattn_moe(nc, t):
    out = t["out"]
    routed = nc.dram_tensor("routed", (E * CAP, ROW), F32).ap()

    with ExitStack() as ctx:
        def sb(name, shape, dt=F32):
            return ctx.enter_context(nc.sbuf_tensor(name, shape, dt))

        def sem(name):
            return ctx.enter_context(nc.semaphore(name))

        fixed = sb("fixed", [P, sum(FIXED.values())])
        view, at = {}, 0
        for name, width in FIXED.items():
            view[name] = fixed[:, at:at + width]
            at += width
        ident, max_rows, region, lane, tokf = (view[n] for n in ("ident", "max_rows", "region", "lane", "tokens"))
        padrow0 = view["padrow0"].rearrange("p (h e) -> p h e", h=2)
        identb = sb("identb", [P, P], BF16)
        trib = sb("trib", [P, P], BF16)
        onesb = sb("onesb", [P, P], BF16)
        gate_x = sb("gate_x", [P, 1])
        gate_f = sb("gate_f", [P, 1])
        consts = sb("consts", [P, 4])
        rw = sb("rw", [P, KD, E])
        rb = sb("rb", [P, E])
        counts = sb("counts", [P, E])
        tiles_i = sb("tiles_i", [1, 2 * E], I32)
        flag_i = sb("flag_i", [1, 2], I32)

        sbA = ExitStack()

        def sba(name, shape, dt=F32):
            return sbA.enter_context(nc.sbuf_tensor(name, shape, dt))

        raw = sba("raw", [P, 2048])
        xin = sba("xin", [P, QT, D])
        cin = sba("cin", [P, QT, D])
        xt = sba("xt_r", [P, 2, KD, S], F32R)
        ct = sba("ct_r", [P, 2, KD, S], F32R)
        qb = sba("qb_r", [P, 2, KD, S], F32R)
        kb = sba("kb_r", [P, 2, KD, S], F32R)
        Wr = {n: sba(f"{n}_r", [P, 2, KD, D], F32R) for n in ("wq", "wk", "wv", "wo")}
        selq = sba("selq_r", [P, 4, 2, P], F32R)
        selk = sba("selk_r", [P, 4, 2, P], F32R)
        bq = sba("bq_c", [P, 2])
        bk = sba("bk_c", [P, 2])
        bv = sba("bv_b", [P, D])
        gbo = sba("gbo_b", [P, D])
        mask_s = sba("mask_s", [P, QT, S], BF16)
        mask_t = sba("mask_t", [P, QT, S], BF16)
        mask_s1 = sba("mask_s1", [P, QT, P], BF16)
        mask_t1 = sba("mask_t1", [P, S], BF16)
        any_q = sba("any_q", [P, QT, QT])
        any_b = sba("any_b", [P, QT, QT], BF16)
        small = sba("small", [P, 32])
        xn = sba("xn", [P, QT, D])
        xres = sba("xres", [P, QT, D])
        shift_row = sba("shift_row_r", [P, 2, P], F32R)
        MS = sba("MS_r", [P, S], F32R)
        QS = sba("QS_r", [P, 8, S], F32R)
        KS = sba("KS_r", [P, 8, S], F32R)
        V = sba("V", [P, QT, H, 32])
        prob = sba("prob", [P, 2, 4, S])
        mx = sba("mx", [P, 16])
        MT = sba("MT", [P, QT, P])
        T1 = sba("T1", [P, S // 32, 32])
        T2 = sba("T2", [P, S // 32, 32])
        T3 = sba("T3", [P, S])
        den = sba("den", [P, S // 32])
        OT = sba("OT_r", [P, 2, 2, S], F32R)
        x2t = sba("x2t", [P, KD, S])
        st = sba("st", [P, 2, QT, 6])
        mv = sba("mv", [P, 2, QT, 2])
        nw = sba("nw", [P, 2, 5, QT])
        lg = sba("lg", [P, 8, QT, E])
        l1 = sba("l1", [P, 5, QT])
        Cb = sba("Cb", [P, QT, E], BF16)
        Rb = sba("Rb", [P, E], BF16)
        Sb = sba("Sb", [P, E])
        slot_i = sba("slot_i", [P, 2, QT], I32)
        x1 = sba("x1", [P, QT, D])
        pay = sba("pay", [P, QT, ROW])

        sbA.close()
        sbE = ExitStack()

        def sbe(name, shape, dt=F32):
            return sbE.enter_context(nc.sbuf_tensor(name, shape, dt))

        up_raw = sbe("up_raw", [P, KD, FF])
        dn_raw = sbe("dn_raw", [P, FF // P, D])
        up_r, dn_r = [], []
        for i in range(2):
            up_r.append(sbe(f"up_r{i}", [P, 2, KD, FF], F32R))
            dn_r.append(sbe(f"dn_r{i}", [P, 2, FF // P, D], F32R))
        xe = sbe("xe", [P, 2, ROW])
        meta = sbe("meta", [P, 2, 1 + E])
        xet = sbe("xet_r", [P, 2, KD, TILE], F32R)
        hf = sbe("hf", [P, 4, 2 * TILE])
        hr = sbe("hr_r", [P, 2, 4, 2 * TILE], F32R)
        ye = sbe("ye", [P, 2, D])
        pads = sbe("pads", [P, 2, ROW])
        pad_i = sbe("pad_i", [P, 2, E], I32)
        tf = sbe("tf", [1, 4 * E])
        ti = sbe("ti", [1, 2 * E], I32)
        sbE.close()

        ps = ctx.enter_context(nc.psum_tensor("ps", [P, 8, S], F32))
        UPB = [0, 1, 2, 6]
        WORK, SC, AV = 0, 3, 7

        names = """gates_in fixed_in mask_in mask_t_in sel_in weights_in const_in
            sel_ready weights_hi wo_scaled const_done any_ready seen_counted flag_done mask_ready gates
            x_in ctx_in xres_in guess1 guess2 step1 step2 scale1 scale2 xn_done xres_done hi_done 
            neg_done st_full exp_done av_done av_free ot_ready x1_done x1_stored xn2_done
            log_in log_exp comb_done slots_done scattered chain_v zeroed
            counted tiles_done pads_set pads_in w_dma w_hi w_lo pads0_in w_pool x_dma meta_dma
            xt_hi xt_lo up_full act_f h_lo down_done y_done added xt_full passed""".split()
        s = {n: sem(n) for n in names}
        full = [sem(f"work_full{i}") for i in range(3)]
        free = [sem(f"work_free{i}") for i in range(3)]

        block = ctx.enter_context(nc.Block())

        class Chain:

            def __init__(self, eng, sem_, base=0):
                self.eng, self.sem, self.n, self.base = eng, sem_, 0, base

            def __call__(self, ins):
                self.n += 1
                ins.then_inc(self.sem, 1)
                return ins

            def wait(self):
                self.eng.wait_ge(self.sem, self.base + self.n)

        def wait_reg(eng, sem_, value):
            eng.wait_ge(sem_, value)
            eng.sem_inc(s["passed"], 1)

        def both(eng, run):
            eng.wait_ge(s["flag_done"], 1)
            fast = eng.value_load(flag_i[0:1, 0:1], min_val=0, max_val=1)
            with eng.If(fast == 1):
                run(1)
            with eng.Else():
                run(QT)
            eng.end_ifs()

        def batches(eng, nt, prologue, body, tail):
            items = body_items(nt)
            start = Work(prologue_items(nt), [0, 0, 0])
            used = Work(items, None).used

            def work(b):
                base = [start.used[i] + b * used[i] for i in range(3)]
                back = [start.used[i] + (b - 1) * used[i] for i in range(3)]
                return Work(items, base, start if isinstance(b, int) and b == 0 else Work(items, back))

            prologue(nt, start)
            body(nt, 0, work(0), False, True)
            with eng.Fori(1, B - 1) as b:
                body(nt, b, work(b), True, True)
            body(nt, B - 1, work(B - 1), True, False)
            tail(nt, Work(TAIL_ITEMS, [start.used[i] + B * used[i] for i in range(3)]))

        def n_split(nt):
            return 4 + 2 * (1 if nt == 1 else 2)

        def split_no(nt, item):
            return (input_items(nt) + project_items(nt)).index(item)

        def w_raw(j):
            return up_raw[:, j, :] if j < 2 else dn_raw[:, 4 * j - 8:4 * j - 4, :].rearrange("p c d -> p (c d)")

        def w_part(par, low, j):
            return up_r[par][:, low, j, :] if j < 2 else dn_r[par][:, low, 4 * j - 8:4 * j - 4, :].rearrange("p c d -> p (c d)")

        WEIGHTS = ("wq", "wk", "wv", "wo")
        raw_mask = raw[:, :].bitcast(I32).rearrange("p (t k) -> p t k", t=QT)
        raw_mask_t = prob[:, 0, :, :].bitcast(I32)
        raw_sel = prob[:, 1, :, :].rearrange("p a n -> p (a n)")
        raw_w = {"wq": x2t[:, 0, :].rearrange("p (k n) -> p k n", k=KD), "wk": x2t[:, 1, :].rearrange("p (k n) -> p k n", k=KD),
                 "wv": pay[:, 0:2, 0:D], "wo": pay[:, 2:4, 0:D]}

        @block.sync
        def _(sp):
            sp.dma_start(xin[:, :, :], t["x"][0].rearrange("(q p) d -> p q d", p=P)).then_inc(s["x_in"], 16)
            sp.dma_start(gate_x[:, :], t["g_xattn"].unsqueeze(0).to_broadcast([P, 1])).then_inc(s["gates_in"], 16)
            sp.dma_start(gate_f[:, :], t["g_ffn"].unsqueeze(0).to_broadcast([P, 1])).then_inc(s["gates_in"], 16)
            sp.dma_start(raw_mask, t["mask"].rearrange("(t p) k -> p t k", p=P)).then_inc(s["mask_in"], 16)
            sp.dma_start(fixed[:, :], t["fixed"]).then_inc(s["fixed_in"], 16)
            for n in WEIGHTS:
                sp.dma_start(raw_w[n], t[n].rearrange("(k p) n -> p k n", p=P)).then_inc(s["weights_in"], 16)
            sp.dma_start(bq[:, :], t["bq"]).then_inc(s["const_in"], 16)
            sp.dma_start(bk[:, :], t["bk"]).then_inc(s["const_in"], 16)
            sp.dma_start(bv[:, :], t["bv"].unsqueeze(0).to_broadcast([P, D])).then_inc(s["const_in"], 16)
            sp.dma_start(gbo[:, :], t["bo"].unsqueeze(0).to_broadcast([P, D])).then_inc(s["const_in"], 16)
            sp.dma_start(rw[:, :, :], t["router_w"].rearrange("(k p) e -> p k e", p=P)).then_inc(s["const_in"], 16)
            sp.dma_start(rb[:, :], t["router_b"].unsqueeze(0).to_broadcast([P, E])).then_inc(s["const_in"], 16)
            sp.dma_start(raw_sel, t["sel"]).then_inc(s["sel_in"], 16)
            sp.dma_start(raw_mask_t, t["mask_t"].rearrange("(t p) k -> p t k", p=P)).then_inc(s["mask_t_in"], 16)

            def load_x(n, row):
                sp.wait_ge(s["xn_done"], n)
                sp.dma_start(xin[:, :, :], t["x"][bass.ds(row, 1)].rearrange("a (q p) d -> p (a q) d", p=P)).then_inc(s["x_in"], 16)

            def load_ctx(nt, b):
                if nt == 1:
                    src = t["ctx"][bass.ds(b, 1), bass.ds(tile_reg * P, P), :].rearrange("a p d -> p (a d)")
                    sp.dma_start(cin[:, 0, :], src).then_inc(s["ctx_in"], 16)
                else:
                    sp.dma_start(cin[:, :, :], t["ctx"][bass.ds(b, 1)].rearrange("a (q p) d -> p (a q) d", p=P)).then_inc(s["ctx_in"], 16)

            def load_xres(b):
                sp.dma_start(xres[:, :, :], t["x"][bass.ds(b, 1)].rearrange("a (q p) d -> p (a q) d", p=P)).then_inc(s["xres_in"], 16)

            def store_x1(b):
                sp.dma_start(out[bass.ds(b * S, S), :].rearrange("(q p) d -> p q d", p=P), x1[:, :, :]).then_inc(s["x1_stored"], 16)

            def prologue(nt, w):
                load_ctx(nt, 0)
                load_xres(0)
                load_x(1, 1)

            def body(nt, b, w, has_before, has_next):
                if has_next:
                    sp.wait_ge(s["hi_done"], n_split(nt) * b + len(input_items(nt)))
                    load_ctx(nt, b + 1)
                    load_x(b + 2, b + 2 if isinstance(b, int) else
                           nc.s_assert_within(sp.snap(((b + 2) < B) * (b + 2)), 0, B - 1, skip_runtime_bounds_check_because="it is 0 past the last batch"))
                else:
                    sp.wait_ge(s["guess1"], B + 1)
                    sp.wait_ge(s["hi_done"], n_split(nt) * B)
                    load_w(0)
                if has_before:
                    sp.wait_ge(s["x1_done"], 2 * b)
                    load_xres(b)
                    store_x1(b - 1)

            def tail(nt, w):
                sp.wait_ge(s["x1_done"], 2 * B)
                store_x1(B - 1)

            def load_w(e):
                sp.dma_start(up_raw[:, :, :], t["up"][bass.ds(e, 1)].rearrange("a (k p) f -> p (a k) f", p=P)).then_inc(s["w_dma"], 16)
                sp.dma_start(dn_raw[:, :, :], t["down"][bass.ds(e, 1)].rearrange("a (c p) d -> p (a c) d", p=P)).then_inc(s["w_dma"], 16)

            sp.wait_ge(s["flag_done"], 1)
            tile_reg = sp.value_load(flag_i[0:1, 1:2], min_val=0, max_val=QT - 1)
            both(sp, lambda nt: batches(sp, nt, prologue, body, tail))

            sp.wait_ge(s["tiles_done"], 1)
            sp.wait_ge(s["scattered"], 16 * 2 * TOK // P + 16)
            sp.wait_ge(s["pads0_in"], 16 * 2)
            sp.dma_start(xe[:, :, :], routed[0:TILE, :].rearrange("(h p) r -> p h r", p=P)).then_inc(s["x_dma"], 16)

            def expert(e, nxt):
                n = sp.value_load(tiles_i[0:1, bass.ds(e, 1)], min_val=1, max_val=TOK // TILE)
                base = sp.value_load(tiles_i[0:1, bass.ds(e + E, 1)], min_val=0, max_val=2 * TOK // TILE + E)
                if nxt:
                    sp.wait_ge(s["w_lo"], 4 * e + 4)
                    load_w(e + 1)
                sp.wait_ge(s["pads_in"], 16 * 2 * (E - 1))
                with sp.Fori(0, n) as i:
                    sp.wait_ge(s["xt_full"], base + i + 1)
                    sp.dma_start(xe[:, :, :], routed[bass.ds(next_row(e, i, n), TILE), :].rearrange("(h p) r -> p h r", p=P)).then_inc(s["x_dma"], 16)
                    sp.wait_ge(s["added"], 32 * (base + i) + 16)
                    sp.dma_start(meta[:, :, :], routed[bass.ds(within(e * CAP + i * TILE), TILE), D:ROW].rearrange("(h p) r -> p h r", p=P)).then_inc(s["meta_dma"], 16)

            def within(row):
                return nc.s_assert_within(row, 0, E * CAP - TILE, skip_runtime_bounds_check_because="an expert has at most TOK rows and the padding")

            def next_row(e, i, n):
                more = sp.snap((i + 1) < n)
                return within(more * (e * CAP + (i + 1) * TILE) + (1 - more) * nxt_row(e))

            def nxt_row(e):
                return ((e + 1) % E) * CAP

            with sp.Fori(0, E // 2 - 1) as k:
                expert(2 * k, True)
                expert(2 * k + 1, True)
            expert(E - 2, True)
            expert(E - 1, False)

        @block.scalar
        def _(act):
            def normalise(k, x_, dst):
                for q in range(QT):
                    ins = nc.scalar.activation(dst[:, q, 0:D], x_[:, q, :], ACT.Identity, scale=nw[:, k, 1, q:q + 1], bias=nw[:, k, 4, q:q + 1])
                return ins

            def normalise1(n):
                act.wait_ge(s["scale1"], n + 1)
                normalise(0, xin, xn).then_inc(s["xn_done"], 1)

            act.wait_ge(s["gates_in"], 32)
            nc.scalar.activation(gate_x[:, :], gate_x[:, :], ACT.Tanh).then_inc(s["gates"], 1)
            nc.scalar.activation(gate_f[:, :], gate_f[:, :], ACT.Tanh).then_inc(s["gates"], 1)
            normalise1(0)
            act.wait_ge(s["weights_in"], 64)
            for n in WEIGHTS:
                if n == "wo":
                    act.wait_ge(s["wo_scaled"], 1)
                nc.scalar.activation(Wr[n][:, 0, :, :], raw_w[n], ACT.Copy).then_inc(s["weights_hi"], 1)

            def hi(w, item, dst, src, bias=None):
                act.wait_ge(full[w.bank(item)], w.before(item) + 1)
                if bias is None:
                    ins = nc.scalar.activation(dst, src, ACT.Copy)
                else:
                    ins = nc.scalar.activation(dst, src, ACT.Identity, bias=bias)
                return ins

            def split(nt, w, items):
                for item in items:
                    kind, m = item
                    bank = ps[:, WORK + w.bank(item), :]
                    if kind == "xt":
                        ins = hi(w, item, xt[:, 0, m, :], bank)
                    elif kind == "ct" and nt == 1:
                        ins = hi(w, item, ct[:, 0, :, 0:P], bank[:, 0:2 * P].rearrange("p (k n) -> p k n", k=2))
                    elif kind == "ct":
                        ins = hi(w, item, ct[:, 0, m, :], bank)
                    elif kind == "q":
                        ins = hi(w, item, qb[:, 0, m, :], bank, bq[:, m:m + 1])
                    elif nt == 1:
                        hi(w, item, kb[:, 0, 0, 0:P], bank[:, 0:P], bk[:, 0:1])
                        ins = nc.scalar.activation(kb[:, 0, 1, 0:P], bank[:, P:2 * P], ACT.Identity, bias=bk[:, 1:2])
                    else:
                        ins = hi(w, item, kb[:, 0, m, :], bank, bk[:, m:m + 1])
                    ins.then_inc(s["hi_done"], 1)

            def stacks(nt, w, g):
                for item in stack_items(nt, g):
                    kind, _, j = item
                    act.wait_ge(full[w.bank(item)], w.before(item) + 1)
                    bank = ps[:, WORK + w.bank(item), :]
                    if kind == "qs":
                        ins = nc.scalar.activation(QS[:, 2 * g + j, :], bank, ACT.Copy)
                    elif nt == 1:
                        for x_ in range(2):
                            r = slice(64 * x_, 64 * x_ + 64)
                            ins = nc.scalar.activation(KS[r, 2 * g:2 * g + 2, x_ * P:(x_ + 1) * P], bank[r, 0:2 * P].rearrange("p (j n) -> p j n", j=2), ACT.Copy)
                    else:
                        ins = nc.scalar.activation(KS[:, 2 * g + j, :], bank, ACT.Copy)
                    ins.then_inc(free[w.bank(item)], 1)

            def copy_maxima(w, ahead, g):
                item = ("shift", ahead, g)
                act.wait_ge(full[w.bank(item)], w.before(item) + 1)
                nc.scalar.activation(MS[:, :], ps[:, WORK + w.bank(item), :], ACT.Copy).then_inc(free[w.bank(item)], 1)

            def exps(nt, b, g):
                for kt in range(nt):
                    u = (b * HG + g) * nt + kt
                    slot = (g * nt + kt) % 2
                    for j in range(2):
                        act.wait_ge(s["st_full"], 2 * u + j + 1)
                        if j == 0:
                            act.wait_ge(s["av_done"], u + 1)
                        nc.scalar.activation(prob[:, slot, 2 * j:2 * j + 2, :], ps[:, SC + 2 * j:SC + 2 * j + 2, :],
                                             ACT.Exp, scale=SCALE).then_inc(s["exp_done"], 1)

            def copy_x2t(w):
                for k in range(2):
                    item = ("x2t", k)
                    act.wait_ge(full[w.bank(item)], w.before(item) + 1)
                    nc.scalar.activation(x2t[:, k, :], ps[:, WORK + w.bank(item), :], ACT.Copy).then_inc(free[w.bank(item)], 1)

            def exp_logits(n):
                act.wait_ge(s["log_in"], n + 1)
                nc.scalar.activation(lg[:, 1, :, :], lg[:, 0, :, :], ACT.Exp).then_inc(s["log_exp"], 1)

            def normalise2(n):
                act.wait_ge(s["scattered"], 16 * 8 * n + 16)
                act.wait_ge(s["scale2"], n + 1)
                normalise(1, x1, pay).then_inc(s["xn2_done"], 1)

            def prologue(nt, w):
                split(nt, w, input_items(nt) + project_items(nt))
                stacks(nt, w, 0)
                stacks(nt, w, 1)
                copy_maxima(w, 1, 0)
                stacks(nt, w, 2)
                stacks(nt, w, 3)

            def body(nt, b, w, has_before, has_next):
                exps(nt, b, 0)
                copy_maxima(w, 0, 1)
                if has_next:
                    normalise1(b + 1)
                exps(nt, b, 1)
                copy_maxima(w, 0, 2)
                if has_next:
                    split(nt, w, input_items(nt))
                if has_before:
                    normalise2(b - 1)
                exps(nt, b, 2)
                copy_maxima(w, 0, 3)
                if has_before:
                    copy_x2t(w)
                if has_next:
                    split(nt, w, project_items(nt))
                if has_before:
                    exp_logits(b - 1)
                if has_next:
                    stacks(nt, w, 0)
                exps(nt, b, 3)
                if has_next:
                    stacks(nt, w, 1)
                    stacks(nt, w, 2)
                    copy_maxima(w, 1, 0)
                    stacks(nt, w, 3)

            def tail(nt, w):
                normalise2(B - 1)
                copy_x2t(w)
                exp_logits(B - 1)

            both(act, lambda nt: batches(act, nt, prologue, body, tail))

            act.wait_ge(s["tiles_done"], 1)

            def high_x(n):
                act.wait_ge(s["xt_full"], n + 1)
                nc.scalar.activation(xet[:, 0, :, :], ps[:, 5, :].rearrange("p (k n) -> p k n", k=2), ACT.Copy).then_inc(s["xt_hi"], 1)

            high_x(0)

            def expert(e, par, nxt):
                n = act.value_load(tiles_i[0:1, bass.ds(e, 1)], min_val=1, max_val=TOK // TILE)
                base_ = act.value_load(tiles_i[0:1, bass.ds(e + E, 1)], min_val=0, max_val=2 * TOK // TILE + E)

                def tile(T, split):
                    for p in range(4):
                        act.wait_ge(s["up_full"], 4 * T + p + 1)
                        act.wait_ge(s["down_done"], 4 * T + p + 1)
                        bank = ps[:, UPB[p], :]
                        nc.scalar.activation(hr[:, 0, p, :], bank, ACT.Gelu)
                        nc.scalar.activation(hf[:, p, :], bank, ACT.Gelu).then_inc(s["act_f"], 1)
                        if split:
                            if p == 0:
                                act.wait_ge(s["w_dma"], 32 * e + 64)
                                act.wait_ge(s["down_done"], 4 * T + 4)
                            nc.scalar.activation(w_part(1 - par, 0, p), w_raw(p), ACT.Copy).then_inc(s["w_hi"], 1)
                    high_x(T + 1)

                tile(base_, nxt)
                with act.If(n > 1):
                    with act.Fori(1, n) as i:
                        tile(act.snap(base_ + i), False)
                act.end_ifs()

            with act.Fori(0, E // 2 - 1) as k:
                expert(2 * k, 0, True)
                expert(2 * k + 1, 1, True)
            expert(E - 2, 0, True)
            expert(E - 1, 1, False)

        @block.tensor
        def _(pe):
            def mm(o, a, b_, start, stop):
                return pe.matmul(o, a, b_, start=start, stop=stop, skip_group_check=True)

            def three(o, a_h, a_l, b_h, b_l, parts):
                n = 0
                for k in parts:
                    for x_, y_ in ((a_h, b_h), (a_l, b_h), (a_h, b_l)):
                        ins = mm(o, x_(k), y_(k), n == 0, n == 3 * len(parts) - 1)
                        n += 1
                return ins

            pe.wait_ge(s["any_ready"], 1)
            for qt in range(QT):
                ins = mm(ps[:, 0, 0:QT], onesb[:, :], any_b[:, qt, :], qt == 0, qt == QT - 1)
            ins.then_inc(s["seen_counted"], 1)
            pe.wait_ge(s["fixed_in"], 16)

            def take(w, item, made=(), made_by=None):
                latest = {}
                for other in made:
                    latest[(made_by or w).bank(other)] = other
                for bank, other in latest.items():
                    if bank != w.bank(item):
                        pe.wait_ge(free[bank], (made_by or w).before(other) + 1)
                n = w.before(item)
                if not (isinstance(n, int) and n <= 0):
                    pe.wait_ge(free[w.bank(item)], n)
                return ps[:, WORK + w.bank(item), :]

            def give(w, item, ins):
                ins.then_inc(full[w.bank(item)], 1)

            def skip(w, items):
                for item in items:
                    take(w, item)
                    pe.sem_inc(full[w.bank(item)], 1)
                    pe.sem_inc(free[w.bank(item)], 1)

            def is_read(w, item):
                pe.wait_ge(free[w.bank(item)], w.before(item) + 1)

            def inputs(nt, w, n):
                for item in input_items(nt):
                    kind, m = item
                    if kind == "xt":
                        pe.wait_ge(s["xn_done"], n + 1)
                        o = take(w, item)
                        for q in range(QT):
                            ins = pe.transpose(o[:, q * P:(q + 1) * P], xn[:, q, m * P:(m + 1) * P], ident[:, :])
                    else:
                        pe.wait_ge(s["ctx_in"], 16 * n + 16)
                        o = take(w, item)
                        for j in range(2 if nt == 1 else QT):
                            src = cin[:, 0, j * P:(j + 1) * P] if nt == 1 else cin[:, j, m * P:(m + 1) * P]
                            ins = pe.transpose(o[:, j * P:(j + 1) * P], src, ident[:, :])
                    give(w, item, ins)

            def project(nt, w):
                for item in project_items(nt):
                    kind, m = item
                    if kind == "q":
                        o = take(w, item, [("xt", 0), ("xt", 1)])
                        ins = three(o, lambda k: Wr["wq"][:, 0, k, m * P:(m + 1) * P], lambda k: Wr["wq"][:, 1, k, m * P:(m + 1) * P],
                                    lambda k: xt[:, 0, k, :], lambda k: xt[:, 1, k, :], range(KD))
                    else:
                        o = take(w, item, input_items(nt)[2:])
                        for mk in (range(2) if nt == 1 else [m]):
                            dst = o[:, mk * P:(mk + 1) * P] if nt == 1 else o
                            ins = three(dst, lambda k: Wr["wk"][:, 0, k, mk * P:(mk + 1) * P], lambda k: Wr["wk"][:, 1, k, mk * P:(mk + 1) * P],
                                        lambda k: ct[:, 0, k, 0:nt * P], lambda k: ct[:, 1, k, 0:nt * P], range(KD))
                    give(w, item, ins)

            def values(nt, w):
                for item in v_items(nt):
                    o = take(w, item)
                    for j in range(1 if nt == 1 else 2):
                        kt = 2 * item[1] + j
                        ins = three(o[:, j * D:(j + 1) * D], lambda k: ct[:, 0, k, kt * P:(kt + 1) * P], lambda k: ct[:, 1, k, kt * P:(kt + 1) * P],
                                    lambda k: Wr["wv"][:, 0, k, :], lambda k: Wr["wv"][:, 1, k, :], range(KD))
                    give(w, item, ins)

            def stacks(nt, w, g):
                for item in stack_items(nt, g):
                    kind, _, j = item
                    if kind == "qs":
                        o = take(w, item, [("q", (2 * g + j) // 4)])
                        pair = 2 * g + j
                        mm(o, selq[:, pair % 4, 0, :], qb[:, 0, pair // 4, :], True, False)
                        ins = mm(o, selq[:, pair % 4, 1, :], qb[:, 1, pair // 4, :], False, True)
                    else:
                        o = take(w, item, [project_items(nt)[2 if nt == 1 else 2 + (2 * g + j) // 4]])
                        for jj in (range(2) if nt == 1 else [j]):
                            pair = 2 * g + jj
                            dst = o[:, jj * P:(jj + 1) * P] if nt == 1 else o
                            mm(dst, selk[:, pair % 4, 0, :], kb[:, 0, pair // 4, 0:nt * P], True, False)
                            ins = mm(dst, selk[:, pair % 4, 1, :], kb[:, 1, pair // 4, 0:nt * P], False, True)
                    give(w, item, ins)

            def scores(nt, w, ahead, g):
                made_by = w if ahead else w.prev
                for item in score_items(nt, ahead, g):
                    i = item[3]
                    o = take(w, item, stack_items(nt, g) if i == 0 else (), made_by)
                    if nt == 1:
                        mm(o.rearrange("p (h n) -> p h n", h=4), identb[:, :], mask_s1[:, i, :].unsqueeze(1).to_broadcast([P, 4, P]), True, False)
                        for j in range(2):
                            ins = mm(o[:, j * 2 * P:(j + 1) * 2 * P], QS[:, 2 * g + j, i * P:(i + 1) * P], KS[:, 2 * g + j, 0:2 * P], False, j == 1)
                    else:
                        q, h = i // 4, i % 4
                        pair, r = 2 * g + h // 2, 64 * (h % 2)
                        mm(o, identb[:, :], mask_s[:, q, :], True, False)
                        ins = mm(o, QS[r:r + 64, pair, q * P:(q + 1) * P], KS[r:r + 64, pair, :], False, True)
                    give(w, item, ins)

            def shift(w, b, ahead, g):
                pe.wait_ge(s["neg_done"], b * HG + g + 1)
                item = ("shift", ahead, g)
                o = take(w, item)
                for q in range(QT):
                    ins = pe.transpose(o[:, q * P:(q + 1) * P], MT[:, q, :], ident[:, :])
                give(w, item, ins)

            def av(nt, w, b, g, kt):
                u = (b * HG + g) * nt + kt
                pe.wait_ge(s["exp_done"], 2 * u + 2 + 2)
                if g == 0 and kt == 0:
                    for item in v_items(nt):
                        is_read(w.prev, item)
                if kt == 0:
                    pe.wait_ge(s["av_free"], b * HG + g + 1)
                slot = (g * nt + kt) % 2
                for h in range(4):
                    ins = mm(ps[32 * h:32 * h + 32, AV, :], V[:, kt, 4 * g + h, :], prob[:, slot, h, :], kt == 0, kt == nt - 1)
                ins.then_inc(s["av_done"], 1)

            def shifted(nt, w, b, g):
                if g:
                    is_read(w, ("shift", 0, g))
                else:
                    is_read(w.prev, ("shift", 1, 0))
                for kt in range(nt):
                    u = (b * HG + g) * nt + kt
                    for j in range(2):
                        pe.wait_ge(s["exp_done"], 2 * u + j + 1)
                        for x_ in range(2):
                            pair, r = 2 * g + j, 64 * x_
                            o = ps[:, SC + 2 * j + x_, :]
                            mm(o, identb[:, :], mask_t1[:, :] if nt == 1 else mask_t[:, kt, :], True, False)
                            keys = x_ if nt == 1 else kt
                            mm(o, KS[r:r + 64, pair, keys * P:(keys + 1) * P], QS[r:r + 64, pair, :], False, False)
                            ins = mm(o, shift_row[r:r + 64, j, :], MS[r:r + 64, :], False, True)
                        ins.then_inc(s["st_full"], 1)
                    if kt:
                        av(nt, w, b, g, kt - 1)

            def proj(w, n):
                pe.wait_ge(s["ot_ready"], 2 * n + 2)
                for i in range(2):
                    item = ("proj", i)
                    o = take(w, item)
                    for j in range(2):
                        q = 2 * i + j
                        ins = three(o[:, j * D:(j + 1) * D], lambda k: OT[:, 0, k, q * P:(q + 1) * P], lambda k: OT[:, 1, k, q * P:(q + 1) * P],
                                    lambda k: Wr["wo"][:, 0, k, :], lambda k: Wr["wo"][:, 1, k, :], range(KD))
                    give(w, item, ins)

            def turn_x2(w, n):
                pe.wait_ge(s["xn2_done"], n + 1)
                for k in range(2):
                    item = ("x2t", k)
                    o = take(w, item)
                    for q in range(QT):
                        ins = pe.transpose(o[:, q * P:(q + 1) * P], pay[:, q, k * P:(k + 1) * P], ident[:, :])
                    give(w, item, ins)

            def logits(w):
                item = ("logits",)
                o = take(w, item, [("x2t", 0), ("x2t", 1)])
                for q in range(QT):
                    for k in range(KD):
                        ins = mm(o[:, q * E:(q + 1) * E], x2t[:, k, q * P:(q + 1) * P], rw[:, k, :], k == 0, k == KD - 1)
                give(w, item, ins)

            def rank(w, n):
                pe.wait_ge(s["comb_done"], n + 1)
                item = ("rank",)
                o = take(w, item)
                mm(o[:, 0:QT * E], trib[:, :], Cb[:, :, :].rearrange("p t e -> p (t e)"), True, False)
                for q in range(1, QT):
                    mm(o[:, q * E:QT * E], onesb[:, :], Cb[:, 0:QT - q, :].rearrange("p t e -> p (t e)"), False, False)
                ins = mm(o[:, 0:QT * E].rearrange("p (t e) -> p t e", e=E), onesb[:, :], Rb[:, :].unsqueeze(1).to_broadcast([P, QT, E]), False, True)
                give(w, item, ins)

            def prologue(nt, w):
                inputs(nt, w, 0)
                pe.wait_ge(s["const_done"], 1)
                project(nt, w)
                pe.wait_ge(s["sel_ready"], 2)
                stacks(nt, w, 0)
                pe.wait_ge(s["mask_ready"], 4)
                scores(nt, w, 1, 0)
                stacks(nt, w, 1)
                shift(w, 0, 1, 0)
                stacks(nt, w, 2)
                scores(nt, w, 1, 1)
                stacks(nt, w, 3)
                values(nt, w)

            def body(nt, b, w, has_before, has_next):
                def before(run, items, *args):
                    run(w, *args) if has_before else skip(w, items)

                def ahead(run, items, *args):
                    run(*args) if has_next else skip(w, items)

                shifted(nt, w, b, 0)
                shift(w, b, 0, 1)
                scores(nt, w, 0, 2)
                before(proj, [("proj", 0), ("proj", 1)], b - 1)
                av(nt, w, b, 0, nt - 1)
                shifted(nt, w, b, 1)
                shift(w, b, 0, 2)
                ahead(inputs, input_items(nt), nt, w, b + 1)
                scores(nt, w, 0, 3)
                av(nt, w, b, 1, nt - 1)
                shifted(nt, w, b, 2)
                shift(w, b, 0, 3)
                before(turn_x2, [("x2t", 0), ("x2t", 1)], b - 1)
                ahead(project, project_items(nt), nt, w)
                before(logits, [("logits",)])
                av(nt, w, b, 2, nt - 1)
                ahead(stacks, stack_items(nt, 0), nt, w, 0)
                shifted(nt, w, b, 3)
                ahead(stacks, stack_items(nt, 1), nt, w, 1)
                ahead(scores, score_items(nt, 1, 0), nt, w, 1, 0)
                before(rank, [("rank",)], b - 1)
                ahead(stacks, stack_items(nt, 2), nt, w, 2)
                ahead(shift, [("shift", 1, 0)], w, b + 1, 1, 0)
                av(nt, w, b, 3, nt - 1)
                ahead(stacks, stack_items(nt, 3), nt, w, 3)
                ahead(scores, score_items(nt, 1, 1), nt, w, 1, 1)
                ahead(values, v_items(nt), nt, w)

            def tail(nt, w):
                proj(w, B - 1)
                turn_x2(w, B - 1)
                logits(w)
                rank(w, B - 1)

            both(pe, lambda nt: batches(pe, nt, prologue, body, tail))

            pe.wait_ge(s["slots_done"], B)
            mm(ps[:, 6, 0:E], onesb[:, :], Rb[:, :], True, True).then_inc(s["counted"], 1)

            def transpose_x(n):
                pe.wait_ge(s["x_dma"], 16 * n + 16)
                pe.wait_ge(s["xt_lo"], n + 1)
                for k in range(KD):
                    for h in range(2):
                        ins = pe.transpose(ps[:, 5, k * TILE + h * P:k * TILE + (h + 1) * P], xe[:, h, k * P:(k + 1) * P], ident[:, :])
                ins.then_inc(s["xt_full"], 1)

            pe.wait_ge(s["tiles_done"], 1)
            transpose_x(0)

            def expert(e, par):
                n = pe.value_load(tiles_i[0:1, bass.ds(e, 1)], min_val=1, max_val=TOK // TILE)
                base_ = pe.value_load(tiles_i[0:1, bass.ds(e + E, 1)], min_val=0, max_val=2 * TOK // TILE + E)
                wait_reg(pe, s["w_lo"], 4 * e + 4)
                with pe.Fori(0, n) as i:
                    T = pe.snap(base_ + i)

                    def up(p):
                        pe.wait_ge(s["act_f"], 4 * T + p + 1)
                        for c in range(2 * p, 2 * p + 2):
                            ins = three(ps[:, UPB[p], (c % 2) * TILE:(c % 2 + 1) * TILE],
                                        lambda k: up_r[par][:, 0, k, c * P:(c + 1) * P], lambda k: up_r[par][:, 1, k, c * P:(c + 1) * P],
                                        lambda k: xet[:, 0, k, :], lambda k: xet[:, 1, k, :], range(KD))
                        ins.then_inc(s["up_full"], 1)

                    def down(p):
                        pe.wait_ge(s["h_lo"], 4 * T + p + 1)
                        if p == 0:
                            pe.wait_ge(s["y_done"], T + 1)
                        for half in range(2):
                            n_ = 0
                            for c in range(2):
                                hs = slice(c * TILE + half * P, c * TILE + (half + 1) * P)
                                for a, b_ in ((0, 0), (1, 0), (0, 1)):
                                    ins = mm(ps[:, 3 + half, 0:D], hr[:, a, p, hs], dn_r[par][:, b_, 2 * p + c, :],
                                             p == 0 and n_ == 0, p == 3 and n_ == 5)
                                    n_ += 1
                        ins.then_inc(s["down_done"], 1)

                    pe.wait_ge(s["xt_lo"], T + 2)
                    up(0)
                    up(1)
                    up(2)
                    down(0)
                    up(3)
                    down(1)
                    pe.wait_ge(s["x_dma"], 16 * T + 32)
                    for k in range(KD):
                        for h in range(2):
                            ins = pe.transpose(ps[:, 5, k * TILE + h * P:k * TILE + (h + 1) * P], xe[:, h, k * P:(k + 1) * P], ident[:, :])
                    ins.then_inc(s["xt_full"], 1)
                    down(2)
                    down(3)

            with pe.Fori(0, E // 2) as k:
                expert(2 * k, 0)
                expert(2 * k + 1, 1)

        @block.vector
        def _(dve):
            v = nc.vector
            ch = Chain(dve, s["chain_v"])

            ch(v.memset(onesb[:, :], 1.0))
            ch(v.memset(MT[:, :, :], 0.0))
            ch(v.memset(V[:, :, :, :], 1.0))
            ch(v.memset(Rb[:, :], 0.0))
            for n, value in enumerate((-0.5, 1.5, -1.0, 0.0)):
                ch(v.memset(consts[:, n:n + 1], value))
            dve.sem_inc(s["av_free"], 1)
            dve.sem_inc(s["exp_done"], 2)
            dve.sem_inc(s["av_done"], 2)
            dve.sem_inc(s["act_f"], 4)
            dve.sem_inc(s["down_done"], 4)
            dve.sem_inc(s["xt_lo"], 1)
            dve.sem_inc(s["y_done"], 1)

            def norm(c, k, x_no=None):
                if k == 0:
                    dve.wait_ge(s["x_in"], 16 * x_no + 16)
                for q in range(QT):
                    c(v.bn_stats(st[:, k, q, :], (xin, x1)[k][:, q, :]))
                wait_reg(dve, c.sem, c.base + c.n)
                for q in range(QT):
                    c(v.bn_aggr(mv[:, k, q, :], st[:, k, q, :]))
                c.wait()
                a, y, u = (nw[:, k, i, :] for i in range(3))
                c(v.tensor_scalar(a, mv[:, k, :, 1], EPS, None, ALU.add))
                c.wait()
                c(v.tensor_scalar(u.bitcast(I32), a.bitcast(I32), 1, None, ALU.logical_shift_right))
                c.wait()
                v.tensor_scalar(y.bitcast(I32), u.bitcast(I32), -1.0, float(0x5F3759DF), ALU.mult, ALU.add).then_inc(s[("guess1", "guess2")[k]], 1)

            norm(ch, 0, 0)
            dve.wait_ge(s["mask_in"], 16)
            ch(v.tensor_scalar(mask_s[:, :, :], raw_mask, 0.0, MASKED, ALU.is_equal, ALU.mult))
            ch.wait()
            for q in range(QT):
                ch(v.tensor_reduce(any_q[:, q, :], mask_s[:, q, :].rearrange("p (a n) -> p a n", a=QT), AX.X, ALU.max))
            ch.wait()
            ch(v.tensor_scalar(any_b[:, :, :], any_q[:, :, :], 0.0, None, ALU.is_equal))
            ch.wait()
            dve.sem_inc(s["any_ready"], 1)
            dve.wait_ge(s["seen_counted"], 1)
            all_see, is_full, number = small[:, 0:4], small[:, 4:5], small[:, 8:12]
            total, only_one, fast_tile = small[:, 12:13], small[:, 13:14], small[:, 14:16]
            ch(v.tensor_scalar(all_see, ps[:, 0, 0:QT], float(S), None, ALU.is_equal))
            ch(v.tensor_reduce(total, ps[:, 0, 0:QT], AX.X, ALU.add))
            ch.wait()
            dve.wait_ge(s["fixed_in"], 16)
            ch(v.tensor_tensor(number, all_see, lane[:, 0:QT], ALU.mult))
            ch(v.tensor_reduce(is_full, all_see, AX.X, ALU.max))
            ch(v.tensor_scalar(only_one, total, float(S), None, ALU.is_equal))
            ch.wait()
            ch(v.tensor_reduce(fast_tile[:, 1:2], number, AX.X, ALU.max))
            ch(v.tensor_tensor(fast_tile[:, 0:1], only_one, is_full, ALU.mult))
            ch.wait()
            ch(v.tensor_copy(flag_i[0:1, :], fast_tile[0:1, :]))
            ch.wait()
            dve.sem_inc(s["flag_done"], 1)
            ch(v.tensor_copy(trib[:, :], view["trimat"]))
            ch(v.tensor_copy(identb[:, :], ident[:, :]))
            ch(v.tensor_copy(shift_row[:, :, :], max_rows.unsqueeze(2).to_broadcast([P, 2, P])))
            dve.wait_ge(s["gates"], 2)
            dve.wait_ge(s["weights_in"], 64)
            v.tensor_scalar(raw_w["wo"], raw_w["wo"], gate_x[:, 0:1], None, ALU.mult).then_inc(s["wo_scaled"], 1)
            dve.wait_ge(s["const_in"], 16 * 6)
            ch(v.tensor_scalar(gbo[:, :], gbo[:, :], gate_x[:, 0:1], None, ALU.mult))
            for n, name in enumerate(WEIGHTS):
                dve.wait_ge(s["weights_hi"], n + 1)
                ch(v.tensor_tensor(Wr[name][:, 1, :, :], raw_w[name], Wr[name][:, 0, :, :].bitcast(F32), ALU.subtract))
            ch.wait()
            dve.sem_inc(s["const_done"], 1)

            def wait_full(w, item):
                dve.wait_ge(full[w.bank(item)], w.before(item) + 1)
                return ps[:, WORK + w.bank(item), :]

            def split(nt, w, b, items):
                for item in items:
                    kind, m = item
                    dve.wait_ge(s["hi_done"], n_split(nt) * b + split_no(nt, item) + 1)
                    bank = ps[:, WORK + w.bank(item), :]
                    if kind == "xt":
                        ins = v.tensor_tensor(xt[:, 1, m, :], bank, xt[:, 0, m, :].bitcast(F32), ALU.subtract)
                    elif kind == "ct" and nt == 1:
                        ins = v.tensor_tensor(ct[:, 1, :, 0:P], bank[:, 0:2 * P].rearrange("p (k n) -> p k n", k=2), ct[:, 0, :, 0:P].bitcast(F32), ALU.subtract)
                    elif kind == "ct":
                        ins = v.tensor_tensor(ct[:, 1, m, :], bank, ct[:, 0, m, :].bitcast(F32), ALU.subtract)
                    elif kind == "q":
                        ins = v.scalar_tensor_tensor(out=qb[:, 1, m, :], in0=bank, scalar=bq[:, m:m + 1], in1=qb[:, 0, m, :].bitcast(F32),
                                                     op0=ALU.add, op1=ALU.subtract)
                    elif nt == 1:
                        v.scalar_tensor_tensor(out=kb[:, 1, 0, 0:P], in0=bank[:, 0:P], scalar=bk[:, 0:1], in1=kb[:, 0, 0, 0:P].bitcast(F32),
                                               op0=ALU.add, op1=ALU.subtract)
                        ins = v.scalar_tensor_tensor(out=kb[:, 1, 1, 0:P], in0=bank[:, P:2 * P], scalar=bk[:, 1:2], in1=kb[:, 0, 1, 0:P].bitcast(F32),
                                                     op0=ALU.add, op1=ALU.subtract)
                    else:
                        ins = v.scalar_tensor_tensor(out=kb[:, 1, m, :], in0=bank, scalar=bk[:, m:m + 1], in1=kb[:, 0, m, :].bitcast(F32),
                                                     op0=ALU.add, op1=ALU.subtract)
                    ins.then_inc(free[w.bank(item)], 1)

            def maxima(nt, w, ahead, g):
                items = score_items(nt, ahead, g)
                for i, item in enumerate(items):
                    bank = wait_full(w, item)
                    if nt == 1:
                        ins = v.tensor_reduce(mx[:, 4 * i:4 * i + 4], bank.rearrange("p (h n) -> p h n", h=4), AX.X, ALU.max)
                    else:
                        ins = v.tensor_reduce(mx[:, i:i + 1], bank, AX.X, ALU.max)
                    ins.then_inc(free[w.bank(item)], 1)
                for item in items[-3:]:
                    dve.wait_ge(free[w.bank(item)], w.before(item) + 1)
                src = mx[:, :].rearrange("p (q j x) -> p q j x", q=QT, j=2)
                for x_ in range(2):
                    ins = v.tensor_scalar(MT[:, :, 48 + 64 * x_:50 + 64 * x_], src[:, :, :, x_], -1.0, None, ALU.mult)
                ins.then_inc(s["neg_done"], 1)

            def values(nt, w):
                for item in v_items(nt):
                    bank = wait_full(w, item)
                    for j in range(1 if nt == 1 else 2):
                        kt = 2 * item[1] + j
                        ins = v.tensor_tensor(V[:, kt, :, 0:DH], bank[:, j * D:(j + 1) * D].rearrange("p (h d) -> p h d", h=H),
                                              bv[:, :].rearrange("p (h d) -> p h d", h=H), ALU.add)
                    ins.then_inc(free[w.bank(item)], 1)

            def heads_out(nt, c, b, g):
                dve.wait_ge(s["av_done"], (b * HG + g + 1) * nt + 2)
                c(v.transpose(T1[:, :, :].rearrange("p a n -> p (a n)"), ps[:, AV, :]))
                c.wait()
                dve.sem_inc(s["av_free"], 1)
                c(v.reciprocal(den[:, :], T1[:, :, DH]))
                c.wait()
                half = g % 2
                c(v.tensor_tensor(T2[:, :, half * DH:(half + 1) * DH], T1[:, :, 0:DH], den[:, :].unsqueeze(2).to_broadcast([P, S // 32, DH]), ALU.mult))
                c.wait()
                if half:
                    c(v.transpose(T3[:, :], T2[:, :, :].rearrange("p a n -> p (a n)")))
                    c.wait()
                    c(v.tensor_copy(OT[:, 0, g // 2, :], T3[:, :]))
                    c.wait()
                    v.tensor_tensor(OT[:, 1, g // 2, :], T3[:, :], OT[:, 0, g // 2, :].bitcast(F32), ALU.subtract).then_inc(s["ot_ready"], 1)

            def residual(c, w, n):
                dve.wait_ge(s["xres_done"], n + 1)
                dve.wait_ge(s["x1_stored"], 16 * n + 16)
                for i in range(2):
                    item = ("proj", i)
                    bank = wait_full(w, item)
                    v.tensor_tensor(x1[:, 2 * i:2 * i + 2, :], bank.rearrange("p (q d) -> p q d", q=2),
                                    xres[:, 2 * i:2 * i + 2, :], ALU.add).then_inc(s["x1_done"], 1)
                    dve.wait_ge(s["x1_done"], 2 * n + i + 1)
                    dve.sem_inc(free[w.bank(item)], 1)

            L, X, Pr, EQ, PEN, O1, O2, TM = (lg[:, i, :, :] for i in range(8))
            m1, r1, i1, m2, i2 = (l1[:, i, :] for i in range(5))

            def bc(a):
                return a.unsqueeze(2).to_broadcast([P, QT, E])

            def bce(a):
                return a.unsqueeze(1).to_broadcast([P, QT, E])

            def choose(c, w, n):
                item = ("logits",)
                bank = wait_full(w, item)
                c(v.tensor_tensor(TM, bank[:, 0:QT * E].rearrange("p (q e) -> p q e", q=QT), bce(rb[:, :]), ALU.add))
                c.wait()
                dve.sem_inc(free[w.bank(item)], 1)
                c(v.tensor_reduce(m1, TM, AX.X, ALU.max))
                c.wait()
                v.tensor_tensor(L, TM, bc(m1), ALU.subtract).then_inc(s["log_in"], 1)
                dve.wait_ge(s["log_exp"], n + 1)
                c(v.tensor_reduce(r1, X, AX.X, ALU.add))
                c.wait()
                c(v.reciprocal(i1, r1))
                c.wait()
                c(v.tensor_tensor(Pr, X, bc(i1), ALU.mult))
                c.wait()

                def pick(src, m, idx, o):
                    c(v.tensor_reduce(m, src, AX.X, ALU.max))
                    c.wait()
                    c(v.tensor_tensor(EQ, src, bc(m), ALU.is_equal))
                    c.wait()
                    c(v.scalar_tensor_tensor(out=PEN, in0=EQ, scalar=-100.0, in1=bce(lane[:, :]), op0=ALU.mult, op1=ALU.add))
                    c.wait()
                    c(v.tensor_reduce(idx, PEN, AX.X, ALU.min))
                    c.wait()
                    c(v.tensor_tensor(o, PEN, bc(idx), ALU.is_equal))
                    c.wait()

                pick(Pr, m1, i1, O1)
                c(v.scalar_tensor_tensor(out=TM, in0=O1, scalar=-2.0, in1=Pr, op0=ALU.mult, op1=ALU.add))
                c.wait()
                pick(TM, m2, i2, O2)
                c(v.tensor_tensor(Cb[:, :, :], O1, O2, ALU.add))
                c.wait()
                dve.sem_inc(s["comb_done"], 1)
                c(v.scalar_tensor_tensor(out=pay[:, :, D + 1:ROW], in0=Pr, scalar=gate_f[:, 0:1], in1=Cb[:, :, :], op0=ALU.mult, op1=ALU.mult))
                c(v.tensor_copy(pay[:, :, D].bitcast(I32), tokf[:, :]))
                c.wait()
                c(v.tensor_scalar(tokf[:, :], tokf[:, :], float(S), None, ALU.add))

            def place(c, w):
                item = ("rank",)
                bank = wait_full(w, item)
                c(v.tensor_tensor(PEN, bank[:, 0:QT * E].rearrange("p (q e) -> p q e", q=QT), bce(region[:, :]), ALU.add))
                c.wait()
                dve.sem_inc(free[w.bank(item)], 1)
                c(v.tensor_tensor(lg[:, 0:2, :, :], lg[:, 5:7, :, :], PEN.unsqueeze(1).to_broadcast([P, 2, QT, E]), ALU.mult))
                c(v.tensor_reduce(Sb[:, :], Cb[:, :, :].rearrange("p q e -> p e q"), AX.X, ALU.add))
                c.wait()
                c(v.tensor_reduce(l1[:, 0:2, :], lg[:, 0:2, :, :], AX.X, ALU.add))
                c(v.tensor_tensor(Rb[:, :], Rb[:, :], Sb[:, :], ALU.add))
                c.wait()
                c(v.tensor_copy(slot_i[:, :, :], l1[:, 0:2, :]))
                c.wait()
                dve.sem_inc(s["slots_done"], 1)

            NORM = 4 + 4 + 2
            HEADS = 2 * 3 + 2 * 5
            ROUTE = 20 + 6
            chained = {"start": NORM, (False, True): NORM + HEADS, (True, True): 2 * NORM + HEADS + ROUTE,
                       (True, False): NORM + HEADS + ROUTE, "tail": NORM + ROUTE}

            def prologue(nt, w):
                c = Chain(dve, s["chain_v"], ch.n)
                split(nt, w, 0, input_items(nt))
                dve.wait_ge(s["sel_in"], 16)
                for n, tile in enumerate((selq, selk)):
                    v.tensor_copy(tile[:, :, :, :].rearrange("p a b c -> p (a b c)"), raw_sel[:, n * 1024:(n + 1) * 1024]).then_inc(s["sel_ready"], 1)
                dve.wait_ge(s["mask_t_in"], 16)
                v.tensor_scalar(mask_t[:, :, :], raw_mask_t, 0.0, MASKED, ALU.is_equal, ALU.mult).then_inc(s["mask_ready"], 1)
                if nt == 1:
                    zeros = MT[:, 0:2, :].rearrange("p a n -> p (a n)").unsqueeze(1).to_broadcast([P, 8, 2 * P])
                    v.tensor_copy(KS[:, :, 0:2 * P], zeros).then_inc(s["mask_ready"], 1)
                    v.tensor_copy(mask_s1[:, :, :], mask_s[:, :, bass.ds(tile_reg * P, P)]).then_inc(s["mask_ready"], 1)
                    dve.wait_ge(s["mask_ready"], 3)
                    v.tensor_copy(mask_t1[:, :], mask_t[:, bass.ds(tile_reg, 1), :].rearrange("p a q -> p (a q)")).then_inc(s["mask_ready"], 1)
                else:
                    dve.sem_inc(s["mask_ready"], 3)
                split(nt, w, 0, project_items(nt))
                maxima(nt, w, 1, 0)
                norm(c, 0, 1)
                maxima(nt, w, 1, 1)
                values(nt, w)
                assert c.n == chained["start"], c.n

            def body(nt, b, w, has_before, has_next):
                base = ch.n + chained["start"]
                if has_before:
                    base = base + chained[False, True] + (b - 1) * chained[True, True]
                c = Chain(dve, s["chain_v"], base)
                maxima(nt, w, 0, 2)
                if has_before:
                    residual(c, w, b - 1)
                    norm(c, 1)
                heads_out(nt, c, b, 0)
                if has_next:
                    split(nt, w, b + 1, input_items(nt))
                maxima(nt, w, 0, 3)
                heads_out(nt, c, b, 1)
                if has_next:
                    split(nt, w, b + 1, project_items(nt))
                if has_before:
                    choose(c, w, b - 1)
                heads_out(nt, c, b, 2)
                if has_next:
                    maxima(nt, w, 1, 0)
                if has_before:
                    place(c, w)
                if has_next:
                    norm(c, 0, b + 2)
                    maxima(nt, w, 1, 1)
                    values(nt, w)
                heads_out(nt, c, b, 3)
                assert c.n == chained[has_before, has_next], (c.n, has_before, has_next, chained)

            before_tail = ch.n + chained["start"] + chained[False, True] + (B - 2) * chained[True, True] + chained[True, False]

            def tail(nt, w):
                c = Chain(dve, s["chain_v"], before_tail)
                dve.wait_ge(s["ot_ready"], 2 * B)
                residual(c, w, B - 1)
                norm(c, 1)
                choose(c, w, B - 1)
                place(c, w)
                assert c.n == chained["tail"], c.n

            tile_reg = dve.value_load(flag_i[0:1, 1:2], min_val=0, max_val=QT - 1)
            both(dve, lambda nt: batches(dve, nt, prologue, body, tail))

            c = Chain(dve, s["chain_v"], before_tail + chained["tail"])
            dve.wait_ge(s["counted"], 1)
            c(v.tensor_copy(counts[:, :], ps[:, 6, 0:E]))
            c(v.memset(pads[:, :, :], 0.0))
            c.wait()
            for h in range(2):
                c(v.tensor_tensor(pad_i[:, h, :], counts[:, :], padrow0[:, h, :], ALU.add))
                c(v.tensor_scalar(pads[:, h, D:D + 1].bitcast(I32), padrow0[:, h, 0:1], float(TOK), None, ALU.add))
            c.wait()
            dve.sem_inc(s["pads_set"], 1)
            c(v.tensor_scalar(ti[:, 0:E], counts[0:1, :], float(TILE - 1), None, ALU.add))
            c.wait()
            c(v.tensor_scalar(ti[:, E:2 * E], ti[:, 0:E], TILE.bit_length() - 1, None, ALU.logical_shift_right))
            c.wait()
            c(v.tensor_scalar(tf[:, 0:E], ti[:, E:2 * E], 1.0, None, ALU.max))
            c(v.memset(tf[:, E:2 * E], 0.0))
            c.wait()
            for e in range(1, E):
                c(v.tensor_tensor(tf[:, E + e:E + e + 1], tf[:, E + e - 1:E + e], tf[:, e - 1:e], ALU.add))
                c.wait()
            c(v.tensor_copy(tiles_i[:, :], tf[:, 0:2 * E]))
            c.wait()
            dve.sem_inc(s["tiles_done"], 1)

            def low_x(n):
                dve.wait_ge(s["xt_hi"], n + 1)
                v.tensor_tensor(xet[:, 1, :, :], ps[:, 5, :].rearrange("p (k n) -> p k n", k=2), xet[:, 0, :, :].bitcast(F32),
                                ALU.subtract).then_inc(s["xt_lo"], 1)

            low_x(0)

            def expert(e, par, nxt):
                n = dve.value_load(tiles_i[0:1, bass.ds(e, 1)], min_val=1, max_val=TOK // TILE)
                base_ = dve.value_load(tiles_i[0:1, bass.ds(e + E, 1)], min_val=0, max_val=2 * TOK // TILE + E)

                def tile(T, split):
                    for p in range(4):
                        dve.wait_ge(s["act_f"], 4 * T + p + 5)
                        v.tensor_tensor(hr[:, 1, p, :], hf[:, p, :], hr[:, 0, p, :].bitcast(F32), ALU.subtract).then_inc(s["h_lo"], 1)
                        if split:
                            dve.wait_ge(s["w_hi"], 4 * e + p + 1)
                            v.tensor_tensor(w_part(1 - par, 1, p), w_raw(p), w_part(1 - par, 0, p).bitcast(F32), ALU.subtract).then_inc(s["w_lo"], 1)
                    low_x(T + 1)
                    dve.wait_ge(s["down_done"], 4 * T + 8)
                    dve.wait_ge(s["meta_dma"], 16 * T + 16)
                    dve.wait_ge(s["added"], 32 * T + 16)
                    for half in range(2):
                        ins = v.tensor_scalar(ye[:, half, :], ps[:, 3 + half, 0:D], meta[:, half, bass.ds(e + 1, 1)], None, ALU.mult)
                    ins.then_inc(s["y_done"], 1)

                tile(base_, nxt)
                with dve.If(n > 1):
                    with dve.Fori(1, n) as i:
                        tile(dve.snap(base_ + i), False)
                dve.end_ifs()

            with dve.Fori(0, E // 2 - 1) as k:
                expert(2 * k, 0, True)
                expert(2 * k + 1, 1, True)
            expert(E - 2, 0, True)
            expert(E - 1, 1, False)

        @block.gpsimd
        def _(pool):
            g_ = nc.gpsimd
            g_.memset(x1[:, 0:2, :], 0.0).then_inc(s["zeroed"], 1)
            pool.wait_ge(s["zeroed"], 1)
            for h, name in enumerate(("scattered", "added")):
                pool.dma_start(out[TOK + h * P:TOK + (h + 1) * P, :], x1[:, h, :]).then_inc(s[name], 16)

            def newton(k, n):
                wait_reg(pool, s[("guess1", "guess2")[k]], n + 1)
                a, y, u, z, shift = (nw[:, k, i, :] for i in range(5))
                done = s[("step1", "step2")[k]]
                base = n * 13
                for i in range(3):
                    g_.tensor_tensor(u, y, y, ALU.mult).then_inc(done, 1)
                    wait_reg(pool, done, base + 4 * i + 1)
                    g_.tensor_tensor(z, u, a, ALU.mult).then_inc(done, 1)
                    wait_reg(pool, done, base + 4 * i + 2)
                    g_.tensor_scalar(u, z, consts[:, 0:1], consts[:, 1:2], ALU.mult, ALU.add).then_inc(done, 1)
                    wait_reg(pool, done, base + 4 * i + 3)
                    g_.tensor_tensor(y, y, u, ALU.mult).then_inc(done, 1)
                    wait_reg(pool, done, base + 4 * i + 4)
                g_.tensor_tensor(z, mv[:, k, :, 0], y, ALU.mult).then_inc(done, 1)
                wait_reg(pool, done, base + 13)
                g_.tensor_scalar(shift, z, consts[:, 2:3], consts[:, 3:4], ALU.mult, ALU.add).then_inc(s[("scale1", "scale2")[k]], 1)

            def add_bias(b):
                wait_reg(pool, s["xres_in"], 16 * b + 16)
                ins = g_.tensor_tensor(xres[:, :, :], xres[:, :, :], gbo[:, :].unsqueeze(1).to_broadcast([P, QT, D]), ALU.add)
                ins.then_inc(s["xres_done"], 1)

            def scatter(n):
                wait_reg(pool, s["slots_done"], n + 1)
                for q in range(QT):
                    for j in range(2):
                        pool.indirect_dma_start(routed, bass.IndirectOffsetOnAxis(ap=slot_i[:, j, q:q + 1], axis=0),
                                                pay[:, q, :], None).then_inc(s["scattered"], 16)

            def prologue(nt, w):
                pool.wait_ge(s["const_done"], 1)
                add_bias(0)
                newton(0, 1)

            def split_first(w):
                wait_reg(pool, s["w_dma"], 32)
                for i in range(3):
                    wait_reg(pool, free[i], w.base[i])
                g_.tensor_copy(up_r[0][:, 0, :, :], up_raw[:, :, :]).then_inc(s["w_pool"], 1)
                g_.tensor_copy(dn_r[0][:, 0, :, :], dn_raw[:, :, :]).then_inc(s["w_pool"], 1)
                wait_reg(pool, s["w_pool"], 2)
                g_.tensor_tensor(up_r[0][:, 1, :, :], up_raw[:, :, :], up_r[0][:, 0, :, :].bitcast(F32), ALU.subtract).then_inc(s["w_lo"], 2)
                g_.tensor_tensor(dn_r[0][:, 1, :, :], dn_raw[:, :, :], dn_r[0][:, 0, :, :].bitcast(F32), ALU.subtract).then_inc(s["w_lo"], 2)

            def body(nt, b, w, has_before, has_next):
                if has_before:
                    newton(1, b - 1)
                    add_bias(b)
                if not has_next:
                    split_first(w)
                if has_next:
                    newton(0, b + 2)
                if has_before:
                    scatter(b - 1)

            def tail(nt, w):
                newton(1, B - 1)
                scatter(B - 1)

            newton(0, 0)
            for name in ("scattered", "added"):
                pool.wait_ge(s[name], 16)
            pool.sem_inc(s["x1_stored"], 16)
            both(pool, lambda nt: batches(pool, nt, prologue, body, tail))

            pool.wait_ge(s["pads_set"], 1)
            for e in range(E):
                for h in range(2):
                    pool.indirect_dma_start(routed, bass.IndirectOffsetOnAxis(ap=pad_i[:, h, e:e + 1], axis=0),
                                            pads[:, h, :], None).then_inc(s["pads_in" if e else "pads0_in"], 16)
            pool.wait_ge(s["tiles_done"], 1)

            def expert(e):
                n = pool.value_load(tiles_i[0:1, bass.ds(e, 1)], min_val=1, max_val=TOK // TILE)
                base_ = pool.value_load(tiles_i[0:1, bass.ds(e + E, 1)], min_val=0, max_val=2 * TOK // TILE + E)
                with pool.Fori(0, n) as i:
                    T = pool.snap(base_ + i)
                    pool.wait_ge(s["meta_dma"], 16 * T + 16)
                    wait_reg(pool, s["y_done"], T + 2)
                    for half in range(2):
                        pool.indirect_dma_start(out, bass.IndirectOffsetOnAxis(ap=meta[:, half, 0:1].bitcast(I32), axis=0),
                                                ye[:, half, :], None, compute_op=ALU.add).then_inc(s["added"], 16)

            pool.wait_ge(s["x1_stored"], 16 * B + 16)
            with pool.Fori(0, E) as e:
                expert(e)
            total = pool.value_load(tiles_i[0:1, E - 1:E], min_val=1, max_val=TOK // TILE)
            base_ = pool.value_load(tiles_i[0:1, 2 * E - 1:2 * E], min_val=0, max_val=2 * TOK // TILE + E)
            wait_reg(pool, s["added"], 32 * (total + base_) + 16)


_INPUTS = ["x", "ctx", "mask", "mask_t", "g_xattn", "g_ffn", "wq", "bq", "wk", "bk", "wv", "bv", "wo", "bo",
           "router_w", "router_b", "up", "down", "fixed", "sel"]


def shape_constants():
    rows = np.arange(P)
    c = {"ident": np.eye(P, dtype=np.float32), "trimat": np.triu(np.ones((P, P), np.float32), 1)}
    selq = np.zeros((P, 4, 2, P), np.float32)
    selk = np.zeros((P, 4, 2, P), np.float32)
    for pair in range(4):
        for x in range(2):
            for d in range(DH):
                r = 32 * pair + DH * x + d
                for term, (pq, pk) in enumerate(((0, 0), (1, 0), (0, 1))):
                    selq[r, pair, pq, 64 * x + DH * term + d] = 1
                    selk[r, pair, pk, 64 * x + DH * term + d] = 1
    ones = np.zeros((P, 2), np.float32)
    for j in range(2):
        ones[[48 + j, 112 + j], j] = 1
    c["max_rows"] = ones
    c["region"] = np.tile((np.arange(E) * CAP).astype(np.float32), (P, 1))
    c["padrow0"] = (np.arange(E)[None, None] * CAP + np.arange(2)[None, :, None] * P + rows[:, None, None]).astype(np.float32)
    c["lane"] = np.tile(np.arange(E, dtype=np.float32), (P, 1))
    c["tokens"] = (np.arange(QT)[None] * P + rows[:, None]).astype(np.float32)
    return {"fixed": np.concatenate([c[n].reshape(P, -1) for n in FIXED], 1),
            "sel": np.concatenate([selq.reshape(P, -1), selk.reshape(P, -1)], 1)}


def kernel(x, ctx_1024, mask_1x1xSxS2_ik0, g_xattn, g_ffn, L0_xattn_wq, L0_xattn_bq, L0_xattn_wk, L0_xattn_bk,
           L0_xattn_wv, L0_xattn_bv, L0_xattn_wo, L0_xattn_bo, L0_ffn_router_w, L0_ffn_router_b,
           L0_ffn_expert_up, L0_ffn_expert_down):
    import concourse.bacc as bacc
    from concourse.bass_utils import run_bass_kernel_spmd

    mask = np.asarray(mask_1x1xSxS2_ik0)[0, 0]
    wo = np.asarray(L0_xattn_wo).T.reshape(2, 2, 4, DH, D).transpose(0, 2, 1, 3, 4).reshape(D, D)
    arrays = {
        "x": x, "ctx": ctx_1024, "mask": mask, "mask_t": mask.T, "g_xattn": g_xattn, "g_ffn": g_ffn,
        "wq": np.asarray(L0_xattn_wq).T, "bq": np.asarray(L0_xattn_bq).reshape(KD, P).T, "wk": np.asarray(L0_xattn_wk).T, "bk": np.asarray(L0_xattn_bk).reshape(KD, P).T,
        "wv": np.asarray(L0_xattn_wv).T, "bv": L0_xattn_bv, "wo": wo, "bo": L0_xattn_bo,
        "router_w": L0_ffn_router_w, "router_b": L0_ffn_router_b,
        "up": np.asarray(L0_ffn_expert_up).transpose(0, 2, 1), "down": np.asarray(L0_ffn_expert_down).transpose(0, 2, 1),
        **shape_constants(),
    }
    nc = bacc.Bacc("TRN2", target_bir_lowering=False, num_devices=1)
    t, feeds = {}, {}
    for name in _INPUTS:
        a = np.ascontiguousarray(arrays[name])
        feeds[f"in_{name}"] = a
        t[name] = nc.dram_tensor(f"in_{name}", a.shape, mybir.dt.from_np(a.dtype), kind="ExternalInput").ap()
    t["out"] = nc.dram_tensor("out_rows", (TOK + TILE, D), F32, kind="ExternalOutput").ap()
    xattn_moe(nc, t)
    r = run_bass_kernel_spmd(nc, [feeds], core_ids=[0])
    return r.results[0]["out_rows"][:TOK].reshape(B, S, D)
```
